# Optimizing a Trainium2 kernel written in Bass

```python
import numpy as np
import jax
import jax.numpy as jnp

def _softmax(x, axis=-1):
    return jax.nn.softmax(x, axis=axis)

def _gelu(x):
    return jax.nn.gelu(x, approximate=True)

def _silu(x):
    return jax.nn.silu(x)

def _sigmoid(x):
    return jax.nn.sigmoid(x)

def _layernorm(x, axis=-1, eps=1e-05):
    m = jnp.mean(x, axis=axis, keepdims=True)
    v = jnp.var(x, axis=axis, keepdims=True)
    return (x - m) / jnp.sqrt(v + eps)

def _scatter_add(tgt, idx, src, axis=0):
    return tgt.at[idx].add(src)

def _segment_sum(src, seg, n):
    return jax.ops.segment_sum(src, seg, n)
kernel_name = 'mk_xattn_seq_d4_seqx_r4_62d3fb'

def setup_inputs(seed: int=0):
    np.random.seed(seed)
    _w = jnp.asarray

    def _rec_inputs():
        import jax
        import jax.numpy as jnp
        _rk = jax.random.key(seed)
        x = -0.0002928 + 1 * jax.random.normal(jax.random.fold_in(_rk, 1), (16, 128, 256), jnp.float32)
        _lenS = 128 - jax.random.randint(jax.random.fold_in(_rk, 7), (16,), 0, max(1, 128 // 4) + 1, jnp.int32)
        _lenS2 = 128 - jax.random.randint(jax.random.fold_in(_rk, 8), (16,), 0, max(1, 128 // 4) + 1, jnp.int32)
        _ctx_1024P = jax.random.normal(jax.random.fold_in(_rk, 11), (16, 16, 256), jnp.float32)
        _ctx_1024c = jax.random.dirichlet(jax.random.fold_in(_rk, 511), 0.3 * jnp.ones((16,), jnp.float32), (16, 128))
        _ctx_1024t = jnp.einsum('bsk,bkd->bsd', _ctx_1024c, _ctx_1024P)
        _ctx_1024t = _ctx_1024t * jax.lax.rsqrt(jnp.mean(jnp.square(_ctx_1024t)) + 1e-12) * 0.953939
        ctx_1024 = -1.39393e-06 + 0.999914 * (_ctx_1024t + 0.3 * jax.random.normal(jax.random.fold_in(_rk, 611), (16, 128, 256), jnp.float32))
        fside_Bx16xSxS2_0 = jax.random.uniform(jax.random.fold_in(_rk, 15), (16, 16, 128, 128), jnp.float32, 0.0, 1)
        _validS = jnp.arange(128)[None, :] < _lenS[:, None]
        _validS2 = jnp.arange(128)[None, :] < _lenS2[:, None]
        _causal = jnp.tril(jnp.ones((128, 128), dtype=bool))
        mask_Bx1x1xS2_bf1 = jnp.ones((16, 1, 1, 128), dtype=bool)
        mask_BxSxS2_ik1 = jnp.where(jnp.broadcast_to(_validS2[:, None, :], (16, 128, 128)), 1, 0).astype(jnp.int32)
        mask_Bx16xSxS2_bk0 = jnp.logical_not(jnp.broadcast_to(_validS2[:, None, None, :], (16, 16, 128, 128)))
        mask_SxS_bk1 = jnp.broadcast_to(_validS[0:1, :], (128, 128))
        return (x, ctx_1024, fside_Bx16xSxS2_0, mask_Bx1x1xS2_bf1, mask_BxSxS2_ik1, mask_Bx16xSxS2_bk0, mask_SxS_bk1)
    x, ctx_1024, fside_Bx16xSxS2_0, mask_Bx1x1xS2_bf1, mask_BxSxS2_ik1, mask_Bx16xSxS2_bk0, mask_SxS_bk1 = _rec_inputs()

    def _L0_xattn_setup():
        import jax, jax.numpy as jnp
        import numpy as np
        D_MODEL = 256
        N_HEADS = 16
        D_K = D_MODEL // N_HEADS
        D_FF = 1024
        EPS = 1e-06

        def _layer_norm(x, gamma, beta):
            mean = jnp.mean(x, axis=-1, keepdims=True)
            std = jnp.std(x, axis=-1, keepdims=True, ddof=1)
            return gamma * (x - mean) / (std + EPS) + beta

        def _split_heads(t):
            B, N, _ = t.shape
            return t.reshape(B, N, N_HEADS, D_K).transpose(0, 2, 1, 3)

        def _merge_heads(t):
            B, H, N, dk = t.shape
            return t.transpose(0, 2, 1, 3).reshape(B, N, H * dk)

        def _attention(xq, xkv, wq, wk, wv, wo, mask_bhqk):
            Q = _split_heads(xq @ wq)
            K = _split_heads(xkv @ wk)
            V = _split_heads(xkv @ wv)
            scores = jnp.einsum('bhqd,bhkd->bhqk', Q, K) / jnp.sqrt(jnp.float32(D_K))
            scores = jnp.where(mask_bhqk, scores, -jnp.inf)
            attn = jax.nn.softmax(scores, axis=-1)
            out = jnp.einsum('bhqk,bhkd->bhqd', attn, V)
            return _merge_heads(out) @ wo
        key = jax.random.key(seed)
        ks = jax.random.split(key, 20)
        w = lambda k, *s: jax.random.normal(k, s, dtype=jnp.float32) * 0.02
        B, N = (2, 512)
        inp = {'x': jax.random.normal(ks[0], (B, N, D_MODEL), dtype=jnp.float32), 'encoder_output': jax.random.normal(ks[1], (B, N, D_MODEL), dtype=jnp.float32), 'kv_pad_mask': jnp.ones((B, 1, 1, N), dtype=bool), 'q_pad_mask': jnp.ones((B, 1, 1, N), dtype=bool), 'mha_wq': w(ks[2], D_MODEL, D_MODEL), 'mha_wk': w(ks[3], D_MODEL, D_MODEL), 'mha_wv': w(ks[4], D_MODEL, D_MODEL), 'mha_wo': w(ks[5], D_MODEL, D_MODEL), 'cmha_wq': w(ks[6], D_MODEL, D_MODEL), 'cmha_wk': w(ks[7], D_MODEL, D_MODEL), 'cmha_wv': w(ks[8], D_MODEL, D_MODEL), 'cmha_wo': w(ks[9], D_MODEL, D_MODEL), 'ff_w1': w(ks[10], D_MODEL, D_FF), 'ff_b1': jnp.zeros((D_FF,), jnp.float32), 'ff_w2': w(ks[11], D_FF, D_MODEL), 'ff_b2': jnp.zeros((D_MODEL,), jnp.float32), 'g1': jnp.ones((D_MODEL,), jnp.float32), 'b1': jnp.zeros((D_MODEL,), jnp.float32), 'g2': jnp.ones((D_MODEL,), jnp.float32), 'b2': jnp.zeros((D_MODEL,), jnp.float32), 'g3': jnp.ones((D_MODEL,), jnp.float32), 'b3': jnp.zeros((D_MODEL,), jnp.float32)}
        return inp
    _L0_xattn_all = _L0_xattn_setup()
    _L0_xattn_in = {k: v for k, v in _L0_xattn_all.items() if k in ('mha_wq', 'mha_wk', 'mha_wv', 'mha_wo', 'cmha_wq', 'cmha_wk', 'cmha_wv', 'cmha_wo', 'ff_w1', 'ff_b1', 'ff_w2', 'ff_b2', 'g1', 'b1', 'g2', 'b2', 'g3', 'b3')}
    del _L0_xattn_all

    def _L1_xattn_setup():
        import jax, jax.numpy as jnp
        import numpy as np
        H = 16
        D_MODEL = 256
        D_K = D_MODEL // H
        NEG = -10000000000.0
        EPS = 1e-06

        def _split_heads(x, B):
            return x.reshape(B, -1, H, D_K).transpose(0, 2, 1, 3)
        key = jax.random.key(seed)
        ks = jax.random.split(key, 16)
        B, S, D = (2, 512, D_MODEL)
        scale = 1.0 / np.sqrt(D)
        inp = {'query': jax.random.normal(ks[0], (B, S, D), jnp.float32), 'key': jax.random.normal(ks[1], (B, S, D), jnp.float32), 'values': jax.random.normal(ks[2], (B, S, D), jnp.float32), 'mask': jax.random.randint(ks[3], (B, S, S), 0, 2, jnp.int32), 'Wq': jax.random.normal(ks[4], (D, D), jnp.float32) * scale, 'bq': jnp.zeros((D,), jnp.float32), 'Wk': jax.random.normal(ks[5], (D, D), jnp.float32) * scale, 'bk': jnp.zeros((D,), jnp.float32), 'Wv': jax.random.normal(ks[6], (D, D), jnp.float32) * scale, 'bv': jnp.zeros((D,), jnp.float32), 'Wo': jax.random.normal(ks[7], (D, D), jnp.float32) * scale, 'bo': jnp.zeros((D,), jnp.float32), 'gamma': jnp.ones((D,), jnp.float32), 'beta': jnp.zeros((D,), jnp.float32)}
        return inp
    _L1_xattn_all = _L1_xattn_setup()
    _L1_xattn_in = {k: v for k, v in _L1_xattn_all.items() if k in ('Wq', 'bq', 'Wk', 'bk', 'Wv', 'bv', 'Wo', 'bo', 'gamma', 'beta')}
    del _L1_xattn_all

    def _L2_xattn_setup():
        import jax, jax.numpy as jnp
        import numpy as np
        D_MODEL = 256
        N_HEADS = 16
        D_HEAD = D_MODEL // N_HEADS
        LN_EPS = 1e-05

        def _xavier(key, shape):
            lim = float(np.sqrt(6.0 / (shape[0] + shape[1])))
            return jax.random.uniform(key, shape, jnp.float32, -lim, lim)
        key = jax.random.key(seed)
        ks = jax.random.split(key, 10)
        B, Nq, Nk = (2, 512, 512)
        queries = jax.random.normal(ks[0], (B, Nq, D_MODEL), jnp.float32)
        keys = jax.random.normal(ks[1], (B, Nk, D_MODEL), jnp.float32)
        values = jax.random.normal(ks[2], (B, Nk, D_MODEL), jnp.float32)
        attention_mask = jax.random.bernoulli(ks[3], 0.1, (B, N_HEADS, Nq, Nk))
        attention_weights = jax.random.uniform(ks[4], (B, N_HEADS, Nq, Nk), jnp.float32)
        Wq = _xavier(ks[5], (D_MODEL, D_MODEL))
        Wk = _xavier(ks[6], (D_MODEL, D_MODEL))
        Wv = _xavier(ks[7], (D_MODEL, D_MODEL))
        Wo = _xavier(ks[8], (D_MODEL, D_MODEL))
        b = jnp.zeros((D_MODEL,), jnp.float32)
        gamma = jnp.ones((D_MODEL,), jnp.float32)
        beta = jnp.zeros((D_MODEL,), jnp.float32)
        return {'queries': queries, 'keys': keys, 'values': values, 'attention_mask': attention_mask, 'attention_weights': attention_weights, 'Wq': Wq, 'bq': b, 'Wk': Wk, 'bk': b, 'Wv': Wv, 'bv': b, 'Wo': Wo, 'bo': b, 'gamma': gamma, 'beta': beta}
    _L2_xattn_all = _L2_xattn_setup()
    _L2_xattn_in = {k: v for k, v in _L2_xattn_all.items() if k in ('Wq', 'bq', 'Wk', 'bk', 'Wv', 'bv', 'Wo', 'bo', 'gamma', 'beta')}
    del _L2_xattn_all

    def _L3_xattn_setup():
        import jax, jax.numpy as jnp
        import numpy as np
        B, S, D, H, FF = (2, 512, 256, 16, 1024)
        DH = D // H
        EPS = 1e-05

        def _layernorm(x, g, b):
            mu = jnp.mean(x, axis=-1, keepdims=True)
            var = jnp.var(x, axis=-1, keepdims=True)
            return (x - mu) * jax.lax.rsqrt(var + EPS) * g + b

        def _attn(xq, xkv, qw, qb, kw, kb, vw, vb, ow, ob, mask):
            Bq, Sq, Dm = xq.shape
            Sk = xkv.shape[1]
            scale = jnp.asarray(DH, xq.dtype) ** (-0.5)
            q = (xq @ qw + qb).reshape(Bq, Sq, H, DH).transpose(0, 2, 1, 3)
            k = (xkv @ kw + kb).reshape(Bq, Sk, H, DH).transpose(0, 2, 1, 3)
            v = (xkv @ vw + vb).reshape(Bq, Sk, H, DH).transpose(0, 2, 1, 3)
            scores = jnp.einsum('bhqd,bhkd->bhqk', q, k) * scale
            if mask is not None:
                scores = jnp.where(mask[None, None], -jnp.inf, scores)
            attn = jax.nn.softmax(scores, axis=-1)
            out = jnp.einsum('bhqk,bhkd->bhqd', attn, v).transpose(0, 2, 1, 3).reshape(Bq, Sq, Dm)
            return out @ ow + ob
        key = jax.random.key(seed)
        ks = jax.random.split(key, 32)
        s = 0.02

        def lin(i, din, dout):
            return (jax.random.normal(ks[i], (din, dout), jnp.float32) * s, jnp.zeros((dout,), jnp.float32))
        inp = {}
        inp['queries'] = jax.random.normal(ks[0], (B, S, D), jnp.float32)
        inp['memory'] = jax.random.normal(ks[1], (B, S, D), jnp.float32)
        inp['causal_mask'] = jnp.triu(jnp.ones((S, S), jnp.bool_), k=1)
        inp['ca_qw'], inp['ca_qb'] = lin(2, D, D)
        inp['ca_kw'], inp['ca_kb'] = lin(3, D, D)
        inp['ca_vw'], inp['ca_vb'] = lin(4, D, D)
        inp['ca_ow'], inp['ca_ob'] = lin(5, D, D)
        inp['sa_qw'], inp['sa_qb'] = lin(6, D, D)
        inp['sa_kw'], inp['sa_kb'] = lin(7, D, D)
        inp['sa_vw'], inp['sa_vb'] = lin(8, D, D)
        inp['sa_ow'], inp['sa_ob'] = lin(9, D, D)
        inp['w1'], inp['b1'] = lin(10, D, FF)
        inp['w2'], inp['b2'] = lin(11, FF, D)
        for i, nm in enumerate(['ln1', 'ln2', 'ln3']):
            inp[nm + '_g'] = jnp.ones((D,), jnp.float32)
            inp[nm + '_b'] = jnp.zeros((D,), jnp.float32)
        return inp
    _L3_xattn_all = _L3_xattn_setup()
    _L3_xattn_in = {k: v for k, v in _L3_xattn_all.items() if k in ('ca_qw', 'ca_qb', 'ca_kw', 'ca_kb', 'ca_vw', 'ca_vb', 'ca_ow', 'ca_ob', 'sa_qw', 'sa_qb', 'sa_kw', 'sa_kb', 'sa_vw', 'sa_vb', 'sa_ow', 'sa_ob', 'w1', 'b1', 'w2', 'b2', 'ln1_g', 'ln1_b', 'ln2_g', 'ln2_b', 'ln3_g', 'ln3_b')}
    del _L3_xattn_all
    return {'x': x, 'ctx_1024': ctx_1024, 'fside_Bx16xSxS2_0': fside_Bx16xSxS2_0, 'mask_Bx1x1xS2_bf1': mask_Bx1x1xS2_bf1, 'mask_BxSxS2_ik1': mask_BxSxS2_ik1, 'mask_Bx16xSxS2_bk0': mask_Bx16xSxS2_bk0, 'mask_SxS_bk1': mask_SxS_bk1, 'L0_xattn_mha_wq': _L0_xattn_in['mha_wq'], 'L0_xattn_mha_wk': _L0_xattn_in['mha_wk'], 'L0_xattn_mha_wv': _L0_xattn_in['mha_wv'], 'L0_xattn_mha_wo': _L0_xattn_in['mha_wo'], 'L0_xattn_cmha_wq': _L0_xattn_in['cmha_wq'], 'L0_xattn_cmha_wk': _L0_xattn_in['cmha_wk'], 'L0_xattn_cmha_wv': _L0_xattn_in['cmha_wv'], 'L0_xattn_cmha_wo': _L0_xattn_in['cmha_wo'], 'L0_xattn_ff_w1': _L0_xattn_in['ff_w1'], 'L0_xattn_ff_b1': _L0_xattn_in['ff_b1'], 'L0_xattn_ff_w2': _L0_xattn_in['ff_w2'], 'L0_xattn_ff_b2': _L0_xattn_in['ff_b2'], 'L0_xattn_g1': _L0_xattn_in['g1'], 'L0_xattn_b1': _L0_xattn_in['b1'], 'L0_xattn_g2': _L0_xattn_in['g2'], 'L0_xattn_b2': _L0_xattn_in['b2'], 'L0_xattn_g3': _L0_xattn_in['g3'], 'L0_xattn_b3': _L0_xattn_in['b3'], 'L1_xattn_Wq': _L1_xattn_in['Wq'], 'L1_xattn_bq': _L1_xattn_in['bq'], 'L1_xattn_Wk': _L1_xattn_in['Wk'], 'L1_xattn_bk': _L1_xattn_in['bk'], 'L1_xattn_Wv': _L1_xattn_in['Wv'], 'L1_xattn_bv': _L1_xattn_in['bv'], 'L1_xattn_Wo': _L1_xattn_in['Wo'], 'L1_xattn_bo': _L1_xattn_in['bo'], 'L1_xattn_gamma': _L1_xattn_in['gamma'], 'L1_xattn_beta': _L1_xattn_in['beta'], 'L2_xattn_Wq': _L2_xattn_in['Wq'], 'L2_xattn_bq': _L2_xattn_in['bq'], 'L2_xattn_Wk': _L2_xattn_in['Wk'], 'L2_xattn_bk': _L2_xattn_in['bk'], 'L2_xattn_Wv': _L2_xattn_in['Wv'], 'L2_xattn_bv': _L2_xattn_in['bv'], 'L2_xattn_Wo': _L2_xattn_in['Wo'], 'L2_xattn_bo': _L2_xattn_in['bo'], 'L2_xattn_gamma': _L2_xattn_in['gamma'], 'L2_xattn_beta': _L2_xattn_in['beta'], 'L3_xattn_ca_qw': _L3_xattn_in['ca_qw'], 'L3_xattn_ca_qb': _L3_xattn_in['ca_qb'], 'L3_xattn_ca_kw': _L3_xattn_in['ca_kw'], 'L3_xattn_ca_kb': _L3_xattn_in['ca_kb'], 'L3_xattn_ca_vw': _L3_xattn_in['ca_vw'], 'L3_xattn_ca_vb': _L3_xattn_in['ca_vb'], 'L3_xattn_ca_ow': _L3_xattn_in['ca_ow'], 'L3_xattn_ca_ob': _L3_xattn_in['ca_ob'], 'L3_xattn_sa_qw': _L3_xattn_in['sa_qw'], 'L3_xattn_sa_qb': _L3_xattn_in['sa_qb'], 'L3_xattn_sa_kw': _L3_xattn_in['sa_kw'], 'L3_xattn_sa_kb': _L3_xattn_in['sa_kb'], 'L3_xattn_sa_vw': _L3_xattn_in['sa_vw'], 'L3_xattn_sa_vb': _L3_xattn_in['sa_vb'], 'L3_xattn_sa_ow': _L3_xattn_in['sa_ow'], 'L3_xattn_sa_ob': _L3_xattn_in['sa_ob'], 'L3_xattn_w1': _L3_xattn_in['w1'], 'L3_xattn_b1': _L3_xattn_in['b1'], 'L3_xattn_w2': _L3_xattn_in['w2'], 'L3_xattn_b2': _L3_xattn_in['b2'], 'L3_xattn_ln1_g': _L3_xattn_in['ln1_g'], 'L3_xattn_ln1_b': _L3_xattn_in['ln1_b'], 'L3_xattn_ln2_g': _L3_xattn_in['ln2_g'], 'L3_xattn_ln2_b': _L3_xattn_in['ln2_b'], 'L3_xattn_ln3_g': _L3_xattn_in['ln3_g'], 'L3_xattn_ln3_b': _L3_xattn_in['ln3_b']}

def reference(x, ctx_1024, fside_Bx16xSxS2_0, mask_Bx1x1xS2_bf1, mask_BxSxS2_ik1, mask_Bx16xSxS2_bk0, mask_SxS_bk1, L0_xattn_mha_wq, L0_xattn_mha_wk, L0_xattn_mha_wv, L0_xattn_mha_wo, L0_xattn_cmha_wq, L0_xattn_cmha_wk, L0_xattn_cmha_wv, L0_xattn_cmha_wo, L0_xattn_ff_w1, L0_xattn_ff_b1, L0_xattn_ff_w2, L0_xattn_ff_b2, L0_xattn_g1, L0_xattn_b1, L0_xattn_g2, L0_xattn_b2, L0_xattn_g3, L0_xattn_b3, L1_xattn_Wq, L1_xattn_bq, L1_xattn_Wk, L1_xattn_bk, L1_xattn_Wv, L1_xattn_bv, L1_xattn_Wo, L1_xattn_bo, L1_xattn_gamma, L1_xattn_beta, L2_xattn_Wq, L2_xattn_bq, L2_xattn_Wk, L2_xattn_bk, L2_xattn_Wv, L2_xattn_bv, L2_xattn_Wo, L2_xattn_bo, L2_xattn_gamma, L2_xattn_beta, L3_xattn_ca_qw, L3_xattn_ca_qb, L3_xattn_ca_kw, L3_xattn_ca_kb, L3_xattn_ca_vw, L3_xattn_ca_vb, L3_xattn_ca_ow, L3_xattn_ca_ob, L3_xattn_sa_qw, L3_xattn_sa_qb, L3_xattn_sa_kw, L3_xattn_sa_kb, L3_xattn_sa_vw, L3_xattn_sa_vb, L3_xattn_sa_ow, L3_xattn_sa_ob, L3_xattn_w1, L3_xattn_b1, L3_xattn_w2, L3_xattn_b2, L3_xattn_ln1_g, L3_xattn_ln1_b, L3_xattn_ln2_g, L3_xattn_ln2_b, L3_xattn_ln3_g, L3_xattn_ln3_b):
    import jax
    import jax.numpy as jnp

    def _L0_xattn_ref(x, encoder_output, kv_pad_mask, q_pad_mask, mha_wq, mha_wk, mha_wv, mha_wo, cmha_wq, cmha_wk, cmha_wv, cmha_wo, ff_w1, ff_b1, ff_w2, ff_b2, g1, b1, g2, b2, g3, b3):
        import jax, jax.numpy as jnp
        import numpy as np
        D_MODEL = 256
        N_HEADS = 16
        D_K = D_MODEL // N_HEADS
        D_FF = 1024
        EPS = 1e-06

        def _layer_norm(x, gamma, beta):
            mean = jnp.mean(x, axis=-1, keepdims=True)
            std = jnp.std(x, axis=-1, keepdims=True, ddof=1)
            return gamma * (x - mean) / (std + EPS) + beta

        def _split_heads(t):
            B, N, _ = t.shape
            return t.reshape(B, N, N_HEADS, D_K).transpose(0, 2, 1, 3)

        def _merge_heads(t):
            B, H, N, dk = t.shape
            return t.transpose(0, 2, 1, 3).reshape(B, N, H * dk)

        def _attention(xq, xkv, wq, wk, wv, wo, mask_bhqk):
            Q = _split_heads(xq @ wq)
            K = _split_heads(xkv @ wk)
            V = _split_heads(xkv @ wv)
            scores = jnp.einsum('bhqd,bhkd->bhqk', Q, K) / jnp.sqrt(jnp.float32(D_K))
            scores = jnp.where(mask_bhqk, scores, -jnp.inf)
            attn = jax.nn.softmax(scores, axis=-1)
            out = jnp.einsum('bhqk,bhkd->bhqd', attn, V)
            return _merge_heads(out) @ wo
        B, N, _ = x.shape
        causal = jnp.tril(jnp.ones((N, N), dtype=bool))
        self_mask = causal[None, None] & q_pad_mask
        x_mha = _attention(x, x, mha_wq, mha_wk, mha_wv, mha_wo, self_mask)
        x = _layer_norm(x + x_mha, g1, b1)
        x_cmha = _attention(x, encoder_output, cmha_wq, cmha_wk, cmha_wv, cmha_wo, kv_pad_mask)
        x = _layer_norm(x + x_cmha, g2, b2)
        x_ff = jax.nn.relu(x @ ff_w1 + ff_b1) @ ff_w2 + ff_b2
        x = _layer_norm(x + x_ff, g3, b3)
        return x

    def _L1_xattn_ref(query, key, values, mask, Wq, bq, Wk, bk, Wv, bv, Wo, bo, gamma, beta):
        import jax, jax.numpy as jnp
        import numpy as np
        H = 16
        D_MODEL = 256
        D_K = D_MODEL // H
        NEG = -10000000000.0
        EPS = 1e-06

        def _split_heads(x, B):
            return x.reshape(B, -1, H, D_K).transpose(0, 2, 1, 3)
        B, S, D = query.shape
        residual = query
        q = _split_heads(query @ Wq.T + bq, B)
        k = _split_heads(key @ Wk.T + bk, B)
        v = _split_heads(values @ Wv.T + bv, B)
        scores = jnp.einsum('bhqd,bhkd->bhqk', q, k) / jnp.sqrt(jnp.float32(D_K))
        scores = jnp.where(mask[:, None, :, :] == 0, jnp.float32(NEG), scores)
        attn = jax.nn.softmax(scores, axis=-1)
        x = jnp.einsum('bhqk,bhkd->bhqd', attn, v)
        x = x.transpose(0, 2, 1, 3).reshape(B, S, D)
        x = x @ Wo.T + bo
        x = x + residual
        mu = jnp.mean(x, axis=-1, keepdims=True)
        var = jnp.var(x, axis=-1, keepdims=True)
        return (x - mu) / jnp.sqrt(var + EPS) * gamma + beta

    def _L2_xattn_ref(queries, keys, values, attention_mask, attention_weights, Wq, bq, Wk, bk, Wv, bv, Wo, bo, gamma, beta):
        import jax, jax.numpy as jnp
        import numpy as np
        D_MODEL = 256
        N_HEADS = 16
        D_HEAD = D_MODEL // N_HEADS
        LN_EPS = 1e-05

        def _xavier(key, shape):
            lim = float(np.sqrt(6.0 / (shape[0] + shape[1])))
            return jax.random.uniform(key, shape, jnp.float32, -lim, lim)
        B, Nq, D = queries.shape
        h, d = (N_HEADS, D_HEAD)
        q = (queries @ Wq.T + bq).reshape(B, Nq, h, d).transpose(0, 2, 1, 3)
        k = (keys @ Wk.T + bk).reshape(B, -1, h, d).transpose(0, 2, 1, 3)
        v = (values @ Wv.T + bv).reshape(B, -1, h, d).transpose(0, 2, 1, 3)
        scores = jnp.einsum('bhqd,bhkd->bhqk', q, k) / jnp.sqrt(jnp.float32(d))
        scores = scores * attention_weights
        scores = jnp.where(attention_mask, -jnp.inf, scores)
        p_attn = jax.nn.softmax(scores, axis=-1)
        out = jnp.einsum('bhqk,bhkd->bhqd', p_attn, v)
        out = out.transpose(0, 2, 1, 3).reshape(B, Nq, D)
        out = out @ Wo.T + bo
        x = queries + out
        mu = jnp.mean(x, axis=-1, keepdims=True)
        var = jnp.mean(jnp.square(x - mu), axis=-1, keepdims=True)
        return (x - mu) * jax.lax.rsqrt(var + LN_EPS) * gamma + beta

    def _L3_xattn_ref(queries, memory, causal_mask, ca_qw, ca_qb, ca_kw, ca_kb, ca_vw, ca_vb, ca_ow, ca_ob, sa_qw, sa_qb, sa_kw, sa_kb, sa_vw, sa_vb, sa_ow, sa_ob, w1, b1, w2, b2, ln1_g, ln1_b, ln2_g, ln2_b, ln3_g, ln3_b):
        import jax, jax.numpy as jnp
        import numpy as np
        B, S, D, H, FF = (2, 512, 256, 16, 1024)
        DH = D // H
        EPS = 1e-05

        def _layernorm(x, g, b):
            mu = jnp.mean(x, axis=-1, keepdims=True)
            var = jnp.var(x, axis=-1, keepdims=True)
            return (x - mu) * jax.lax.rsqrt(var + EPS) * g + b

        def _attn(xq, xkv, qw, qb, kw, kb, vw, vb, ow, ob, mask):
            Bq, Sq, Dm = xq.shape
            Sk = xkv.shape[1]
            scale = jnp.asarray(DH, xq.dtype) ** (-0.5)
            q = (xq @ qw + qb).reshape(Bq, Sq, H, DH).transpose(0, 2, 1, 3)
            k = (xkv @ kw + kb).reshape(Bq, Sk, H, DH).transpose(0, 2, 1, 3)
            v = (xkv @ vw + vb).reshape(Bq, Sk, H, DH).transpose(0, 2, 1, 3)
            scores = jnp.einsum('bhqd,bhkd->bhqk', q, k) * scale
            if mask is not None:
                scores = jnp.where(mask[None, None], -jnp.inf, scores)
            attn = jax.nn.softmax(scores, axis=-1)
            out = jnp.einsum('bhqk,bhkd->bhqd', attn, v).transpose(0, 2, 1, 3).reshape(Bq, Sq, Dm)
            return out @ ow + ob
        q = _layernorm(queries, ln1_g, ln1_b)
        h = _attn(q, memory, ca_qw, ca_qb, ca_kw, ca_kb, ca_vw, ca_vb, ca_ow, ca_ob, None)
        x = queries + h
        q = _layernorm(x, ln2_g, ln2_b)
        h = _attn(q, q, sa_qw, sa_qb, sa_kw, sa_kb, sa_vw, sa_vb, sa_ow, sa_ob, causal_mask)
        x = x + h
        q = _layernorm(x, ln3_g, ln3_b)
        x = x + (jax.nn.gelu(q @ w1 + b1, approximate=False) @ w2 + b2)
        return x
    x = _L0_xattn_ref(x, ctx_1024, mask_Bx1x1xS2_bf1, mask_Bx1x1xS2_bf1, L0_xattn_mha_wq, L0_xattn_mha_wk, L0_xattn_mha_wv, L0_xattn_mha_wo, L0_xattn_cmha_wq, L0_xattn_cmha_wk, L0_xattn_cmha_wv, L0_xattn_cmha_wo, L0_xattn_ff_w1, L0_xattn_ff_b1, L0_xattn_ff_w2, L0_xattn_ff_b2, L0_xattn_g1, L0_xattn_b1, L0_xattn_g2, L0_xattn_b2, L0_xattn_g3, L0_xattn_b3)
    x = _L1_xattn_ref(x, ctx_1024, ctx_1024, mask_BxSxS2_ik1, L1_xattn_Wq, L1_xattn_bq, L1_xattn_Wk, L1_xattn_bk, L1_xattn_Wv, L1_xattn_bv, L1_xattn_Wo, L1_xattn_bo, L1_xattn_gamma, L1_xattn_beta)
    x = _L2_xattn_ref(x, ctx_1024, ctx_1024, mask_Bx16xSxS2_bk0, fside_Bx16xSxS2_0, L2_xattn_Wq, L2_xattn_bq, L2_xattn_Wk, L2_xattn_bk, L2_xattn_Wv, L2_xattn_bv, L2_xattn_Wo, L2_xattn_bo, L2_xattn_gamma, L2_xattn_beta)
    x = _L3_xattn_ref(x, ctx_1024, mask_SxS_bk1, L3_xattn_ca_qw, L3_xattn_ca_qb, L3_xattn_ca_kw, L3_xattn_ca_kb, L3_xattn_ca_vw, L3_xattn_ca_vb, L3_xattn_ca_ow, L3_xattn_ca_ob, L3_xattn_sa_qw, L3_xattn_sa_qb, L3_xattn_sa_kw, L3_xattn_sa_kb, L3_xattn_sa_vw, L3_xattn_sa_vb, L3_xattn_sa_ow, L3_xattn_sa_ob, L3_xattn_w1, L3_xattn_b1, L3_xattn_w2, L3_xattn_b2, L3_xattn_ln1_g, L3_xattn_ln1_b, L3_xattn_ln2_g, L3_xattn_ln2_b, L3_xattn_ln3_g, L3_xattn_ln3_b)
    return x

_drawn_inputs = setup_inputs


def setup_inputs(seed=0):
    import zlib

    import numpy as np

    out = dict(_drawn_inputs(seed))
    spreads = {'L0_xattn_ff_b1': (0.0, 0.1),
     'L0_xattn_ff_b2': (0.0, 0.1),
     'L0_xattn_g1': (1.0, 0.2),
     'L0_xattn_b1': (0.0, 0.1),
     'L0_xattn_g2': (1.0, 0.2),
     'L0_xattn_b2': (0.0, 0.1),
     'L0_xattn_g3': (1.0, 0.2),
     'L0_xattn_b3': (0.0, 0.1),
     'L1_xattn_bq': (0.0, 0.469),
     'L1_xattn_bk': (0.0, 2.0),
     'L1_xattn_bv': (0.0, 0.1),
     'L1_xattn_bo': (0.0, 0.1),
     'L1_xattn_gamma': (1.0, 0.2),
     'L1_xattn_beta': (0.0, 0.1),
     'L2_xattn_bq': (0.0, 0.735),
     'L2_xattn_bk': (0.0, 0.8),
     'L2_xattn_bv': (0.0, 0.1),
     'L2_xattn_bo': (0.0, 0.1),
     'L2_xattn_gamma': (1.0, 0.2),
     'L2_xattn_beta': (0.0, 0.1),
     'L3_xattn_ca_qb': (0.0, 0.8),
     'L3_xattn_ca_kb': (0.0, 2.0),
     'L3_xattn_ca_vb': (0.0, 0.1),
     'L3_xattn_ca_ob': (0.0, 0.1),
     'L3_xattn_sa_qb': (0.0, 2.0),
     'L3_xattn_sa_kb': (0.0, 2.0),
     'L3_xattn_sa_vb': (0.0, 0.294),
     'L3_xattn_sa_ob': (0.0, 0.1),
     'L3_xattn_b1': (0.0, 0.1),
     'L3_xattn_b2': (0.0, 0.1),
     'L3_xattn_ln1_g': (1.0, 0.6),
     'L3_xattn_ln1_b': (0.0, 0.8),
     'L3_xattn_ln2_g': (1.0, 0.6),
     'L3_xattn_ln2_b': (0.0, 0.794),
     'L3_xattn_ln3_g': (1.0, 0.6),
     'L3_xattn_ln3_b': (0.0, 0.8)}
    factors = {'L0_xattn_mha_wq': 8.0,
     'L0_xattn_mha_wk': 8.0,
     'L0_xattn_mha_wv': 3.388,
     'L0_xattn_mha_wo': 3.426,
     'L0_xattn_cmha_wq': 8.0,
     'L0_xattn_cmha_wk': 8.0,
     'L3_xattn_ca_qw': 8.0,
     'L3_xattn_ca_kw': 8.0,
     'L3_xattn_sa_qw': 8.0,
     'L3_xattn_sa_kw': 8.0}
    for name, (base, spread) in spreads.items():
        noise = np.random.default_rng([zlib.crc32(name.encode()), seed]).standard_normal(out[name].shape)
        drawn = base * np.exp(spread * noise) if base else spread * noise
        out[name] = jnp.asarray(drawn.astype(out[name].dtype))
    for name, factor in factors.items():
        out[name] = (out[name] * factor).astype(out[name].dtype)
    return out
```

```python
from contextlib import ExitStack

import concourse.bass as bass
from concourse import mybir

F32 = mybir.dt.float32
F16 = mybir.dt.float16
BF16 = mybir.dt.bfloat16
U8 = mybir.dt.uint8
I32 = mybir.dt.int32
ALU = mybir.AluOpType
ACT = mybir.ActivationFunctionType
AX_X = mybir.AxisListType.X

B, N, D, H = 16, 128, 256, 16
DH = D // H
FF = 1024
KC = D // 128
FC = FF // 128
QUADS, QH = 4, 4
STREAMS = 2
MASKED = -(2.0 ** 100)
OVERFLOW = 2.0 ** 60
CHAIN_BANKS = 3

ATTN = {
    "A0": dict(w=("L0_xattn_mha_wq", "L0_xattn_mha_wk", "L0_xattn_mha_wv", "L0_xattn_mha_wo"), b=None,
               kv="self", mask=0, nan=True, pre=False, next=["LN0"]),
    "A1": dict(w=("L0_xattn_cmha_wq", "L0_xattn_cmha_wk", "L0_xattn_cmha_wv", "L0_xattn_cmha_wo"), b=None,
               kv="ctx", mask=1, nan=True, pre=False, next=["LN1"]),
    "A2": dict(w=("L1_xattn_Wq", "L1_xattn_Wk", "L1_xattn_Wv", "L1_xattn_Wo"),
               b=("L1_xattn_bq", "L1_xattn_bk", "L1_xattn_bv", "L1_xattn_bo"),
               kv="ctx", mask=2, nan=False, pre=False, next=["LN3"]),
    "A3": dict(w=("L2_xattn_Wq", "L2_xattn_Wk", "L2_xattn_Wv", "L2_xattn_Wo"),
               b=("L2_xattn_bq", "L2_xattn_bk", "L2_xattn_bv", "L2_xattn_bo"),
               kv="ctx", mask=None, nan=True, pre=False, next=["LN4", "LN5"]),
    "A4": dict(w=("L3_xattn_ca_qw", "L3_xattn_ca_kw", "L3_xattn_ca_vw", "L3_xattn_ca_ow"),
               b=("L3_xattn_ca_qb", "L3_xattn_ca_kb", "L3_xattn_ca_vb", "L3_xattn_ca_ob"),
               kv="ctx", mask=None, nan=False, pre=True, next=["LN6"]),
    "A5": dict(w=("L3_xattn_sa_qw", "L3_xattn_sa_kw", "L3_xattn_sa_vw", "L3_xattn_sa_ow"),
               b=("L3_xattn_sa_qb", "L3_xattn_sa_kb", "L3_xattn_sa_vb", "L3_xattn_sa_ob"),
               kv="self", mask=3, nan=True, pre=True, next=["LN7"]),
}
FFN = {
    "F0": dict(w1="L0_xattn_ff_w1", b1="L0_xattn_ff_b1", w2="L0_xattn_ff_w2", b2="L0_xattn_ff_b2",
               gelu=False, pre=False, next=["LN2"]),
    "F1": dict(w1="L3_xattn_w1", b1="L3_xattn_b1", w2="L3_xattn_w2", b2="L3_xattn_b2",
               gelu=True, pre=True, next=[]),
}
STAGES = ["A0", "A1", "F0", "A2", "A3", "A4", "A5", "F1"]
LN = {
    "LN0": dict(g="L0_xattn_g1", b="L0_xattn_b1", ddof=1, eps=1e-6, on_root=True, to="x", of="sum", after=("sum", "A0")),
    "LN1": dict(g="L0_xattn_g2", b="L0_xattn_b2", ddof=1, eps=1e-6, on_root=True, to="x", of="sum", after=("sum", "A1")),
    "LN2": dict(g="L0_xattn_g3", b="L0_xattn_b3", ddof=1, eps=1e-6, on_root=True, to="x", of="sum", after=("sum", "F0")),
    "LN3": dict(g="L1_xattn_gamma", b="L1_xattn_beta", ddof=0, eps=1e-6, on_root=False, to="x", of="sum", after=("sum", "A2")),
    "LN4": dict(g="L2_xattn_gamma", b="L2_xattn_beta", ddof=0, eps=1e-5, on_root=False, to="x", of="sum", after=("sum", "A3")),
    "LN5": dict(g="L3_xattn_ln1_g", b="L3_xattn_ln1_b", ddof=0, eps=1e-5, on_root=False, to="xn", of="x", after=("norm", "LN4")),
    "LN6": dict(g="L3_xattn_ln2_g", b="L3_xattn_ln2_b", ddof=0, eps=1e-5, on_root=False, to="xn", of="x", after=("sum", "A4")),
    "LN7": dict(g="L3_xattn_ln3_g", b="L3_xattn_ln3_b", ddof=0, eps=1e-5, on_root=False, to="xn", of="x", after=("sum", "A5")),
}


def stream_beats():
    beats = [("bias", "in")]
    for s in STAGES:
        beats += [("xT", s), ("x_t", s)]
        if s in ATTN:
            beats += [(k, s) for k in ("kv", "k32", "v", "k_high", "k_low", "kT", "k_stack",
                                       "q", "q32", "q_high", "q_low", "qT", "q_stack")]
            for u in range(QUADS):
                beats += [("S", s, u)] + ([("times", s, u), ("lower", s, u)] if s == "A3" else [])
                beats += [("max", s, u), ("exp", s, u), ("pT", s, u), ("p_t", s, u), ("PV", s, u)]
            beats += [("flag", s)] if ATTN[s]["nan"] else []
            beats += [(k, s) for k in ("o_raw", "oT", "o_norm", "nT", "o_t", "O", "sum")]
        else:
            beats += [(k, s) for k in ("H0", "h_t0", "H1", "h_t1", "Y", "sum")]
        for n in (ATTN.get(s) or FFN[s])["next"]:
            beats += [(k, n) for k in ("stats", "centre", "root", "norm")]
            beats += [("res", n)] if MAKES_RES[n] else []
    return beats


FED_BY = {"LN0": "A1", "LN1": "F0", "LN2": "A2", "LN3": "A3", "LN4": None, "LN5": "A4", "LN6": "A5", "LN7": "F1"}
MAKES_RES = {n: bool(s and (s in FFN or ATTN[s]["b"])) for n, s in FED_BY.items()}

NTH, _seen = {}, {}
for _beat in stream_beats():
    _kind = _beat[0] if _beat[0] != "p_t" else ("p_t", _beat[2] % 2)
    NTH[_beat] = _seen[_kind] = _seen.get(_kind, 0) + 1

TENSOR = """
xT.0.A0 xT.1.A0 q.0.A0 kv.0.A0 kv.1.A0 qT.0.A0 q.1.A0 kT.0.A0 kT.1.A0 qT.1.A0 S.0.A0.0 S.0.A0.1 S.1.A0.0 S.1.A0.1
S.0.A0.2 pT.0.A0.0 S.0.A0.3 pT.0.A0.1 S.1.A0.2 PV.0.A0.0 S.1.A0.3 PV.0.A0.1 pT.0.A0.2 pT.0.A0.3 PV.0.A0.2
PV.0.A0.3 kv.0.A1 oT.0.A0 pT.1.A0.0 PV.1.A0.0 pT.1.A0.1 nT.0.A0 pT.1.A0.2 PV.1.A0.1 pT.1.A0.3 O.0.A0 PV.1.A0.2
kT.0.A1 PV.1.A0.3 kv.1.A1 xT.0.A1 oT.1.A0 q.0.A1 nT.1.A0 kT.1.A1 O.1.A0 qT.0.A1 S.0.A1.0 S.0.A1.1 xT.1.A1 q.1.A1
S.0.A1.2 pT.0.A1.0 S.0.A1.3 pT.0.A1.1 PV.0.A1.0 qT.1.A1 pT.0.A1.2 PV.0.A1.1 pT.0.A1.3 S.1.A1.0 PV.0.A1.2 S.1.A1.1
PV.0.A1.3 kv.0.A2 pT.1.A1.0 S.1.A1.2 pT.1.A1.1 PV.1.A1.0 S.1.A1.3 oT.0.A1 PV.1.A1.1 pT.1.A1.2 pT.1.A1.3 nT.0.A1
PV.1.A1.2 kT.0.A2 PV.1.A1.3 O.0.A1 kv.1.A2 oT.1.A1 xT.0.F0 nT.1.A1 H0.0.F0 O.1.A1 H1.0.F0 kT.1.A2 xT.1.F0 Y.0.F0
H1.1.F0 H0.1.F0 xT.0.A2 q.0.A2 Y.1.F0 qT.0.A2 S.0.A2.0 S.0.A2.1 xT.1.A2 q.1.A2 S.0.A2.2 pT.0.A2.0 S.0.A2.3
pT.0.A2.1 PV.0.A2.0 qT.1.A2 pT.0.A2.2 PV.0.A2.1 pT.0.A2.3 S.1.A2.0 PV.0.A2.2 S.1.A2.1 PV.0.A2.3 kv.0.A3 oT.0.A2
pT.1.A2.0 S.1.A2.2 pT.1.A2.1 S.1.A2.3 nT.0.A2 PV.1.A2.0 PV.1.A2.1 pT.1.A2.2 O.0.A2 pT.1.A2.3 PV.1.A2.2 kT.0.A3
PV.1.A2.3 kv.1.A3 oT.1.A2 xT.0.A3 q.0.A3 nT.1.A2 kT.1.A3 O.1.A2 qT.0.A3 S.0.A3.0 S.0.A3.1 xT.1.A3 S.0.A3.2 q.1.A3
S.0.A3.3 pT.0.A3.0 qT.1.A3 PV.0.A3.0 pT.0.A3.1 S.1.A3.0 pT.0.A3.2 S.1.A3.1 PV.0.A3.1 pT.0.A3.3 S.1.A3.2 PV.0.A3.2
S.1.A3.3 PV.0.A3.3 kv.0.A4 pT.1.A3.0 oT.0.A3 PV.1.A3.0 pT.1.A3.1 nT.0.A3 pT.1.A3.2 PV.1.A3.1 pT.1.A3.3 O.0.A3
PV.1.A3.2 kT.0.A4 PV.1.A3.3 kv.1.A4 oT.1.A3 nT.1.A3 O.1.A3 xT.0.A4 kT.1.A4 q.0.A4 qT.0.A4 xT.1.A4 S.0.A4.0 q.1.A4
S.0.A4.1 S.0.A4.2 pT.0.A4.0 qT.1.A4 S.0.A4.3 PV.0.A4.0 pT.0.A4.1 S.1.A4.0 pT.0.A4.2 S.1.A4.1 PV.0.A4.1 pT.0.A4.3
PV.0.A4.2 S.1.A4.2 PV.0.A4.3 pT.1.A4.0 S.1.A4.3 pT.1.A4.1 oT.0.A4 PV.1.A4.0 pT.1.A4.2 PV.1.A4.1 pT.1.A4.3 nT.0.A4
PV.1.A4.2 PV.1.A4.3 O.0.A4 oT.1.A4 nT.1.A4 xT.0.A5 O.1.A4 kv.0.A5 q.0.A5 xT.1.A5 kv.1.A5 qT.0.A5 kT.0.A5 q.1.A5
kT.1.A5 S.0.A5.0 S.0.A5.1 qT.1.A5 pT.0.A5.0 S.0.A5.2 pT.0.A5.1 S.0.A5.3 PV.0.A5.0 S.1.A5.0 PV.0.A5.1 pT.0.A5.2
S.1.A5.1 pT.0.A5.3 PV.0.A5.2 S.1.A5.2 PV.0.A5.3 pT.1.A5.0 S.1.A5.3 oT.0.A5 pT.1.A5.1 PV.1.A5.0 pT.1.A5.2 nT.0.A5
pT.1.A5.3 PV.1.A5.1 O.0.A5 PV.1.A5.2 PV.1.A5.3 oT.1.A5 xT.0.F1 nT.1.A5 H0.0.F1 H1.0.F1 O.1.A5 Y.0.F1 xT.1.F1
H1.1.F1 H0.1.F1 Y.1.F1
"""
VECTOR = """
bias.0.in bias.1.in q32.0.A0 q_low.0.A0 k32.0.A0 k_low.0.A0 k32.1.A0 q_stack.0.A0 q32.1.A0 k_low.1.A0 q_low.1.A0
q_stack.1.A0 max.0.A0.0 max.0.A0.1 max.1.A0.0 max.1.A0.1 max.0.A0.2 max.0.A0.3 p_t.0.A0.1 max.1.A0.2 max.1.A0.3
k32.0.A1 o_norm.0.A0 k_low.0.A1 p_t.1.A0.1 sum.0.A0 stats.0.LN0 centre.0.LN0 norm.0.LN0 k32.1.A1 o_norm.1.A0
k_low.1.A1 q32.0.A1 q_low.0.A1 sum.1.A0 stats.1.LN0 q_stack.0.A1 centre.1.LN0 norm.1.LN0 max.0.A1.0 max.0.A1.1
q32.1.A1 max.0.A1.2 q_low.1.A1 max.0.A1.3 p_t.0.A1.1 q_stack.1.A1 max.1.A1.0 max.1.A1.1 k32.0.A2 v.0.A2 max.1.A1.2
p_t.1.A1.1 max.1.A1.3 o_norm.0.A1 k_low.0.A2 sum.0.A1 stats.0.LN1 centre.0.LN1 k32.1.A2 norm.0.LN1 o_norm.1.A1
k_low.1.A2 v.1.A2 h_t0.0.F0 sum.1.A1 stats.1.LN1 centre.1.LN1 norm.1.LN1 h_t1.0.F0 sum.0.F0 stats.0.LN2
centre.0.LN2 norm.0.LN2 h_t1.1.F0 h_t0.1.F0 q32.0.A2 q_low.0.A2 sum.1.F0 stats.1.LN2 q_stack.0.A2 centre.1.LN2
norm.1.LN2 max.0.A2.0 max.0.A2.1 q32.1.A2 max.0.A2.2 q_low.1.A2 max.0.A2.3 p_t.0.A2.1 q_stack.1.A2 max.1.A2.0
max.1.A2.1 k32.0.A3 v.0.A3 o_norm.0.A2 max.1.A2.2 p_t.1.A2.1 max.1.A2.3 k_low.0.A3 sum.0.A2 stats.0.LN3
centre.0.LN3 norm.0.LN3 k32.1.A3 v.1.A3 o_norm.1.A2 k_low.1.A3 q32.0.A3 q_low.0.A3 sum.1.A2 stats.1.LN3
q_stack.0.A3 centre.1.LN3 norm.1.LN3 times.0.A3.0 times.0.A3.1 lower.0.A3.0 times.0.A3.2 q32.1.A3 max.0.A3.0
times.0.A3.3 lower.0.A3.1 q_low.1.A3 lower.0.A3.2 max.0.A3.1 lower.0.A3.3 max.0.A3.2 q_stack.1.A3 max.0.A3.3
p_t.0.A3.1 times.1.A3.0 times.1.A3.1 lower.1.A3.0 times.1.A3.2 max.1.A3.0 times.1.A3.3 lower.1.A3.1 k32.0.A4
lower.1.A3.2 max.1.A3.1 lower.1.A3.3 max.1.A3.2 o_norm.0.A3 max.1.A3.3 k_low.0.A4 v.0.A4 p_t.1.A3.1 sum.0.A3
stats.0.LN4 centre.0.LN4 norm.0.LN4 stats.0.LN5 k32.1.A4 centre.0.LN5 o_norm.1.A3 norm.0.LN5 k_low.1.A4 v.1.A4
sum.1.A3 stats.1.LN4 centre.1.LN4 q32.0.A4 norm.1.LN4 stats.1.LN5 q_low.0.A4 centre.1.LN5 norm.1.LN5 q_stack.0.A4
max.0.A4.0 q32.1.A4 max.0.A4.1 q_low.1.A4 max.0.A4.2 q_stack.1.A4 max.0.A4.3 p_t.0.A4.1 max.1.A4.0 max.1.A4.1
max.1.A4.2 max.1.A4.3 p_t.1.A4.1 o_norm.0.A4 sum.0.A4 stats.0.LN6 o_norm.1.A4 centre.0.LN6 norm.0.LN6 sum.1.A4
stats.1.LN6 centre.1.LN6 k32.0.A5 norm.1.LN6 v.0.A5 q32.0.A5 k_low.0.A5 q_low.0.A5 k32.1.A5 v.1.A5 q_stack.0.A5
k_low.1.A5 q32.1.A5 max.0.A5.0 q_low.1.A5 max.0.A5.1 q_stack.1.A5 max.0.A5.2 p_t.0.A5.1 max.0.A5.3 max.1.A5.0
max.1.A5.1 max.1.A5.2 max.1.A5.3 o_norm.0.A5 p_t.1.A5.1 sum.0.A5 stats.0.LN7 centre.0.LN7 norm.0.LN7 o_norm.1.A5
sum.1.A5 stats.1.LN7 centre.1.LN7 norm.1.LN7 sum.0.F1 sum.1.F1
"""
SCALAR = """
x_t.0.A0 x_t.1.A0 q_high.0.A0 v.0.A0 k_high.0.A0 k_high.1.A0 v.1.A0 q_high.1.A0 k_stack.0.A0 k_stack.1.A0
exp.0.A0.0 exp.0.A0.1 exp.1.A0.0 p_t.0.A0.0 exp.1.A0.1 exp.0.A0.2 exp.0.A0.3 p_t.0.A0.2 p_t.0.A0.3 o_raw.0.A0
k_high.0.A1 p_t.1.A0.0 exp.1.A0.2 v.0.A1 exp.1.A0.3 o_t.0.A0 p_t.1.A0.2 p_t.1.A0.3 k_stack.0.A1 o_raw.1.A0
x_t.0.A1 k_high.1.A1 v.1.A1 o_t.1.A0 q_high.0.A1 k_stack.1.A1 x_t.1.A1 exp.0.A1.0 exp.0.A1.1 q_high.1.A1
p_t.0.A1.0 exp.0.A1.2 exp.0.A1.3 p_t.0.A1.2 p_t.0.A1.3 exp.1.A1.0 o_raw.0.A1 exp.1.A1.1 p_t.1.A1.0 k_high.0.A2
exp.1.A1.2 exp.1.A1.3 p_t.1.A1.2 p_t.1.A1.3 o_t.0.A1 k_stack.0.A2 o_raw.1.A1 k_high.1.A2 x_t.0.F0 o_t.1.A1
k_stack.1.A2 x_t.1.F0 x_t.0.A2 q_high.0.A2 x_t.1.A2 exp.0.A2.0 exp.0.A2.1 q_high.1.A2 p_t.0.A2.0 exp.0.A2.2
exp.0.A2.3 p_t.0.A2.2 p_t.0.A2.3 exp.1.A2.0 o_raw.0.A2 exp.1.A2.1 k_high.0.A3 p_t.1.A2.0 exp.1.A2.2 o_t.0.A2
exp.1.A2.3 p_t.1.A2.2 p_t.1.A2.3 k_stack.0.A3 o_raw.1.A2 k_high.1.A3 x_t.0.A3 o_t.1.A2 q_high.0.A3 k_stack.1.A3
x_t.1.A3 q_high.1.A3 exp.0.A3.0 p_t.0.A3.0 exp.0.A3.1 exp.0.A3.2 exp.0.A3.3 p_t.0.A3.2 p_t.0.A3.3 o_raw.0.A3
exp.1.A3.0 p_t.1.A3.0 k_high.0.A4 exp.1.A3.1 exp.1.A3.2 exp.1.A3.3 o_t.0.A3 p_t.1.A3.2 p_t.1.A3.3 k_stack.0.A4
o_raw.1.A3 k_high.1.A4 o_t.1.A3 x_t.0.A4 k_stack.1.A4 q_high.0.A4 x_t.1.A4 exp.0.A4.0 q_high.1.A4 exp.0.A4.1
p_t.0.A4.0 exp.0.A4.2 exp.0.A4.3 p_t.0.A4.2 exp.1.A4.0 p_t.0.A4.3 exp.1.A4.1 o_raw.0.A4 p_t.1.A4.0 exp.1.A4.2
exp.1.A4.3 p_t.1.A4.2 p_t.1.A4.3 o_t.0.A4 o_raw.1.A4 o_t.1.A4 x_t.0.A5 k_high.0.A5 x_t.1.A5 q_high.0.A5
k_high.1.A5 k_stack.0.A5 q_high.1.A5 k_stack.1.A5 exp.0.A5.0 exp.0.A5.1 p_t.0.A5.0 exp.0.A5.2 exp.0.A5.3
p_t.0.A5.2 exp.1.A5.0 p_t.0.A5.3 exp.1.A5.1 o_raw.0.A5 p_t.1.A5.0 exp.1.A5.2 exp.1.A5.3 o_t.0.A5 p_t.1.A5.2
p_t.1.A5.3 o_raw.1.A5 x_t.0.F1 o_t.1.A5 h_t0.0.F1 h_t1.0.F1 x_t.1.F1 h_t1.1.F1 h_t0.1.F1
"""
POOL = """
flag.0.A0 flag.1.A0 root.0.LN0 root.1.LN0 flag.0.A1 flag.1.A1 root.0.LN1 res.0.LN1 root.1.LN1 res.1.LN1 root.0.LN2
res.0.LN2 root.1.LN2 res.1.LN2 root.0.LN3 res.0.LN3 root.1.LN3 res.1.LN3 flag.0.A3 flag.1.A3 root.0.LN4 root.0.LN5
res.0.LN5 root.1.LN4 root.1.LN5 res.1.LN5 root.0.LN6 res.0.LN6 root.1.LN6 res.1.LN6 flag.0.A5 flag.1.A5 root.0.LN7
res.0.LN7 root.1.LN7 res.1.LN7
"""


def parse(text):
    beats = []
    for word in text.split():
        kind, x, *where = word.split(".")
        beats.append((kind, int(x), where[0], *(int(u) for u in where[1:])))
    return beats


TENSOR_ORDER, VECTOR_ORDER, SCALAR_ORDER, POOL_ORDER = (parse(t) for t in (TENSOR, VECTOR, SCALAR, POOL))
assert sorted(TENSOR_ORDER + VECTOR_ORDER + SCALAR_ORDER + POOL_ORDER) == sorted(
    (b[0], x, *b[1:]) for b in stream_beats() for x in range(STREAMS))

READERS = {"xT": ["x_t"], "kv": ["k32", "v"], "kT": ["k_stack"], "q": ["q32"], "qT": ["q_stack"], "pT": ["p_t"],
           "oT": ["o_norm"], "nT": ["o_t"], "O": ["sum"], "H0": ["h_t0"], "H1": ["h_t1"], "Y": ["sum"]}
FILLS = [beat for beat in TENSOR_ORDER if beat[0] in READERS]
FILL_AT = {beat: n for n, beat in enumerate(FILLS)}
OUTPUT_TURNS = [beat[1:3] for beat in TENSOR_ORDER if beat[0] == "PV" and beat[3] == 0]


def program(nc, dram, out):
    with ExitStack() as ctx:
        def sb(name, shape, dt=F32):
            return ctx.enter_context(nc.sbuf_tensor(name, shape, dt))

        def pb(name, shape=(128, 512), dt=F32):
            return ctx.enter_context(nc.psum_tensor(name, list(shape), dt))

        def sem(name):
            return ctx.enter_context(nc.semaphore(name))

        w_q = {s: sb(f"w_q_{s}", [128, KC, D]) for s in ATTN}
        w_kv = {s: sb(f"w_kv_{s}", [128, KC, 2 * D]) for s in ATTN}
        w_o = {s: sb(f"w_o_{s}", [128, KC, D]) for s in ATTN}
        b_q = {s: sb(f"b_q_{s}", [128, D]) for s in ATTN if ATTN[s]["b"]}
        b_kv = {s: sb(f"b_kv_{s}", [128, 2 * D]) for s in ATTN if ATTN[s]["b"]}
        b_res = {s: sb(f"b_res_{s}", [128, D]) for s in STAGES if s in FFN or ATTN[s]["b"]}
        w_1 = {s: sb(f"w_1_{s}", [128, KC, FF]) for s in FFN}
        w_2 = {s: sb(f"w_2_{s}", [128, FC, D]) for s in FFN}
        b_1 = {s: sb(f"b_1_{s}", [128, FC]) for s in FFN}
        gain = {s: sb(f"gain_{s}", [128, D]) for s in LN}
        shift = {s: sb(f"shift_{s}", [128, D]) for s in LN}

        id32 = sb("id32", [128, 128])
        id16 = sb("id16", [128, 128], F16)
        idb = sb("idb", [128, 128], BF16)
        causal = sb("causal", [128, 128], BF16)
        halves = sb("halves", [128, 2])
        overflow = sb("overflow", [128, H])
        sxs_raw = sb("sxs_raw", [128, 128], U8)
        sxs_bias = sb("sxs_bias", [128, 128], BF16)

        def per_stream(name, shape, dt=F32):
            return [sb(f"{name}{x}", shape, dt) for x in range(STREAMS)]

        x_run = per_stream("x_run", [128, D])
        x_norm = per_stream("x_norm", [128, D])
        x_sum = per_stream("x_sum", [128, D])
        x_res = per_stream("x_res", [128, D])
        x_t = per_stream("x_t", [128, KC, N])
        ctx_t = per_stream("ctx_t", [128, KC, N])
        q32 = per_stream("q32", [128, D])
        k32 = per_stream("k32", [128, D])
        q_parts = per_stream("q_parts", [128, H, 4, DH], F16)
        k_parts = per_stream("k_parts", [128, H, 4, DH], F16)
        q_stack = per_stream("q_stack", [128, H // 2, N], F16)
        k_stack = per_stream("k_stack", [128, H // 2, N], F16)
        v_one = per_stream("v_one", [128, H, 2 * DH])
        key_raw = per_stream("key_raw", [128, 128], U8)
        ik_raw = per_stream("ik_raw", [128, 128], I32)
        bias = per_stream("bias", [128, 3, 128], BF16)
        weight = per_stream("weight", [128, H, N])
        drop_raw = per_stream("drop_raw", [128, H, N], U8)
        neg_max = per_stream("neg_max", [128, H])
        grown = per_stream("grown", [128, H])
        nan_flag = per_stream("nan_flag", [128, H])
        exps = per_stream("exps", [128, 2, QH * N])
        exps_t = per_stream("exps_t", [128, 2, QH * N])
        o_raw = per_stream("o_raw", [128, QUADS, N])
        recip = per_stream("recip", [128, 2, H])
        o_norm = per_stream("o_norm", [128, D])
        o_t = per_stream("o_t", [128, KC, N])
        h_t = per_stream("h_t", [128, FC, N])
        bn = per_stream("bn", [128, 6])
        mean_var = per_stream("mean_var", [128, 2])
        var_eps = per_stream("var_eps", [128, 1])
        root = per_stream("root", [128, 1])
        root_eps = per_stream("root_eps", [128, 1])
        inv_root = per_stream("inv_root", [128, 1])

        s_bank = [[pb(f"s_bank{x}_{r}") for r in range(2)] for x in range(STREAMS)]
        o_bank = pb("o_bank")
        chain = [pb(f"chain{b}") for b in range(CHAIN_BANKS)]

        stage_loaded = {s: sem(f"stage_loaded_{s}") for s in STAGES}
        ln_loaded = sem("ln_loaded")
        sxs_loaded = sem("sxs_loaded")
        cleared = sem("cleared")
        const_made = sem("const_made")
        buffers_cleared = sem("buffers_cleared")
        sxs_made = sem("sxs_made")

        def sems(name):
            return [sem(f"{name}{x}") for x in range(STREAMS)]

        x_loaded = sems("x_loaded")
        ctx_loaded = sems("ctx_loaded")
        masks_loaded = sems("masks_loaded")
        weight_loaded = sems("weight_loaded")
        stored = sems("stored")
        key_bias_made = sems("key_bias_made")
        done = {k: sems(f"done_{k}_") for k in ("xT", "kv", "kT", "q", "qT", "S", "pT", "PV", "oT", "nT", "O",
                                                "H0", "H1", "Y")}
        done |= {k: sems(f"done_{k}_") for k in ("bias", "x_t", "k32", "v", "k_high", "k_low", "k_stack", "q32",
                                                 "q_high", "q_low", "q_stack", "times", "lower", "max", "exp",
                                                 "flag", "o_raw", "o_norm", "o_t", "sum", "h_t0", "h_t1",
                                                 "stats", "centre", "root", "norm", "res")}
        p_t_done = [sems("p_t_even_done"), sems("p_t_odd_done")]
        grown_made = sems("grown_made")
        recip_made = sems("recip_made")
        recip_flagged = sems("recip_flagged")
        bn_made = sems("bn_made")
        aggr_made = sems("aggr_made")
        root_shifted = sems("root_shifted")
        root_inverted = sems("root_inverted")

        first_cleared, last_cleared = x_loaded[0].num, root_inverted[-1].num

        def nth(*beat):
            return NTH[beat]

        def quads_before(s, u, back):
            return QUADS * list(ATTN).index(s) + u + 1 - back

        def bank(beat):
            return chain[FILL_AT[beat] % CHAIN_BANKS]

        def last_readers(beat):
            n = FILL_AT[beat] - CHAIN_BANKS
            if n < 0:
                return []
            kind, x, *where = FILLS[n]
            return [(p_t_done[where[1] % 2][x] if r == "p_t" else done[r][x], nth(r, *where)) for r in READERS[kind]]

        def source(s):
            return {"A0": None, "A1": "LN0", "F0": "LN1", "A2": "LN2", "A3": "LN3", "A4": "LN5",
                    "A5": "LN6", "F1": "LN7"}[s]

        def stage_input(x, s):
            d = ATTN.get(s) or FFN[s]
            return x_norm[x] if d["pre"] else x_run[x]

        def feeds_res(s):
            return next((n for n, made in MAKES_RES.items() if made and FED_BY[n] == s), None)

        def residual(x, s):
            return x_res[x] if feeds_res(s) else x_run[x]

        def mask_bias(x, s):
            m = ATTN[s]["mask"]
            return sxs_bias[:] if m == 3 else bias[x][:, m, :]

        def four(ap):
            return ap.unsqueeze(1).broadcast_to([128, QH, 128])

        def slots(u):
            return slice(QH * u, QH * u + QH)

        def all_loaded(s):
            return 16 * (4 if s in FFN else 3 + 2 * KC + (4 if ATTN[s]["b"] else 0))

        with nc.Block() as block:
            @block.scalar
            def _(act):
                def spread(name):
                    return dram[name].rearrange("(a d) -> a d", a=1).broadcast_to([128, D])

                def load_attn(s):
                    q, k, v, _ = (dram[n].rearrange("(c p) n -> p c n", p=128) for n in ATTN[s]["w"])
                    act.dma_start(w_kv[s][:, :, 0:D], k).then_inc(stage_loaded[s], 16)
                    act.dma_start(w_kv[s][:, :, D:2 * D], v).then_inc(stage_loaded[s], 16)
                    act.dma_start(w_q[s][:], q).then_inc(stage_loaded[s], 16)
                    rows = dram[ATTN[s]["w"][3]].rearrange("(c i r d) n -> c r i d n", c=KC, i=QH, r=2, d=DH)
                    for c in range(KC):
                        for r in range(2):
                            act.dma_start(w_o[s][64 * r:64 * r + 64, c, :], rows[c, r]).then_inc(stage_loaded[s], 16)
                    if ATTN[s]["b"]:
                        bq, bk, bv, bo = (spread(n) for n in ATTN[s]["b"])
                        act.dma_start(b_q[s][:], bq).then_inc(stage_loaded[s], 16)
                        act.dma_start(b_kv[s][:, 0:D], bk).then_inc(stage_loaded[s], 16)
                        act.dma_start(b_kv[s][:, D:2 * D], bv).then_inc(stage_loaded[s], 16)
                        act.dma_start(b_res[s][:], bo).then_inc(stage_loaded[s], 16)

                def load_ffn(s):
                    d = FFN[s]
                    act.dma_start(w_1[s][:], dram[d["w1"]].rearrange("(c p) n -> p c n", p=128)
                                  ).then_inc(stage_loaded[s], 16)
                    act.dma_start(w_2[s][:], dram[d["w2"]].rearrange("(c p) n -> p c n", p=128)
                                  ).then_inc(stage_loaded[s], 16)
                    act.dma_start(b_1[s][:], dram[d["b1"]]).then_inc(stage_loaded[s], 16)
                    act.dma_start(b_res[s][:], spread(d["b2"])).then_inc(stage_loaded[s], 16)

                for s in STAGES:
                    load_attn(s) if s in ATTN else load_ffn(s)
                    if s == "A0":
                        act.dma_start(sxs_raw[:], dram["sxs"]).then_inc(sxs_loaded, 16)
                        for n in LN:
                            act.dma_start(gain[n][:], spread(LN[n]["g"])).then_inc(ln_loaded, 16)
                            act.dma_start(shift[n][:], spread(LN[n]["b"])).then_inc(ln_loaded, 16)
            @block.gpsimd
            def _(pool):
                for t in (id32, id16, idb, causal):
                    nc.gpsimd.memset(t[:], 0.0).then_inc(cleared, 1)
                nc.gpsimd.memset(halves[:, 0:1], -0.5).then_inc(const_made, 1)
                nc.gpsimd.memset(halves[:, 1:2], 0.5).then_inc(const_made, 1)
                nc.gpsimd.memset(overflow[:], OVERFLOW).then_inc(const_made, 1)
                pool.wait_ge(cleared, 4)
                for t in (id32, id16, idb):
                    nc.gpsimd.affine_select(out=t[:], in_=t[:], compare_op=ALU.not_equal, fill=1.0, base=0,
                                            pattern=[[-1, 128]], channel_multiplier=1).then_inc(const_made, 1)
                nc.gpsimd.affine_select(out=causal[:], in_=causal[:], compare_op=ALU.is_ge, fill=MASKED, base=0,
                                        pattern=[[-1, 128]], channel_multiplier=1).then_inc(const_made, 1)

            @block.vector
            def _(dve):
                for x in range(STREAMS):
                    nc.vector.memset(v_one[x][:, :, DH:DH + 1], 1.0).then_inc(buffers_cleared, 1)
                    nc.vector.memset(v_one[x][:, :, DH + 1:2 * DH], 0.0).then_inc(buffers_cleared, 1)
                    nc.vector.memset(q_parts[x][:, :, 3, :], 0.0).then_inc(buffers_cleared, 1)
                    nc.vector.memset(k_parts[x][:, :, 3, :], 0.0).then_inc(buffers_cleared, 1)
                dve.wait_ge(sxs_loaded, 16)
                nc.vector.tensor_scalar(sxs_bias[:], sxs_raw[:], 0.0, MASKED, ALU.is_gt, ALU.mult
                                        ).then_inc(sxs_made, 1)

        with nc.Fori(0, B // STREAMS) as i:
            with nc.Block() as block:

                @block.sync
                def _(sp):
                    def one(name, b):
                        t = dram[name]
                        dims = " ".join("cdef"[:len(t.shape) - 1])
                        return t[bass.ds(b, 1)].rearrange(f"a {dims} -> (a {dims[0]}) {dims[2:]}")

                    for x in range(STREAMS):
                        b = STREAMS * i + x
                        sp.dma_start(x_run[x][:], one("x", b)).then_inc(x_loaded[x], 16)
                        sp.dma_start(key_raw[x][:], dram["kmask"][bass.ds(b, 1)].rearrange("a c d e -> (a c d) e")
                                     .broadcast_to([128, N])).then_inc(masks_loaded[x], 16)
                        sp.dma_start(ik_raw[x][:], one("ik", b)).then_inc(masks_loaded[x], 16)
                        sp.dma_start(ctx_t[x][:], dram["ctx_t"][bass.ds(b, 1)].rearrange("a (c p) n -> p (a c) n", p=128)
                                     ).then_inc(ctx_loaded[x], 16)
                    for x in range(STREAMS):
                        b = STREAMS * i + x
                        sp.dma_start(weight[x][:], one("fside", b)
                                     ).then_inc(weight_loaded[x], 16)
                        sp.dma_start(drop_raw[x][:], one("drop", b)
                                     ).then_inc(weight_loaded[x], 16)
                    for x in range(STREAMS):
                        sp.wait_ge(done["sum"][x], nth("sum", "F1"))
                        sp.dma_start(out[bass.ds(STREAMS * i + x, 1)].rearrange("a q d -> (a q) d"), x_sum[x][:]
                                     ).then_inc(stored[x], 16)
                    for x in range(STREAMS):
                        sp.wait_ge(stored[x], 16)

                @block.gpsimd
                def _(pool):
                    def row_flags(x, s):
                        pool.wait_ge(done["max"][x], nth("max", s, QUADS - 1))
                        nc.gpsimd.tensor_tensor(grown[x][:], neg_max[x][:], overflow[:], ALU.mult
                                                ).then_inc(grown_made[x], 1)
                        pool.wait_ge(grown_made[x], nth("flag", s))
                        nc.gpsimd.tensor_tensor(nan_flag[x][:], grown[x][:], grown[x][:], ALU.subtract
                                                ).then_inc(done["flag"][x], 1)

                    def var_root(x, n):
                        pool.wait_ge(done["stats"][x], nth("stats", n))
                        e = 1 if LN[n]["on_root"] else 0
                        nc.gpsimd.tensor_tensor(root[x][:], var_eps[x][:], halves[:, e:e + 1], ALU.pow
                                                ).then_inc(done["root"][x], 1)

                    def next_residual(x, n):
                        s = FED_BY[n]
                        pool.wait_ge(done["norm"][x], nth("norm", n))
                        pool.wait_ge(stage_loaded[s], all_loaded(s))
                        nc.gpsimd.tensor_tensor(x_res[x][:], x_run[x][:], b_res[s][:], ALU.add
                                                ).then_inc(done["res"][x], 1)

                    for kind, x, *where in POOL_ORDER:
                        if kind == "flag":
                            row_flags(x, *where)
                        elif kind == "root":
                            var_root(x, *where)
                        elif kind == "res":
                            next_residual(x, *where)

                @block.tensor
                def _(pe):
                    def free_bank(beat):
                        for read, times in last_readers(beat):
                            pe.wait_ge(read, times)
                        return bank(beat)

                    def transposes32(dst, src, blocks):
                        for c in range(blocks):
                            mm = nc.tensor.matmul(dst[:, 128 * c:128 * c + 128], src[:, 128 * c:128 * c + 128], id32[:],
                                                  start=True, stop=True, is_transpose=True)
                        return mm

                    def product(dst, left, right, chunks):
                        for c in range(chunks):
                            mm = nc.tensor.matmul(dst, left[:, c, :], right[:, c, :], start=(c == 0), stop=(c == chunks - 1))
                        return mm

                    def keys_values(dst, x, s):
                        pe.wait_ge(stage_loaded[s], all_loaded(s))
                        if ATTN[s]["kv"] == "self":
                            pe.wait_ge(done["x_t"][x], nth("x_t", s))
                            kv_t = x_t[x]
                        else:
                            pe.wait_ge(ctx_loaded[x], 16)
                            kv_t = ctx_t[x]
                        product(dst[:, :], kv_t, w_kv[s], KC).then_inc(done["kv"][x], 1)

                    def stack(dst, parts):
                        flat = parts[:].rearrange("p h t d -> p (h t d)")
                        for pair in range(H // 2):
                            mm = nc.tensor.transpose(dst[:].bitcast(F16)[:, 128 * pair:128 * pair + 128],
                                                     flat[:, 128 * pair:128 * pair + 128], id16[:])
                        return mm

                    def scores(x, s, u):
                        c, r = u // 2, u % 2
                        if u == 0:
                            pe.wait_ge(done["k_stack"][x], nth("k_stack", s))
                            pe.wait_ge(done["q_stack"][x], nth("q_stack", s))
                            if ATTN[s]["mask"] in (0, 1, 2):
                                pe.wait_ge(done["bias"][x], 1)
                            elif ATTN[s]["mask"] == 3:
                                pe.wait_ge(sxs_made, 1)
                        if s == "A3" and u >= 2:
                            pe.wait_ge(done["times"][x], nth("times", s, u - 2))
                        elif quads_before(s, u, 2) > 0:
                            pe.wait_ge(done["exp"][x], quads_before(s, u, 2))
                        masked = ATTN[s]["mask"] is not None
                        dst = s_bank[x][r]
                        if masked:
                            nc.tensor.matmul(dst[:], idb[:], four(mask_bias(x, s)), start=True, stop=True)
                        rows = slice(64 * r, 64 * r + 64)
                        for n in range(QH):
                            mm = nc.tensor.matmul(dst[:, 128 * n:128 * n + 128], q_stack[x][rows, QH * c + n, :],
                                                  k_stack[x][rows, QH * c + n, :], start=not masked,
                                                  stop=True, skip_group_check=masked)
                        mm.then_inc(done["S"][x], 1)

                    def outputs(x, s, u):
                        pe.wait_ge(p_t_done[u % 2][x], nth("p_t", s, u))
                        if u == 0:
                            pe.wait_ge(done["v"][x], nth("v", s))
                            turn = OUTPUT_TURNS.index((x, s))
                            if turn:
                                last_x, last_s = OUTPUT_TURNS[turn - 1]
                                pe.wait_ge(done["o_raw"][last_x], nth("o_raw", last_s))
                        for n in range(QH):
                            h = 8 * (u // 2) + 2 * n + u % 2
                            mm = nc.tensor.matmul(o_bank[32 * n:32 * n + 32, 128 * u:128 * u + 128], v_one[x][:, h, :],
                                                  exps_t[x][:, u % 2, 128 * n:128 * n + 128], start=True, stop=True)
                        mm.then_inc(done["PV"][x], 1)

                    def hidden(dst, x, s, half):
                        pe.wait_ge(stage_loaded[s], all_loaded(s))
                        pe.wait_ge(done["x_t"][x], nth("x_t", s))
                        for n in range(QH):
                            f = QH * half + n
                            for c in range(KC):
                                mm = nc.tensor.matmul(dst[:, 128 * n:128 * n + 128], w_1[s][:, c, 128 * f:128 * f + 128],
                                                      x_t[x][:, c, :], start=(c == 0), stop=(c == KC - 1))
                        return mm

                    for beat in TENSOR_ORDER:
                        kind, x, s = beat[:3]
                        dst = free_bank(beat) if kind in READERS else None
                        if kind == "xT":
                            if s == "A0":
                                pe.wait_ge(x_loaded[x], 16)
                            else:
                                pe.wait_ge(done["norm"][x], nth("norm", source(s)))
                            transposes32(dst, stage_input(x, s), KC).then_inc(done["xT"][x], 1)
                        elif kind == "kv":
                            keys_values(dst, x, s)
                        elif kind == "q":
                            pe.wait_ge(stage_loaded[s], all_loaded(s))
                            pe.wait_ge(done["x_t"][x], nth("x_t", s))
                            product(dst[:, 0:D], x_t[x], w_q[s], KC).then_inc(done["q"][x], 1)
                        elif kind == "kT":
                            pe.wait_ge(done["k_low"][x], nth("k_low", s))
                            stack(dst, k_parts[x]).then_inc(done["kT"][x], 1)
                        elif kind == "qT":
                            pe.wait_ge(done["q_low"][x], nth("q_low", s))
                            stack(dst, q_parts[x]).then_inc(done["qT"][x], 1)
                        elif kind == "S":
                            scores(x, s, beat[3])
                        elif kind == "pT":
                            pe.wait_ge(done["exp"][x], nth("exp", s, beat[3]))
                            transposes32(dst, exps[x][:, beat[3] % 2, :], QH).then_inc(done["pT"][x], 1)
                        elif kind == "PV":
                            outputs(x, s, beat[3])
                        elif kind == "oT":
                            pe.wait_ge(done["o_raw"][x], nth("o_raw", s))
                            transposes32(dst, o_raw[x][:].rearrange("p u q -> p (u q)"), QUADS).then_inc(done["oT"][x], 1)
                        elif kind == "nT":
                            pe.wait_ge(done["o_norm"][x], nth("o_norm", s))
                            transposes32(dst, o_norm[x], KC).then_inc(done["nT"][x], 1)
                        elif kind == "O":
                            pe.wait_ge(done["o_t"][x], nth("o_t", s))
                            product(dst[:, 0:D], o_t[x], w_o[s], KC).then_inc(done["O"][x], 1)
                        elif kind in ("H0", "H1"):
                            hidden(dst, x, s, int(kind[1])).then_inc(done[kind][x], 1)
                        elif kind == "Y":
                            pe.wait_ge(done["h_t0"][x], nth("h_t0", s))
                            pe.wait_ge(done["h_t1"][x], nth("h_t1", s))
                            product(dst[:, 0:D], h_t[x], w_2[s], FC).then_inc(done["Y"][x], 1)

                @block.scalar
                def _(act):
                    def split_high(dst, src, scale):
                        return nc.scalar.activation(dst, src[:].rearrange("p (h t d) -> p h t d", h=H, t=1)
                                                    .broadcast_to([128, H, 2, DH]), ACT.Copy, scale=scale)

                    def exponentials(x, s, u):
                        act.wait_ge(done["max"][x], nth("max", s, u))
                        if quads_before(s, u, 2) > 0:
                            act.wait_ge(done["pT"][x], quads_before(s, u, 2))
                        for n in range(QH):
                            cols = slice(128 * n, 128 * n + 128)
                            slot = QH * u + n
                            src = weight[x][:, slot, :] if s == "A3" else s_bank[x][u % 2][:, cols]
                            ins = nc.scalar.activation(exps[x][:, u % 2, cols], src, ACT.Exp,
                                                       bias=neg_max[x][:, slot:slot + 1])
                        ins.then_inc(done["exp"][x], 1)

                    for beat in SCALAR_ORDER:
                        kind, x, s = beat[:3]
                        if kind == "x_t":
                            act.wait_ge(done["xT"][x], nth("xT", s))
                            nc.scalar.copy(x_t[x][:], bank(("xT", x, s))[:, 0:D].rearrange("p (c q) -> p c q", c=KC)
                                           ).then_inc(done["x_t"][x], 1)
                        elif kind == "v":
                            act.wait_ge(done["k32"][x], nth("k32", s))
                            if s != "A0":
                                act.wait_ge(done["PV"][x], quads_before(s, 0, 1))
                            nc.scalar.copy(v_one[x][:, :, 0:DH], bank(("kv", x, s))[:, D:2 * D].rearrange(
                                "p (h d) -> p h d", h=H)).then_inc(done["v"][x], 1)
                        elif kind == "k_high":
                            act.wait_ge(done["k32"][x], nth("k32", s))
                            split_high(k_parts[x][:, :, 0:3:2, :], k32[x], 1.0).then_inc(done["k_high"][x], 1)
                        elif kind == "q_high":
                            act.wait_ge(done["q32"][x], nth("q32", s))
                            split_high(q_parts[x][:, :, 0:2, :], q32[x], DH ** -0.5).then_inc(done["q_high"][x], 1)
                        elif kind == "k_stack":
                            act.wait_ge(done["kT"][x], nth("kT", s))
                            nc.scalar.copy(k_stack[x][:], bank(("kT", x, s))[:].bitcast(F16).rearrange(
                                "p (h k) -> p h k", h=H // 2)).then_inc(done["k_stack"][x], 1)
                        elif kind == "q_stack":
                            act.wait_ge(done["qT"][x], nth("qT", s))
                            nc.scalar.copy(q_stack[x][:], bank(("qT", x, s))[:].bitcast(F16).rearrange(
                                "p (h k) -> p h k", h=H // 2)).then_inc(done["q_stack"][x], 1)
                        elif kind == "exp":
                            exponentials(x, s, beat[3])
                        elif kind == "p_t":
                            u = beat[3]
                            act.wait_ge(done["pT"][x], nth("pT", s, u))
                            if quads_before(s, u, 2) > 0:
                                act.wait_ge(done["PV"][x], quads_before(s, u, 2))
                            nc.scalar.copy(exps_t[x][:, u % 2, :], bank(("pT", x, s, u))[:]
                                           ).then_inc(p_t_done[u % 2][x], 1)
                        elif kind == "o_raw":
                            act.wait_ge(done["PV"][x], nth("PV", s, QUADS - 1))
                            nc.scalar.copy(o_raw[x][:], o_bank[:].rearrange("p (u q) -> p u q", u=QUADS)
                                           ).then_inc(done["o_raw"][x], 1)
                        elif kind == "o_t":
                            act.wait_ge(done["nT"][x], nth("nT", s))
                            nc.scalar.copy(o_t[x][:], bank(("nT", x, s))[:, 0:D].rearrange("p (c q) -> p c q", c=KC)
                                           ).then_inc(done["o_t"][x], 1)
                        elif kind in ("h_t0", "h_t1"):
                            half = int(kind[3])
                            act.wait_ge(done[f"H{half}"][x], nth(f"H{half}", s))
                            for n in range(QH):
                                f = QH * half + n
                                ins = nc.scalar.activation(h_t[x][:, f, :], bank((f"H{half}", x, s))[:, 128 * n:128 * n + 128],
                                                           ACT.Gelu, bias=b_1[s][:, f:f + 1])
                            ins.then_inc(done[kind][x], 1)

                @block.vector
                def _(dve):
                    def mask_biases(x):
                        dve.wait_ge(masks_loaded[x], 32)
                        nc.vector.tensor_scalar(bias[x][:, 1, :], key_raw[x][:], 0.0, MASKED, ALU.is_equal, ALU.mult
                                                ).then_inc(key_bias_made[x], 1)
                        nc.vector.tensor_scalar(bias[x][:, 2, :], ik_raw[x][:], 0.0, MASKED, ALU.is_equal, ALU.mult
                                                ).then_inc(key_bias_made[x], 1)
                        dve.wait_ge(key_bias_made[x], 2)
                        nc.vector.tensor_tensor(bias[x][:, 0, :], bias[x][:, 1, :], causal[:], ALU.add
                                                ).then_inc(done["bias"][x], 1)

                    def values(x, s):
                        dve.wait_ge(done["kv"][x], nth("kv", s))
                        dve.wait_ge(done["PV"][x], quads_before(s, 0, 1))
                        nc.vector.tensor_tensor(v_one[x][:, :, 0:DH], bank(("kv", x, s))[:, D:2 * D].rearrange(
                            "p (h d) -> p h d", h=H), b_kv[s][:, D:2 * D].rearrange("p (h d) -> p h d", h=H), ALU.add
                                                ).then_inc(done["v"][x], 1)

                    def quad_max(x, s, u):
                        if s == "A3":
                            dve.wait_ge(done["lower"][x], nth("lower", s, u))
                            heads = weight[x][:, slots(u), :]
                        else:
                            dve.wait_ge(done["S"][x], nth("S", s, u))
                            heads = s_bank[x][u % 2][:].rearrange("p (n k) -> p n k", n=QH)
                        nc.vector.tensor_reduce(neg_max[x][:, slots(u)], heads, AX_X, ALU.max, negate=True
                                                ).then_inc(done["max"][x], 1)

                    def normalise(x, s):
                        heads = bank(("oT", x, s))[:].rearrange("p (h e) -> p h e", h=H)
                        dve.wait_ge(done["oT"][x], nth("oT", s))
                        nc.vector.reciprocal(recip[x][:, 0, :].unsqueeze(2), heads[:, :, DH:DH + 1]
                                             ).then_inc(recip_made[x], 1)
                        dve.wait_ge(recip_made[x], nth("oT", s))
                        which = 0
                        if ATTN[s]["nan"]:
                            dve.wait_ge(done["flag"][x], nth("flag", s))
                            nc.vector.tensor_tensor(recip[x][:, 1, :], recip[x][:, 0, :], nan_flag[x][:], ALU.add
                                                    ).then_inc(recip_flagged[x], 1)
                            dve.wait_ge(recip_flagged[x], nth("flag", s))
                            which = 1
                        nc.vector.tensor_tensor(o_norm[x][:].rearrange("p (h d) -> p h d", h=H), heads[:, :, 0:DH],
                                                recip[x][:, which, :].unsqueeze(2).broadcast_to([128, H, DH]), ALU.mult
                                                ).then_inc(done["o_norm"][x], 1)

                    def add_residual(x, s):
                        product = ("O" if s in ATTN else "Y", x, s)
                        dst = x_run[x] if s in ("A4", "A5") else x_sum[x]
                        dve.wait_ge(done[product[0]][x], nth(product[0], s))
                        if feeds_res(s):
                            dve.wait_ge(done["res"][x], nth("res", feeds_res(s)))
                        nc.vector.tensor_tensor(dst[:], bank(product)[:, 0:D], residual(x, s)[:], ALU.add
                                                ).then_inc(done["sum"][x], 1)

                    def norm_stats(x, n):
                        d = LN[n]
                        src = x_sum[x] if d["of"] == "sum" else x_run[x]
                        kind, before = d["after"]
                        dve.wait_ge(done[kind][x], nth(kind, before))
                        nc.vector.bn_stats(bn[x][:], src[:]).then_inc(bn_made[x], 1)
                        dve.wait_ge(bn_made[x], nth("stats", n))
                        nc.vector.bn_aggr(mean_var[x][:], bn[x][:]).then_inc(aggr_made[x], 1)
                        dve.wait_ge(aggr_made[x], nth("stats", n))
                        scale = D / (D - d["ddof"])
                        nc.vector.tensor_scalar(var_eps[x][:], mean_var[x][:, 1:2], scale, 0.0 if d["on_root"] else d["eps"],
                                                ALU.mult, ALU.add).then_inc(done["stats"][x], 1)

                    def norm_apply(x, n):
                        d = LN[n]
                        dst = x_run[x] if d["to"] == "x" else x_norm[x]
                        dve.wait_ge(done["root"][x], nth("root", n))
                        by = root[x]
                        if d["on_root"]:
                            nc.vector.tensor_scalar(root_eps[x][:], root[x][:], d["eps"], None, ALU.add
                                                    ).then_inc(root_shifted[x], 1)
                            dve.wait_ge(root_shifted[x], nth("norm", n))
                            nc.vector.reciprocal(inv_root[x][:], root_eps[x][:]).then_inc(root_inverted[x], 1)
                            dve.wait_ge(root_inverted[x], nth("norm", n))
                            by = inv_root[x]
                        dve.wait_ge(done["centre"][x], nth("centre", n))
                        nc.vector.scalar_tensor_tensor(out=dst[:], in0=x_sum[x][:], scalar=by[:, 0:1], in1=shift[n][:],
                                                       op0=ALU.mult, op1=ALU.add).then_inc(done["norm"][x], 1)

                    for kind, x, s, *u in VECTOR_ORDER:
                        if kind == "bias":
                            mask_biases(x)
                        elif kind == "k32":
                            dve.wait_ge(done["kv"][x], nth("kv", s))
                            src = bank(("kv", x, s))[:, 0:D]
                            if ATTN[s]["b"]:
                                nc.vector.tensor_tensor(k32[x][:], src, b_kv[s][:, 0:D], ALU.add).then_inc(done["k32"][x], 1)
                            else:
                                nc.vector.tensor_copy(k32[x][:], src).then_inc(done["k32"][x], 1)
                        elif kind == "v":
                            values(x, s)
                        elif kind == "k_low":
                            dve.wait_ge(done["k_high"][x], nth("k_high", s))
                            nc.vector.tensor_tensor(k_parts[x][:, :, 1, :], k32[x][:].rearrange("p (h d) -> p h d", h=H),
                                                    k_parts[x][:, :, 0, :], ALU.subtract).then_inc(done["k_low"][x], 1)
                        elif kind == "q32":
                            dve.wait_ge(done["q"][x], nth("q", s))
                            src = bank(("q", x, s))[:, 0:D]
                            if ATTN[s]["b"]:
                                nc.vector.tensor_tensor(q32[x][:], src, b_q[s][:], ALU.add).then_inc(done["q32"][x], 1)
                            else:
                                nc.vector.tensor_copy(q32[x][:], src).then_inc(done["q32"][x], 1)
                        elif kind == "q_low":
                            dve.wait_ge(done["q_high"][x], nth("q_high", s))
                            nc.vector.scalar_tensor_tensor(
                                out=q_parts[x][:, :, 2, :], in0=q32[x][:].rearrange("p (h d) -> p h d", h=H),
                                scalar=DH ** -0.5, in1=q_parts[x][:, :, 0, :], op0=ALU.mult, op1=ALU.subtract
                            ).then_inc(done["q_low"][x], 1)
                        elif kind == "q_stack":
                            dve.wait_ge(done["qT"][x], nth("qT", s))
                            nc.vector.tensor_copy(q_stack[x][:], bank(("qT", x, s))[:].bitcast(F16).rearrange(
                                "p (h q) -> p h q", h=H // 2)).then_inc(done["q_stack"][x], 1)
                        elif kind == "times":
                            if u[0] == 0:
                                dve.wait_ge(weight_loaded[x], 32)
                            dve.wait_ge(done["S"][x], nth("S", s, *u))
                            part = weight[x][:, slots(*u), :]
                            nc.vector.tensor_tensor(part, s_bank[x][u[0] % 2][:].rearrange("p (n k) -> p n k", n=QH), part,
                                                    ALU.mult).then_inc(done["times"][x], 1)
                        elif kind == "lower":
                            dve.wait_ge(done["times"][x], nth("times", s, *u))
                            part = weight[x][:, slots(*u), :]
                            nc.vector.scalar_tensor_tensor(out=part, in0=drop_raw[x][:, slots(*u), :], scalar=MASKED, in1=part,
                                                           op0=ALU.mult, op1=ALU.add).then_inc(done["lower"][x], 1)
                        elif kind == "max":
                            quad_max(x, s, *u)
                        elif kind == "p_t":
                            dve.wait_ge(done["pT"][x], nth("pT", s, *u))
                            if quads_before(s, *u, 2) > 0:
                                dve.wait_ge(done["PV"][x], quads_before(s, *u, 2))
                            nc.vector.tensor_copy(exps_t[x][:, u[0] % 2, :], bank(("pT", x, s, *u))[:]
                                                  ).then_inc(p_t_done[u[0] % 2][x], 1)
                        elif kind == "o_norm":
                            normalise(x, s)
                        elif kind == "sum":
                            add_residual(x, s)
                        elif kind == "stats":
                            norm_stats(x, s)
                        elif kind == "centre":
                            if x == 0 and s == "LN0":
                                dve.wait_ge(ln_loaded, 16 * 2 * len(LN))
                            dve.wait_ge(done["stats"][x], nth("stats", s))
                            src = x_sum[x] if LN[s]["of"] == "sum" else x_run[x]
                            nc.vector.scalar_tensor_tensor(out=x_sum[x][:], in0=src[:], scalar=mean_var[x][:, 0:1],
                                                           in1=gain[s][:], op0=ALU.subtract, op1=ALU.mult
                                                           ).then_inc(done["centre"][x], 1)
                        elif kind == "norm":
                            norm_apply(x, s)
                        elif kind in ("h_t0", "h_t1"):
                            half = int(kind[3])
                            dve.wait_ge(done[f"H{half}"][x], nth(f"H{half}", s))
                            for n in range(QH):
                                f = QH * half + n
                                ins = nc.vector.tensor_scalar(h_t[x][:, f, :], bank((f"H{half}", x, s))[:, 128 * n:128 * n + 128],
                                                              b_1[s][:, f:f + 1], 0.0, ALU.add, ALU.max)
                            ins.then_inc(done[kind][x], 1)

            nc.all_engine_barrier(sems_to_clear=range(first_cleared, last_cleared + 1))


WEIGHTS = sorted({n for d in ATTN.values() for n in d["w"] + (d["b"] or ())}
                 | {d[k] for d in FFN.values() for k in ("w1", "b1", "w2", "b2")}
                 | {d[k] for d in LN.values() for k in ("g", "b")})


def kernel(**inputs):
    import numpy as np
    from concourse import bacc
    from concourse.bass_utils import run_bass_kernel_spmd

    arrays = {n: np.asarray(inputs[n]) for n in WEIGHTS}
    for n in WEIGHTS:
        if n[:3] in ("L1_", "L2_") and n.split("_")[-1][0] == "W":
            arrays[n] = arrays[n].T
        if n in (FFN["F0"]["b1"], FFN["F1"]["b1"]):
            arrays[n] = arrays[n].reshape(FC, 128).T
    arrays["x"] = np.asarray(inputs["x"])
    arrays["ctx_t"] = np.asarray(inputs["ctx_1024"]).transpose(0, 2, 1)
    slot_head = [8 * (u // 2) + 2 * n + u % 2 for u in range(QUADS) for n in range(QH)]
    arrays["fside"] = np.asarray(inputs["fside_Bx16xSxS2_0"])[:, slot_head].transpose(0, 2, 1, 3)
    arrays["ik"] = np.asarray(inputs["mask_BxSxS2_ik1"])
    arrays["kmask"] = np.asarray(inputs["mask_Bx1x1xS2_bf1"])
    arrays["drop"] = np.asarray(inputs["mask_Bx16xSxS2_bk0"])[:, slot_head].transpose(0, 2, 1, 3)
    arrays["sxs"] = np.asarray(inputs["mask_SxS_bk1"])
    arrays = {n: np.ascontiguousarray(a) for n, a in arrays.items()}

    nc = bacc.Bacc("TRN2", target_bir_lowering=False, num_devices=1)
    dram = {n: nc.dram_tensor(f"in_{n}", a.shape, mybir.dt.from_np(a.dtype), kind="ExternalInput").ap()
            for n, a in arrays.items()}
    out = nc.dram_tensor("out_0", (B, N, D), F32, kind="ExternalOutput").ap()
    program(nc, dram, out)
    r = run_bass_kernel_spmd(nc, [{f"in_{n}": a for n, a in arrays.items()}], core_ids=[0])
    return r.results[0]["out_0"]
```

```python
from contextlib import ExitStack

import concourse.bass as bass
from concourse import mybir

F32 = mybir.dt.float32
F16 = mybir.dt.float16
BF16 = mybir.dt.bfloat16
U8 = mybir.dt.uint8
I32 = mybir.dt.int32
ALU = mybir.AluOpType
ACT = mybir.ActivationFunctionType
AX_X = mybir.AxisListType.X

B, N, D, H = 16, 128, 256, 16
DH = D // H
FF = 1024
KC = D // 128
FC = FF // 128
QUADS, QH = 4, 4
STREAMS = 2
MASKED = -(2.0 ** 100)
OVERFLOW = 2.0 ** 60
CHAIN_BANKS = 3

ATTN = {
    "A0": dict(w=("L0_xattn_mha_wq", "L0_xattn_mha_wk", "L0_xattn_mha_wv", "L0_xattn_mha_wo"), b=None,
               kv="self", mask=0, nan=True, pre=False, next=["LN0"]),
    "A1": dict(w=("L0_xattn_cmha_wq", "L0_xattn_cmha_wk", "L0_xattn_cmha_wv", "L0_xattn_cmha_wo"), b=None,
               kv="ctx", mask=1, nan=True, pre=False, next=["LN1"]),
    "A2": dict(w=("L1_xattn_Wq", "L1_xattn_Wk", "L1_xattn_Wv", "L1_xattn_Wo"),
               b=("L1_xattn_bq", "L1_xattn_bk", "L1_xattn_bv", "L1_xattn_bo"),
               kv="ctx", mask=2, nan=False, pre=False, next=["LN3"]),
    "A3": dict(w=("L2_xattn_Wq", "L2_xattn_Wk", "L2_xattn_Wv", "L2_xattn_Wo"),
               b=("L2_xattn_bq", "L2_xattn_bk", "L2_xattn_bv", "L2_xattn_bo"),
               kv="ctx", mask=None, nan=True, pre=False, next=["LN4", "LN5"]),
    "A4": dict(w=("L3_xattn_ca_qw", "L3_xattn_ca_kw", "L3_xattn_ca_vw", "L3_xattn_ca_ow"),
               b=("L3_xattn_ca_qb", "L3_xattn_ca_kb", "L3_xattn_ca_vb", "L3_xattn_ca_ob"),
               kv="ctx", mask=None, nan=False, pre=True, next=["LN6"]),
    "A5": dict(w=("L3_xattn_sa_qw", "L3_xattn_sa_kw", "L3_xattn_sa_vw", "L3_xattn_sa_ow"),
               b=("L3_xattn_sa_qb", "L3_xattn_sa_kb", "L3_xattn_sa_vb", "L3_xattn_sa_ob"),
               kv="self", mask=3, nan=True, pre=True, next=["LN7"]),
}
FFN = {
    "F0": dict(w1="L0_xattn_ff_w1", b1="L0_xattn_ff_b1", w2="L0_xattn_ff_w2", b2="L0_xattn_ff_b2",
               gelu=False, pre=False, next=["LN2"]),
    "F1": dict(w1="L3_xattn_w1", b1="L3_xattn_b1", w2="L3_xattn_w2", b2="L3_xattn_b2",
               gelu=True, pre=True, next=[]),
}
STAGES = ["A0", "A1", "F0", "A2", "A3", "A4", "A5", "F1"]
LN = {
    "LN0": dict(g="L0_xattn_g1", b="L0_xattn_b1", ddof=1, eps=1e-6, on_root=True, to="x", of="sum", after=("sum", "A0")),
    "LN1": dict(g="L0_xattn_g2", b="L0_xattn_b2", ddof=1, eps=1e-6, on_root=True, to="x", of="sum", after=("sum", "A1")),
    "LN2": dict(g="L0_xattn_g3", b="L0_xattn_b3", ddof=1, eps=1e-6, on_root=True, to="x", of="sum", after=("sum", "F0")),
    "LN3": dict(g="L1_xattn_gamma", b="L1_xattn_beta", ddof=0, eps=1e-6, on_root=False, to="x", of="sum", after=("sum", "A2")),
    "LN4": dict(g="L2_xattn_gamma", b="L2_xattn_beta", ddof=0, eps=1e-5, on_root=False, to="x", of="sum", after=("sum", "A3")),
    "LN5": dict(g="L3_xattn_ln1_g", b="L3_xattn_ln1_b", ddof=0, eps=1e-5, on_root=False, to="xn", of="x", after=("norm", "LN4")),
    "LN6": dict(g="L3_xattn_ln2_g", b="L3_xattn_ln2_b", ddof=0, eps=1e-5, on_root=False, to="xn", of="x", after=("sum", "A4")),
    "LN7": dict(g="L3_xattn_ln3_g", b="L3_xattn_ln3_b", ddof=0, eps=1e-5, on_root=False, to="xn", of="x", after=("sum", "A5")),
}


def norms_after(s):
    return (ATTN.get(s) or FFN[s])["next"]


VECTORS = {s: list((ATTN[s]["b"] or ()) if s in ATTN else (FFN[s]["b2"],))
           + [LN[n][k] for n in norms_after(s) for k in ("g", "b")] for s in STAGES}
WEIGHT_COLS = {s: 4 * KC * D if s in ATTN else KC * FF + FC * D + FC for s in STAGES}


def stream_beats():
    beats = [("bias", "in")]
    for s in STAGES:
        beats += [("xT", s), ("x_t", s)]
        if s in ATTN:
            beats += [(k, s) for k in ("kv", "k32", "v", "k_high", "k_low", "kT", "k_stack",
                                       "q", "q32", "q_high", "q_low", "qT", "q_stack")]
            for u in range(QUADS):
                beats += [("S", s, u)] + ([("times", s, u), ("lower", s, u)] if s == "A3" else [])
                beats += [("max", s, u), ("exp", s, u), ("pT", s, u), ("p_t", s, u), ("PV", s, u)]
            beats += [("flag", s)] if ATTN[s]["nan"] else []
            beats += [(k, s) for k in ("o_raw", "oT", "o_norm", "nT", "o_t", "O", "sum")]
        else:
            beats += [(k, s) for k in ("H0", "h_t0", "H1", "h_t1", "Y", "sum")]
        for n in norms_after(s):
            beats += [(k, n) for k in ("stats", "centre", "root", "norm")]
            beats += [("res", n)] if MAKES_RES[n] else []
    return beats


FED_BY = {"LN0": "A1", "LN1": "F0", "LN2": "A2", "LN3": "A3", "LN4": None, "LN5": "A4", "LN6": "A5", "LN7": "F1"}
MAKES_RES = {n: bool(s and (s in FFN or ATTN[s]["b"])) for n, s in FED_BY.items()}

NTH, _seen = {}, {}
for _beat in stream_beats():
    _kind = _beat[0] if _beat[0] != "p_t" else ("p_t", _beat[2] % 2)
    NTH[_beat] = _seen[_kind] = _seen.get(_kind, 0) + 1

TENSOR = """
xT.0.A0 xT.1.A0 q.0.A0 kv.0.A0 kv.1.A0 qT.0.A0 kT.0.A0 q.1.A0 S.0.A0.0 S.0.A0.1 kT.1.A0 qT.1.A0 S.0.A0.2 pT.0.A0.0
S.1.A0.0 pT.0.A0.1 PV.0.A0.0 S.0.A0.3 S.1.A0.1 PV.0.A0.1 pT.0.A0.2 S.1.A0.2 pT.0.A0.3 PV.0.A0.2 PV.0.A0.3 S.1.A0.3
pT.1.A0.0 oT.0.A0 pT.1.A0.1 PV.1.A0.0 pT.1.A0.2 PV.1.A0.1 nT.0.A0 kv.0.A1 O.0.A0 PV.1.A0.2 pT.1.A0.3 kT.0.A1
PV.1.A0.3 kv.1.A1 xT.0.A1 oT.1.A0 q.0.A1 nT.1.A0 kT.1.A1 O.1.A0 qT.0.A1 S.0.A1.0 S.0.A1.1 xT.1.A1 q.1.A1 S.0.A1.2
pT.0.A1.0 S.0.A1.3 pT.0.A1.1 PV.0.A1.0 pT.0.A1.2 qT.1.A1 PV.0.A1.1 pT.0.A1.3 PV.0.A1.2 S.1.A1.0 S.1.A1.1 PV.0.A1.3
kv.0.A2 oT.0.A1 pT.1.A1.0 S.1.A1.2 pT.1.A1.1 S.1.A1.3 nT.0.A1 PV.1.A1.0 PV.1.A1.1 kT.0.A2 pT.1.A1.2 O.0.A1
pT.1.A1.3 PV.1.A1.2 PV.1.A1.3 kv.1.A2 xT.0.F0 oT.1.A1 H1.0.F0 nT.1.A1 H0.0.F0 O.1.A1 kT.1.A2 Y.0.F0 xT.1.F0
H0.1.F0 H1.1.F0 xT.0.A2 q.0.A2 Y.1.F0 qT.0.A2 S.0.A2.0 S.0.A2.1 xT.1.A2 q.1.A2 S.0.A2.2 pT.0.A2.0 S.0.A2.3
pT.0.A2.1 PV.0.A2.0 qT.1.A2 pT.0.A2.2 PV.0.A2.1 S.1.A2.0 pT.0.A2.3 S.1.A2.1 PV.0.A2.2 PV.0.A2.3 kv.0.A3 oT.0.A2
pT.1.A2.0 S.1.A2.2 pT.1.A2.1 S.1.A2.3 nT.0.A2 PV.1.A2.0 kT.0.A3 PV.1.A2.1 pT.1.A2.2 O.0.A2 pT.1.A2.3 PV.1.A2.2
PV.1.A2.3 kv.1.A3 xT.0.A3 oT.1.A2 q.0.A3 nT.1.A2 kT.1.A3 O.1.A2 qT.0.A3 S.0.A3.0 S.0.A3.1 xT.1.A3 S.0.A3.2 q.1.A3
S.0.A3.3 pT.0.A3.0 PV.0.A3.0 qT.1.A3 pT.0.A3.1 pT.0.A3.2 S.1.A3.0 PV.0.A3.1 S.1.A3.1 S.1.A3.2 pT.0.A3.3 PV.0.A3.2
S.1.A3.3 PV.0.A3.3 kv.0.A4 oT.0.A3 pT.1.A3.0 PV.1.A3.0 nT.0.A3 pT.1.A3.1 O.0.A3 kT.0.A4 PV.1.A3.1 pT.1.A3.2
pT.1.A3.3 PV.1.A3.2 PV.1.A3.3 kv.1.A4 xT.0.A4 oT.1.A3 q.0.A4 nT.1.A3 kT.1.A4 O.1.A3 qT.0.A4 S.0.A4.0 S.0.A4.1
S.0.A4.2 pT.0.A4.0 xT.1.A4 S.0.A4.3 pT.0.A4.1 q.1.A4 pT.0.A4.2 PV.0.A4.0 PV.0.A4.1 pT.0.A4.3 PV.0.A4.2 qT.1.A4
PV.0.A4.3 S.1.A4.0 S.1.A4.1 oT.0.A4 S.1.A4.2 nT.0.A4 pT.1.A4.0 S.1.A4.3 pT.1.A4.1 O.0.A4 PV.1.A4.0 pT.1.A4.2
PV.1.A4.1 pT.1.A4.3 PV.1.A4.2 PV.1.A4.3 xT.0.A5 oT.1.A4 kv.0.A5 nT.1.A4 q.0.A5 O.1.A4 kT.0.A5 qT.0.A5 S.0.A5.0
xT.1.A5 S.0.A5.1 kv.1.A5 q.1.A5 S.0.A5.2 pT.0.A5.0 S.0.A5.3 kT.1.A5 pT.0.A5.1 PV.0.A5.0 qT.1.A5 pT.0.A5.2
PV.0.A5.1 S.1.A5.0 pT.0.A5.3 PV.0.A5.2 S.1.A5.1 PV.0.A5.3 S.1.A5.2 pT.1.A5.0 oT.0.A5 pT.1.A5.1 S.1.A5.3 PV.1.A5.0
pT.1.A5.2 nT.0.A5 PV.1.A5.1 PV.1.A5.2 pT.1.A5.3 O.0.A5 PV.1.A5.3 oT.1.A5 nT.1.A5 xT.0.F1 O.1.A5 H0.0.F1 H1.0.F1
xT.1.F1 H0.1.F1 H1.1.F1 Y.0.F1 Y.1.F1
"""
VECTOR = """
bias.1.in bias.0.in x_t.1.A0 q32.0.A0 q_low.0.A0 k32.0.A0 v.0.A0 k_low.0.A0 k32.1.A0 v.1.A0 k_stack.0.A0 q32.1.A0
k_low.1.A0 max.0.A0.0 q_low.1.A0 max.0.A0.1 k_stack.1.A0 q_stack.1.A0 max.0.A0.2 max.1.A0.0 p_t.0.A0.1 max.0.A0.3
max.1.A0.1 max.1.A0.2 p_t.0.A0.3 max.1.A0.3 p_t.1.A0.0 o_norm.0.A0 p_t.1.A0.2 o_t.0.A0 k32.0.A1 sum.0.A0
k_low.0.A1 stats.0.LN0 centre.0.LN0 k_stack.0.A1 norm.0.LN0 k32.1.A1 o_norm.1.A0 k_low.1.A1 q32.0.A1 k_stack.1.A1
q_low.0.A1 sum.1.A0 stats.1.LN0 centre.1.LN0 norm.1.LN0 max.0.A1.0 x_t.1.A1 max.0.A1.1 q32.1.A1 max.0.A1.2
p_t.0.A1.0 max.0.A1.3 q_low.1.A1 p_t.0.A1.1 p_t.0.A1.2 q_stack.1.A1 p_t.0.A1.3 max.1.A1.0 max.1.A1.1 k32.0.A2
v.0.A2 o_norm.0.A1 max.1.A1.2 k_low.0.A2 max.1.A1.3 o_t.0.A1 k_stack.0.A2 p_t.1.A1.2 sum.0.A1 stats.0.LN1
centre.0.LN1 norm.0.LN1 k32.1.A2 v.1.A2 o_norm.1.A1 k_low.1.A2 h_t1.0.F0 o_t.1.A1 h_t0.0.F0 sum.1.A1 stats.1.LN1
k_stack.1.A2 centre.1.LN1 norm.1.LN1 sum.0.F0 stats.0.LN2 centre.0.LN2 norm.0.LN2 h_t0.1.F0 h_t1.1.F0 q32.0.A2
q_low.0.A2 sum.1.F0 stats.1.LN2 centre.1.LN2 norm.1.LN2 max.0.A2.0 x_t.1.A2 max.0.A2.1 q32.1.A2 max.0.A2.2
q_low.1.A2 max.0.A2.3 p_t.0.A2.1 q_stack.1.A2 p_t.0.A2.2 max.1.A2.0 max.1.A2.1 k32.0.A3 v.0.A3 o_norm.0.A2
max.1.A2.2 k_low.0.A3 max.1.A2.3 k_stack.0.A3 sum.0.A2 stats.0.LN3 centre.0.LN3 norm.0.LN3 k32.1.A3 v.1.A3
o_norm.1.A2 k_low.1.A3 q32.0.A3 q_low.0.A3 sum.1.A2 stats.1.LN3 centre.1.LN3 norm.1.LN3 times.0.A3.0 times.0.A3.1
lower.0.A3.0 times.0.A3.2 max.0.A3.0 times.0.A3.3 lower.0.A3.1 q32.1.A3 max.0.A3.1 lower.0.A3.2 q_low.1.A3
max.0.A3.2 lower.0.A3.3 q_stack.1.A3 max.0.A3.3 times.1.A3.0 times.1.A3.1 lower.1.A3.0 times.1.A3.2 max.1.A3.0
times.1.A3.3 lower.1.A3.1 max.1.A3.1 k32.0.A4 o_norm.0.A3 lower.1.A3.2 v.0.A4 max.1.A3.2 k_low.0.A4 lower.1.A3.3
max.1.A3.3 sum.0.A3 stats.0.LN4 k_stack.0.A4 centre.0.LN4 norm.0.LN4 stats.0.LN5 centre.0.LN5 norm.0.LN5 k32.1.A4
v.1.A4 o_norm.1.A3 k_low.1.A4 q32.0.A4 q_low.0.A4 sum.1.A3 stats.1.LN4 centre.1.LN4 norm.1.LN4 max.0.A4.0
stats.1.LN5 max.0.A4.1 centre.1.LN5 norm.1.LN5 max.0.A4.2 x_t.1.A4 max.0.A4.3 p_t.0.A4.1 q32.1.A4 p_t.0.A4.2
q_low.1.A4 p_t.0.A4.3 max.1.A4.0 max.1.A4.1 o_norm.0.A4 max.1.A4.2 p_t.1.A4.0 max.1.A4.3 p_t.1.A4.1 sum.0.A4
stats.0.LN6 centre.0.LN6 norm.0.LN6 x_t.0.A5 o_norm.1.A4 k32.0.A5 v.0.A5 q32.0.A5 k_low.0.A5 sum.1.A4 q_low.0.A5
stats.1.LN6 centre.1.LN6 norm.1.LN6 max.0.A5.0 max.0.A5.1 k32.1.A5 v.1.A5 q32.1.A5 k_low.1.A5 max.0.A5.2
q_low.1.A5 max.0.A5.3 k_stack.1.A5 q_stack.1.A5 p_t.0.A5.2 max.1.A5.0 p_t.0.A5.3 max.1.A5.1 max.1.A5.2 p_t.1.A5.0
o_norm.0.A5 max.1.A5.3 p_t.1.A5.2 sum.0.A5 stats.0.LN7 centre.0.LN7 o_norm.1.A5 norm.0.LN7 sum.1.A5 stats.1.LN7
centre.1.LN7 norm.1.LN7 x_t.1.F1 sum.0.F1 sum.1.F1
"""
SCALAR = """
x_t.0.A0 q_high.0.A0 k_high.0.A0 q_stack.0.A0 k_high.1.A0 q_high.1.A0 exp.0.A0.0 exp.0.A0.1 p_t.0.A0.0 exp.0.A0.2
exp.1.A0.0 exp.0.A0.3 p_t.0.A0.2 exp.1.A0.1 o_raw.0.A0 exp.1.A0.2 p_t.1.A0.1 exp.1.A0.3 k_high.0.A1 v.0.A1
p_t.1.A0.3 o_raw.1.A0 x_t.0.A1 v.1.A1 k_high.1.A1 o_t.1.A0 q_high.0.A1 q_stack.0.A1 exp.0.A1.0 exp.0.A1.1
q_high.1.A1 exp.0.A1.2 exp.0.A1.3 o_raw.0.A1 exp.1.A1.0 exp.1.A1.1 k_high.0.A2 p_t.1.A1.0 p_t.1.A1.1 exp.1.A1.2
exp.1.A1.3 p_t.1.A1.3 o_raw.1.A1 x_t.0.F0 k_high.1.A2 x_t.1.F0 x_t.0.A2 q_high.0.A2 q_stack.0.A2 exp.0.A2.0
exp.0.A2.1 q_high.1.A2 p_t.0.A2.0 exp.0.A2.2 exp.0.A2.3 p_t.0.A2.3 exp.1.A2.0 o_raw.0.A2 exp.1.A2.1 k_high.0.A3
p_t.1.A2.0 p_t.1.A2.1 exp.1.A2.2 o_t.0.A2 exp.1.A2.3 p_t.1.A2.2 p_t.1.A2.3 o_raw.1.A2 x_t.0.A3 k_high.1.A3
o_t.1.A2 q_high.0.A3 k_stack.1.A3 q_stack.0.A3 x_t.1.A3 exp.0.A3.0 q_high.1.A3 p_t.0.A3.0 exp.0.A3.1 exp.0.A3.2
p_t.0.A3.1 exp.0.A3.3 p_t.0.A3.2 p_t.0.A3.3 o_raw.0.A3 exp.1.A3.0 exp.1.A3.1 p_t.1.A3.0 k_high.0.A4 o_t.0.A3
exp.1.A3.2 p_t.1.A3.1 exp.1.A3.3 p_t.1.A3.2 p_t.1.A3.3 o_raw.1.A3 x_t.0.A4 k_high.1.A4 o_t.1.A3 q_high.0.A4
k_stack.1.A4 q_stack.0.A4 exp.0.A4.0 exp.0.A4.1 p_t.0.A4.0 exp.0.A4.2 exp.0.A4.3 q_high.1.A4 q_stack.1.A4
o_raw.0.A4 exp.1.A4.0 exp.1.A4.1 o_t.0.A4 exp.1.A4.2 exp.1.A4.3 p_t.1.A4.2 p_t.1.A4.3 o_raw.1.A4 o_t.1.A4
k_high.0.A5 q_high.0.A5 k_stack.0.A5 q_stack.0.A5 x_t.1.A5 exp.0.A5.0 exp.0.A5.1 k_high.1.A5 q_high.1.A5
p_t.0.A5.0 exp.0.A5.2 p_t.0.A5.1 exp.0.A5.3 exp.1.A5.0 o_raw.0.A5 exp.1.A5.1 exp.1.A5.2 p_t.1.A5.1 exp.1.A5.3
o_t.0.A5 p_t.1.A5.3 o_raw.1.A5 o_t.1.A5 x_t.0.F1 h_t0.0.F1 h_t1.0.F1 h_t0.1.F1 h_t1.1.F1
"""
POOL = """
flag.0.A0 flag.1.A0 root.0.LN0 root.1.LN0 flag.0.A1 flag.1.A1 root.0.LN1 res.0.LN1 root.1.LN1 res.1.LN1 root.0.LN2
res.0.LN2 root.1.LN2 res.1.LN2 root.0.LN3 res.0.LN3 root.1.LN3 res.1.LN3 flag.0.A3 flag.1.A3 root.0.LN4 root.0.LN5
res.0.LN5 root.1.LN4 root.1.LN5 res.1.LN5 root.0.LN6 res.0.LN6 root.1.LN6 res.1.LN6 flag.0.A5 flag.1.A5 root.0.LN7
res.0.LN7 root.1.LN7 res.1.LN7
"""


def parse(text):
    beats = []
    for word in text.split():
        kind, x, *where = word.split(".")
        beats.append((kind, int(x), where[0], *(int(u) for u in where[1:])))
    return beats


TENSOR_ORDER, VECTOR_ORDER, SCALAR_ORDER, POOL_ORDER = (parse(t) for t in (TENSOR, VECTOR, SCALAR, POOL))
assert sorted(TENSOR_ORDER + VECTOR_ORDER + SCALAR_ORDER + POOL_ORDER) == sorted(
    (b[0], x, *b[1:]) for b in stream_beats() for x in range(STREAMS))

READERS = {"xT": ["x_t"], "kv": ["k32", "v"], "kT": ["k_stack"], "q": ["q32"], "qT": ["q_stack"], "pT": ["p_t"],
           "oT": ["o_norm"], "nT": ["o_t"], "O": ["sum"], "H0": ["h_t0"], "H1": ["h_t1"], "Y": ["sum"]}
COPIES = ("x_t", "v", "k_stack", "q_stack", "p_t", "o_t")
FILLS = [beat for beat in TENSOR_ORDER if beat[0] in READERS]
FILL_AT = {beat: n for n, beat in enumerate(FILLS)}
OUTPUT_TURNS = [beat[1:3] for beat in TENSOR_ORDER if beat[0] == "PV" and beat[3] == 0]


def program(nc, dram, out):
    with ExitStack() as ctx:
        def sb(name, shape, dt=F32):
            return ctx.enter_context(nc.sbuf_tensor(name, shape, dt))

        def pb(name, shape=(128, 512), dt=F32):
            return ctx.enter_context(nc.psum_tensor(name, list(shape), dt))

        def sem(name):
            return ctx.enter_context(nc.semaphore(name))

        weights = {s: sb(f"weights_{s}", [128, WEIGHT_COLS[s]]) for s in STAGES}
        vectors = {s: sb(f"vectors_{s}", [128, D * len(VECTORS[s])]) for s in STAGES if VECTORS[s]}

        def chunks(s, first, count, width):
            return weights[s][:, first:first + count * width].rearrange("p (c n) -> p c n", c=count)

        def vector(s, name, count=1):
            at = D * VECTORS[s].index(name)
            return vectors[s][:, at:at + D * count]

        w_kv = {s: chunks(s, 0, KC, 2 * D) for s in ATTN}
        w_q = {s: chunks(s, 2 * KC * D, KC, D) for s in ATTN}
        w_o = {s: chunks(s, 3 * KC * D, KC, D) for s in ATTN}
        w_1 = {s: chunks(s, 0, KC, FF) for s in FFN}
        w_2 = {s: chunks(s, KC * FF, FC, D) for s in FFN}
        b_1 = {s: weights[s][:, KC * FF + FC * D:] for s in FFN}
        b_q = {s: vector(s, ATTN[s]["b"][0]) for s in ATTN if ATTN[s]["b"]}
        b_kv = {s: vector(s, ATTN[s]["b"][1], 2) for s in ATTN if ATTN[s]["b"]}
        b_res = {s: vector(s, FFN[s]["b2"] if s in FFN else ATTN[s]["b"][3]) for s in STAGES if s in FFN or ATTN[s]["b"]}
        gain = {n: vector(s, LN[n]["g"]) for s in STAGES for n in norms_after(s)}
        shift = {n: vector(s, LN[n]["b"]) for s in STAGES for n in norms_after(s)}

        id32 = sb("id32", [128, 128])
        id16 = sb("id16", [128, 128], F16)
        idb = sb("idb", [128, 128], BF16)
        causal = sb("causal", [128, 128], BF16)
        halves = sb("halves", [128, 2])
        overflow = sb("overflow", [128, H])
        sxs_raw = sb("sxs_raw", [128, 128], U8)
        sxs_bias = sb("sxs_bias", [128, 128], BF16)

        def per_stream(name, shape, dt=F32):
            return [sb(f"{name}{x}", shape, dt) for x in range(STREAMS)]

        x_run = per_stream("x_run", [128, D])
        x_norm = per_stream("x_norm", [128, D])
        x_sum = per_stream("x_sum", [128, D])
        x_res = per_stream("x_res", [128, D])
        x_t = per_stream("x_t", [128, KC, N])
        ctx_t = per_stream("ctx_t", [128, KC, N])
        q32 = per_stream("q32", [128, D])
        k32 = per_stream("k32", [128, D])
        q_parts = per_stream("q_parts", [128, H, 4, DH], F16)
        k_parts = per_stream("k_parts", [128, H, 4, DH], F16)
        q_stack = per_stream("q_stack", [128, H // 2, N], F16)
        k_stack = per_stream("k_stack", [128, H // 2, N], F16)
        v_one = per_stream("v_one", [128, H, 2 * DH])
        key_raw = per_stream("key_raw", [128, 128], U8)
        ik_raw = per_stream("ik_raw", [128, 128], I32)
        bias = per_stream("bias", [128, 3, 128], BF16)
        weight = per_stream("weight", [128, H, N])
        drop_raw = per_stream("drop_raw", [128, H, N], U8)
        neg_max = per_stream("neg_max", [128, H])
        grown = per_stream("grown", [128, H])
        nan_flag = per_stream("nan_flag", [128, H])
        exps = per_stream("exps", [128, 2, QH * N])
        exps_t = per_stream("exps_t", [128, 2, QH * N])
        o_raw = per_stream("o_raw", [128, QUADS, N])
        recip = per_stream("recip", [128, 2, H])
        o_norm = per_stream("o_norm", [128, D])
        o_t = per_stream("o_t", [128, KC, N])
        h_t = per_stream("h_t", [128, FC, N])
        bn = per_stream("bn", [128, 6])
        mean_var = per_stream("mean_var", [128, 2])
        var_eps = per_stream("var_eps", [128, 1])
        root = per_stream("root", [128, 1])
        root_eps = per_stream("root_eps", [128, 1])
        inv_root = per_stream("inv_root", [128, 1])

        s_bank = [[pb(f"s_bank{x}_{r}") for r in range(2)] for x in range(STREAMS)]
        o_bank = pb("o_bank")
        chain = [pb(f"chain{b}") for b in range(CHAIN_BANKS)]

        stage_loaded = {s: sem(f"stage_loaded_{s}") for s in STAGES}
        sxs_loaded = sem("sxs_loaded")
        first_x_loaded = [sem(f"first_x_loaded{x}") for x in range(STREAMS)]
        first_ctx_loaded = [sem(f"first_ctx_loaded{x}") for x in range(STREAMS)]
        first_masks_loaded = [sem(f"first_masks_loaded{x}") for x in range(STREAMS)]
        first_weight_loaded = [sem(f"first_weight_loaded{x}") for x in range(STREAMS)]
        cleared = sem("cleared")
        const_made = sem("const_made")
        buffers_cleared = sem("buffers_cleared")
        sxs_made = sem("sxs_made")

        def sems(name):
            return [sem(f"{name}{x}") for x in range(STREAMS)]

        x_loaded = sems("x_loaded")
        ctx_loaded = sems("ctx_loaded")
        masks_loaded = sems("masks_loaded")
        weight_loaded = sems("weight_loaded")
        stored = sems("stored")
        key_bias_made = sems("key_bias_made")
        done = {k: sems(f"done_{k}_") for k in ("xT", "kv", "kT", "q", "qT", "S", "pT", "PV", "oT", "nT", "O",
                                                "H0", "H1", "Y")}
        done |= {k: sems(f"done_{k}_") for k in ("bias", "x_t", "k32", "v", "k_high", "k_low", "k_stack", "q32",
                                                 "q_high", "q_low", "q_stack", "times", "lower", "max", "exp",
                                                 "flag", "o_raw", "o_norm", "o_t", "sum", "h_t0", "h_t1",
                                                 "stats", "centre", "root", "norm", "res")}
        p_t_done = [sems("p_t_even_done"), sems("p_t_odd_done")]
        grown_made = sems("grown_made")
        recip_made = sems("recip_made")
        recip_flagged = sems("recip_flagged")
        bn_made = sems("bn_made")
        aggr_made = sems("aggr_made")
        root_shifted = sems("root_shifted")
        root_inverted = sems("root_inverted")

        first_cleared, last_cleared = x_loaded[0].num, root_inverted[-1].num

        def nth(*beat):
            return NTH[beat]

        def quads_before(s, u, back):
            return QUADS * list(ATTN).index(s) + u + 1 - back

        def bank(beat):
            return chain[FILL_AT[beat] % CHAIN_BANKS]

        def last_readers(beat):
            n = FILL_AT[beat] - CHAIN_BANKS
            if n < 0:
                return []
            kind, x, *where = FILLS[n]
            return [(p_t_done[where[1] % 2][x] if r == "p_t" else done[r][x], nth(r, *where)) for r in READERS[kind]]

        def source(s):
            return {"A0": None, "A1": "LN0", "F0": "LN1", "A2": "LN2", "A3": "LN3", "A4": "LN5",
                    "A5": "LN6", "F1": "LN7"}[s]

        def stage_input(x, s):
            d = ATTN.get(s) or FFN[s]
            return x_norm[x] if d["pre"] else x_run[x]

        def feeds_res(s):
            return next((n for n, made in MAKES_RES.items() if made and FED_BY[n] == s), None)

        def residual(x, s):
            return x_res[x] if feeds_res(s) else x_run[x]

        def mask_bias(x, s):
            m = ATTN[s]["mask"]
            return sxs_bias[:] if m == 3 else bias[x][:, m, :]

        def four(ap):
            return ap.unsqueeze(1).broadcast_to([128, QH, 128])

        def slots(u):
            return slice(QH * u, QH * u + QH)

        def all_loaded(s):
            return 32

        def one(name, b):
            t = dram[name]
            dims = " ".join("cdef"[:len(t.shape) - 1])
            return t[bass.ds(b, 1)].rearrange(f"a {dims} -> (a {dims[0]}) {dims[2:]}")

        def load_x(queue, x, b, loaded):
            queue.dma_start(x_run[x][:], one("x", b)).then_inc(loaded[x], 16)

        def load_ctx(queue, x, b, loaded):
            queue.dma_start(ctx_t[x][:], dram["ctx_t"][bass.ds(b, 1)].rearrange("a (c p) n -> p (a c) n", p=128)
                            ).then_inc(loaded[x], 16)

        def load_masks(queue, x, b, loaded):
            queue.dma_start(key_raw[x][:], dram["kmask"][bass.ds(b, 1)].rearrange("a c d e -> (a c d) e")
                            .broadcast_to([128, N])).then_inc(loaded[x], 16)
            queue.dma_start(ik_raw[x][:], one("ik", b)).then_inc(loaded[x], 16)

        def load_weight(queue, x, b, loaded):
            queue.dma_start(weight[x][:], one("fside", b)).then_inc(loaded[x], 16)
            queue.dma_start(drop_raw[x][:], one("drop", b)).then_inc(loaded[x], 16)

        def load_stage(queue, s):
            queue.dma_start(weights[s][:], dram[f"weights_{s}"]).then_inc(stage_loaded[s], 16)
            queue.dma_start(vectors[s][:], dram[f"vectors_{s}"].rearrange("(a n) -> a n", a=1)
                            .broadcast_to([128, D * len(VECTORS[s])])).then_inc(stage_loaded[s], 16)

        with nc.Block() as block:
            @block.scalar
            def _(act):
                load_stage(act, "A0")
                for x in range(STREAMS):
                    load_ctx(act, x, x, first_ctx_loaded)
                for s in ("F0", "A3", "A5"):
                    load_stage(act, s)

            @block.sync
            def _(sp):
                for x in range(STREAMS):
                    load_x(sp, x, x, first_x_loaded)
                for x in range(STREAMS):
                    load_masks(sp, x, x, first_masks_loaded)
                sp.dma_start(sxs_raw[:], dram["sxs"]).then_inc(sxs_loaded, 16)
                load_stage(sp, "A1")
                load_stage(sp, "A2")
                for x in range(STREAMS):
                    load_weight(sp, x, x, first_weight_loaded)
                load_stage(sp, "A4")
                load_stage(sp, "F1")

            @block.gpsimd
            def _(pool):
                for t in (id32, id16, idb, causal):
                    nc.gpsimd.memset(t[:], 0.0).then_inc(cleared, 1)
                nc.gpsimd.memset(halves[:, 0:1], -0.5).then_inc(const_made, 1)
                nc.gpsimd.memset(halves[:, 1:2], 0.5).then_inc(const_made, 1)
                nc.gpsimd.memset(overflow[:], OVERFLOW).then_inc(const_made, 1)
                pool.wait_ge(cleared, 4)
                for t in (id32, id16, idb):
                    nc.gpsimd.affine_select(out=t[:], in_=t[:], compare_op=ALU.not_equal, fill=1.0, base=0,
                                            pattern=[[-1, 128]], channel_multiplier=1).then_inc(const_made, 1)
                nc.gpsimd.affine_select(out=causal[:], in_=causal[:], compare_op=ALU.is_ge, fill=MASKED, base=0,
                                        pattern=[[-1, 128]], channel_multiplier=1).then_inc(const_made, 1)

            @block.vector
            def _(dve):
                for x in range(STREAMS):
                    nc.vector.memset(v_one[x][:, :, DH:DH + 1], 1.0).then_inc(buffers_cleared, 1)
                    nc.vector.memset(v_one[x][:, :, DH + 1:2 * DH], 0.0).then_inc(buffers_cleared, 1)
                    nc.vector.memset(q_parts[x][:, :, 3, :], 0.0).then_inc(buffers_cleared, 1)
                    nc.vector.memset(k_parts[x][:, :, 3, :], 0.0).then_inc(buffers_cleared, 1)
                dve.wait_ge(sxs_loaded, 16)
                nc.vector.tensor_scalar(sxs_bias[:], sxs_raw[:], 0.0, MASKED, ALU.is_gt, ALU.mult
                                        ).then_inc(sxs_made, 1)

        with nc.Fori(0, B // STREAMS) as i:
            with nc.Block() as block:

                @block.sync
                def _(sp):
                    following = [(STREAMS * i + STREAMS + x) & (B - 1) for x in range(STREAMS)]
                    for x in range(STREAMS):
                        sp.wait_ge(done["bias"][x], 1)
                        load_masks(sp, x, following[x], masks_loaded)
                    for x in range(STREAMS):
                        sp.wait_ge(done["exp"][x], nth("exp", "A3", QUADS - 1))
                        load_weight(sp, x, following[x], weight_loaded)
                    for x in range(STREAMS):
                        sp.wait_ge(done["kv"][x], nth("kv", "A4"))
                        load_ctx(sp, x, following[x], ctx_loaded)
                    for x in range(STREAMS):
                        sp.wait_ge(done["res"][x], nth("res", "LN7"))
                        load_x(sp, x, following[x], x_loaded)
                    for x in range(STREAMS):
                        sp.wait_ge(done["sum"][x], nth("sum", "F1"))
                        sp.dma_start(out[bass.ds(STREAMS * i + x, 1)].rearrange("a q d -> (a q) d"), x_sum[x][:]
                                     ).then_inc(stored[x], 16)
                    for x in range(STREAMS):
                        sp.wait_ge(masks_loaded[x], 32)
                        sp.wait_ge(weight_loaded[x], 32)
                        sp.wait_ge(ctx_loaded[x], 16)
                        sp.wait_ge(x_loaded[x], 16)
                        sp.wait_ge(stored[x], 16)

                @block.gpsimd
                def _(pool):
                    def row_flags(x, s):
                        pool.wait_ge(done["max"][x], nth("max", s, QUADS - 1))
                        nc.gpsimd.tensor_tensor(grown[x][:], neg_max[x][:], overflow[:], ALU.mult
                                                ).then_inc(grown_made[x], 1)
                        pool.wait_ge(grown_made[x], nth("flag", s))
                        nc.gpsimd.tensor_tensor(nan_flag[x][:], grown[x][:], grown[x][:], ALU.subtract
                                                ).then_inc(done["flag"][x], 1)

                    def var_root(x, n):
                        pool.wait_ge(done["stats"][x], nth("stats", n))
                        e = 1 if LN[n]["on_root"] else 0
                        nc.gpsimd.tensor_tensor(root[x][:], var_eps[x][:], halves[:, e:e + 1], ALU.pow
                                                ).then_inc(done["root"][x], 1)

                    def next_residual(x, n):
                        s = FED_BY[n]
                        pool.wait_ge(done["norm"][x], nth("norm", n))
                        pool.wait_ge(stage_loaded[s], all_loaded(s))
                        nc.gpsimd.tensor_tensor(x_res[x][:], x_run[x][:], b_res[s], ALU.add
                                                ).then_inc(done["res"][x], 1)

                    for kind, x, *where in POOL_ORDER:
                        if kind == "flag":
                            row_flags(x, *where)
                        elif kind == "root":
                            var_root(x, *where)
                        elif kind == "res":
                            next_residual(x, *where)

                @block.tensor
                def _(pe):
                    def free_bank(beat):
                        for read, times in last_readers(beat):
                            pe.wait_ge(read, times)
                        return bank(beat)

                    def transposes32(dst, src, blocks):
                        for c in range(blocks):
                            mm = nc.tensor.matmul(dst[:, 128 * c:128 * c + 128], src[:, 128 * c:128 * c + 128], id32[:],
                                                  start=True, stop=True, is_transpose=True)
                        return mm

                    def product(dst, left, right, chunks):
                        for c in range(chunks):
                            mm = nc.tensor.matmul(dst, left[:, c, :], right[:, c, :], start=(c == 0), stop=(c == chunks - 1))
                        return mm

                    def keys_values(dst, x, s):
                        pe.wait_ge(stage_loaded[s], all_loaded(s))
                        if ATTN[s]["kv"] == "self":
                            pe.wait_ge(done["x_t"][x], nth("x_t", s))
                            kv_t = x_t[x]
                        else:
                            pe.wait_ge(first_ctx_loaded[x], 16)
                            kv_t = ctx_t[x]
                        product(dst[:, :], kv_t, w_kv[s], KC).then_inc(done["kv"][x], 1)

                    def stack(dst, parts):
                        flat = parts[:].rearrange("p h t d -> p (h t d)")
                        for pair in range(H // 2):
                            mm = nc.tensor.transpose(dst[:].bitcast(F16)[:, 128 * pair:128 * pair + 128],
                                                     flat[:, 128 * pair:128 * pair + 128], id16[:])
                        return mm

                    def scores(x, s, u):
                        c, r = u // 2, u % 2
                        if u == 0:
                            pe.wait_ge(done["k_stack"][x], nth("k_stack", s))
                            pe.wait_ge(done["q_stack"][x], nth("q_stack", s))
                            if ATTN[s]["mask"] in (0, 1, 2):
                                pe.wait_ge(done["bias"][x], 1)
                            elif ATTN[s]["mask"] == 3:
                                pe.wait_ge(sxs_made, 1)
                        if s == "A3" and u >= 2:
                            pe.wait_ge(done["times"][x], nth("times", s, u - 2))
                        elif quads_before(s, u, 2) > 0:
                            pe.wait_ge(done["exp"][x], quads_before(s, u, 2))
                        masked = ATTN[s]["mask"] is not None
                        dst = s_bank[x][r]
                        if masked:
                            nc.tensor.matmul(dst[:], idb[:], four(mask_bias(x, s)), start=True, stop=True)
                        rows = slice(64 * r, 64 * r + 64)
                        for n in range(QH):
                            mm = nc.tensor.matmul(dst[:, 128 * n:128 * n + 128], q_stack[x][rows, QH * c + n, :],
                                                  k_stack[x][rows, QH * c + n, :], start=not masked,
                                                  stop=True, skip_group_check=masked)
                        mm.then_inc(done["S"][x], 1)

                    def outputs(x, s, u):
                        pe.wait_ge(p_t_done[u % 2][x], nth("p_t", s, u))
                        if u == 0:
                            pe.wait_ge(done["v"][x], nth("v", s))
                            turn = OUTPUT_TURNS.index((x, s))
                            if turn:
                                last_x, last_s = OUTPUT_TURNS[turn - 1]
                                pe.wait_ge(done["o_raw"][last_x], nth("o_raw", last_s))
                        for n in range(QH):
                            h = 8 * (u // 2) + 2 * n + u % 2
                            mm = nc.tensor.matmul(o_bank[32 * n:32 * n + 32, 128 * u:128 * u + 128], v_one[x][:, h, :],
                                                  exps_t[x][:, u % 2, 128 * n:128 * n + 128], start=True, stop=True)
                        mm.then_inc(done["PV"][x], 1)

                    def hidden(dst, x, s, half):
                        pe.wait_ge(stage_loaded[s], all_loaded(s))
                        pe.wait_ge(done["x_t"][x], nth("x_t", s))
                        for n in range(QH):
                            f = QH * half + n
                            for c in range(KC):
                                mm = nc.tensor.matmul(dst[:, 128 * n:128 * n + 128], w_1[s][:, c, 128 * f:128 * f + 128],
                                                      x_t[x][:, c, :], start=(c == 0), stop=(c == KC - 1))
                        return mm

                    for beat in TENSOR_ORDER:
                        kind, x, s = beat[:3]
                        dst = free_bank(beat) if kind in READERS else None
                        if kind == "xT":
                            if s == "A0":
                                pe.wait_ge(first_x_loaded[x], 16)
                            else:
                                pe.wait_ge(done["norm"][x], nth("norm", source(s)))
                            transposes32(dst, stage_input(x, s), KC).then_inc(done["xT"][x], 1)
                        elif kind == "kv":
                            keys_values(dst, x, s)
                        elif kind == "q":
                            pe.wait_ge(stage_loaded[s], all_loaded(s))
                            pe.wait_ge(done["x_t"][x], nth("x_t", s))
                            product(dst[:, 0:D], x_t[x], w_q[s], KC).then_inc(done["q"][x], 1)
                        elif kind == "kT":
                            pe.wait_ge(done["k_low"][x], nth("k_low", s))
                            stack(dst, k_parts[x]).then_inc(done["kT"][x], 1)
                        elif kind == "qT":
                            pe.wait_ge(done["q_low"][x], nth("q_low", s))
                            stack(dst, q_parts[x]).then_inc(done["qT"][x], 1)
                        elif kind == "S":
                            scores(x, s, beat[3])
                        elif kind == "pT":
                            pe.wait_ge(done["exp"][x], nth("exp", s, beat[3]))
                            transposes32(dst, exps[x][:, beat[3] % 2, :], QH).then_inc(done["pT"][x], 1)
                        elif kind == "PV":
                            outputs(x, s, beat[3])
                        elif kind == "oT":
                            pe.wait_ge(done["o_raw"][x], nth("o_raw", s))
                            transposes32(dst, o_raw[x][:].rearrange("p u q -> p (u q)"), QUADS).then_inc(done["oT"][x], 1)
                        elif kind == "nT":
                            pe.wait_ge(done["o_norm"][x], nth("o_norm", s))
                            transposes32(dst, o_norm[x], KC).then_inc(done["nT"][x], 1)
                        elif kind == "O":
                            pe.wait_ge(done["o_t"][x], nth("o_t", s))
                            product(dst[:, 0:D], o_t[x], w_o[s], KC).then_inc(done["O"][x], 1)
                        elif kind in ("H0", "H1"):
                            hidden(dst, x, s, int(kind[1])).then_inc(done[kind][x], 1)
                        elif kind == "Y":
                            pe.wait_ge(done["h_t0"][x], nth("h_t0", s))
                            pe.wait_ge(done["h_t1"][x], nth("h_t1", s))
                            product(dst[:, 0:D], h_t[x], w_2[s], FC).then_inc(done["Y"][x], 1)

                def copy_beat(engine, copy, kind, x, s, u=None):
                    if kind == "x_t":
                        engine.wait_ge(done["xT"][x], nth("xT", s))
                        copy(x_t[x][:], bank(("xT", x, s))[:, 0:D].rearrange("p (c q) -> p c q", c=KC)
                             ).then_inc(done["x_t"][x], 1)
                    elif kind == "v":
                        engine.wait_ge(done["k32"][x], nth("k32", s))
                        if s != "A0":
                            engine.wait_ge(done["PV"][x], quads_before(s, 0, 1))
                        copy(v_one[x][:, :, 0:DH], bank(("kv", x, s))[:, D:2 * D].rearrange("p (h d) -> p h d", h=H)
                             ).then_inc(done["v"][x], 1)
                    elif kind == "k_stack":
                        engine.wait_ge(done["kT"][x], nth("kT", s))
                        copy(k_stack[x][:], bank(("kT", x, s))[:].bitcast(F16).rearrange("p (h k) -> p h k", h=H // 2)
                             ).then_inc(done["k_stack"][x], 1)
                    elif kind == "q_stack":
                        engine.wait_ge(done["qT"][x], nth("qT", s))
                        copy(q_stack[x][:], bank(("qT", x, s))[:].bitcast(F16).rearrange("p (h q) -> p h q", h=H // 2)
                             ).then_inc(done["q_stack"][x], 1)
                    elif kind == "p_t":
                        engine.wait_ge(done["pT"][x], nth("pT", s, u))
                        if quads_before(s, u, 2) > 0:
                            engine.wait_ge(done["PV"][x], quads_before(s, u, 2))
                        copy(exps_t[x][:, u % 2, :], bank(("pT", x, s, u))[:]).then_inc(p_t_done[u % 2][x], 1)
                    elif kind == "o_t":
                        engine.wait_ge(done["nT"][x], nth("nT", s))
                        copy(o_t[x][:], bank(("nT", x, s))[:, 0:D].rearrange("p (c q) -> p c q", c=KC)
                             ).then_inc(done["o_t"][x], 1)

                @block.scalar
                def _(act):
                    def split_high(dst, src, scale):
                        return nc.scalar.activation(dst, src[:].rearrange("p (h t d) -> p h t d", h=H, t=1)
                                                    .broadcast_to([128, H, 2, DH]), ACT.Copy, scale=scale)

                    def exponentials(x, s, u):
                        act.wait_ge(done["max"][x], nth("max", s, u))
                        if quads_before(s, u, 2) > 0:
                            act.wait_ge(done["pT"][x], quads_before(s, u, 2))
                        for n in range(QH):
                            cols = slice(128 * n, 128 * n + 128)
                            slot = QH * u + n
                            src = weight[x][:, slot, :] if s == "A3" else s_bank[x][u % 2][:, cols]
                            ins = nc.scalar.activation(exps[x][:, u % 2, cols], src, ACT.Exp,
                                                       bias=neg_max[x][:, slot:slot + 1])
                        ins.then_inc(done["exp"][x], 1)

                    for beat in SCALAR_ORDER:
                        kind, x, s = beat[:3]
                        if kind in COPIES:
                            copy_beat(act, nc.scalar.copy, *beat)
                        elif kind == "k_high":
                            act.wait_ge(done["k32"][x], nth("k32", s))
                            split_high(k_parts[x][:, :, 0:3:2, :], k32[x], 1.0).then_inc(done["k_high"][x], 1)
                        elif kind == "q_high":
                            act.wait_ge(done["q32"][x], nth("q32", s))
                            split_high(q_parts[x][:, :, 0:2, :], q32[x], DH ** -0.5).then_inc(done["q_high"][x], 1)
                        elif kind == "exp":
                            exponentials(x, s, beat[3])
                        elif kind == "o_raw":
                            act.wait_ge(done["PV"][x], nth("PV", s, QUADS - 1))
                            nc.scalar.copy(o_raw[x][:], o_bank[:].rearrange("p (u q) -> p u q", u=QUADS)
                                           ).then_inc(done["o_raw"][x], 1)
                        elif kind in ("h_t0", "h_t1"):
                            half = int(kind[3])
                            act.wait_ge(done[f"H{half}"][x], nth(f"H{half}", s))
                            for n in range(QH):
                                f = QH * half + n
                                ins = nc.scalar.activation(h_t[x][:, f, :], bank((f"H{half}", x, s))[:, 128 * n:128 * n + 128],
                                                           ACT.Gelu, bias=b_1[s][:, f:f + 1])
                            ins.then_inc(done[kind][x], 1)

                @block.vector
                def _(dve):
                    def mask_biases(x):
                        dve.wait_ge(first_masks_loaded[x], 32)
                        nc.vector.tensor_scalar(bias[x][:, 1, :], key_raw[x][:], 0.0, MASKED, ALU.is_equal, ALU.mult
                                                ).then_inc(key_bias_made[x], 1)
                        nc.vector.tensor_scalar(bias[x][:, 2, :], ik_raw[x][:], 0.0, MASKED, ALU.is_equal, ALU.mult
                                                ).then_inc(key_bias_made[x], 1)
                        dve.wait_ge(key_bias_made[x], 2)
                        nc.vector.tensor_tensor(bias[x][:, 0, :], bias[x][:, 1, :], causal[:], ALU.add
                                                ).then_inc(done["bias"][x], 1)

                    def values(x, s):
                        dve.wait_ge(done["kv"][x], nth("kv", s))
                        dve.wait_ge(done["PV"][x], quads_before(s, 0, 1))
                        nc.vector.tensor_tensor(v_one[x][:, :, 0:DH], bank(("kv", x, s))[:, D:2 * D].rearrange(
                            "p (h d) -> p h d", h=H), b_kv[s][:, D:2 * D].rearrange("p (h d) -> p h d", h=H), ALU.add
                                                ).then_inc(done["v"][x], 1)

                    def quad_max(x, s, u):
                        if s == "A3":
                            dve.wait_ge(done["lower"][x], nth("lower", s, u))
                            heads = weight[x][:, slots(u), :]
                        else:
                            dve.wait_ge(done["S"][x], nth("S", s, u))
                            heads = s_bank[x][u % 2][:].rearrange("p (n k) -> p n k", n=QH)
                        nc.vector.tensor_reduce(neg_max[x][:, slots(u)], heads, AX_X, ALU.max, negate=True
                                                ).then_inc(done["max"][x], 1)

                    def normalise(x, s):
                        heads = bank(("oT", x, s))[:].rearrange("p (h e) -> p h e", h=H)
                        dve.wait_ge(done["oT"][x], nth("oT", s))
                        nc.vector.reciprocal(recip[x][:, 0, :].unsqueeze(2), heads[:, :, DH:DH + 1]
                                             ).then_inc(recip_made[x], 1)
                        dve.wait_ge(recip_made[x], nth("oT", s))
                        which = 0
                        if ATTN[s]["nan"]:
                            dve.wait_ge(done["flag"][x], nth("flag", s))
                            nc.vector.tensor_tensor(recip[x][:, 1, :], recip[x][:, 0, :], nan_flag[x][:], ALU.add
                                                    ).then_inc(recip_flagged[x], 1)
                            dve.wait_ge(recip_flagged[x], nth("flag", s))
                            which = 1
                        nc.vector.tensor_tensor(o_norm[x][:].rearrange("p (h d) -> p h d", h=H), heads[:, :, 0:DH],
                                                recip[x][:, which, :].unsqueeze(2).broadcast_to([128, H, DH]), ALU.mult
                                                ).then_inc(done["o_norm"][x], 1)

                    def add_residual(x, s):
                        product = ("O" if s in ATTN else "Y", x, s)
                        dst = x_run[x] if s in ("A4", "A5") else x_sum[x]
                        dve.wait_ge(done[product[0]][x], nth(product[0], s))
                        if feeds_res(s):
                            dve.wait_ge(done["res"][x], nth("res", feeds_res(s)))
                        nc.vector.tensor_tensor(dst[:], bank(product)[:, 0:D], residual(x, s)[:], ALU.add
                                                ).then_inc(done["sum"][x], 1)

                    def norm_stats(x, n):
                        d = LN[n]
                        src = x_sum[x] if d["of"] == "sum" else x_run[x]
                        kind, before = d["after"]
                        dve.wait_ge(done[kind][x], nth(kind, before))
                        nc.vector.bn_stats(bn[x][:], src[:]).then_inc(bn_made[x], 1)
                        dve.wait_ge(bn_made[x], nth("stats", n))
                        nc.vector.bn_aggr(mean_var[x][:], bn[x][:]).then_inc(aggr_made[x], 1)
                        dve.wait_ge(aggr_made[x], nth("stats", n))
                        scale = D / (D - d["ddof"])
                        nc.vector.tensor_scalar(var_eps[x][:], mean_var[x][:, 1:2], scale, 0.0 if d["on_root"] else d["eps"],
                                                ALU.mult, ALU.add).then_inc(done["stats"][x], 1)

                    def norm_apply(x, n):
                        d = LN[n]
                        dst = x_run[x] if d["to"] == "x" else x_norm[x]
                        dve.wait_ge(done["root"][x], nth("root", n))
                        by = root[x]
                        if d["on_root"]:
                            nc.vector.tensor_scalar(root_eps[x][:], root[x][:], d["eps"], None, ALU.add
                                                    ).then_inc(root_shifted[x], 1)
                            dve.wait_ge(root_shifted[x], nth("norm", n))
                            nc.vector.reciprocal(inv_root[x][:], root_eps[x][:]).then_inc(root_inverted[x], 1)
                            dve.wait_ge(root_inverted[x], nth("norm", n))
                            by = inv_root[x]
                        dve.wait_ge(done["centre"][x], nth("centre", n))
                        nc.vector.scalar_tensor_tensor(out=dst[:], in0=x_sum[x][:], scalar=by[:, 0:1], in1=shift[n],
                                                       op0=ALU.mult, op1=ALU.add).then_inc(done["norm"][x], 1)

                    for kind, x, s, *u in VECTOR_ORDER:
                        if kind in COPIES and not (kind == "v" and ATTN[s]["b"]):
                            copy_beat(dve, nc.vector.tensor_copy, kind, x, s, *u)
                        elif kind == "bias":
                            mask_biases(x)
                        elif kind == "k32":
                            dve.wait_ge(done["kv"][x], nth("kv", s))
                            src = bank(("kv", x, s))[:, 0:D]
                            if ATTN[s]["b"]:
                                nc.vector.tensor_tensor(k32[x][:], src, b_kv[s][:, 0:D], ALU.add).then_inc(done["k32"][x], 1)
                            else:
                                nc.vector.tensor_copy(k32[x][:], src).then_inc(done["k32"][x], 1)
                        elif kind == "v":
                            values(x, s)
                        elif kind == "k_low":
                            dve.wait_ge(done["k_high"][x], nth("k_high", s))
                            nc.vector.tensor_tensor(k_parts[x][:, :, 1, :], k32[x][:].rearrange("p (h d) -> p h d", h=H),
                                                    k_parts[x][:, :, 0, :], ALU.subtract).then_inc(done["k_low"][x], 1)
                        elif kind == "q32":
                            dve.wait_ge(done["q"][x], nth("q", s))
                            src = bank(("q", x, s))[:, 0:D]
                            if ATTN[s]["b"]:
                                nc.vector.tensor_tensor(q32[x][:], src, b_q[s], ALU.add).then_inc(done["q32"][x], 1)
                            else:
                                nc.vector.tensor_copy(q32[x][:], src).then_inc(done["q32"][x], 1)
                        elif kind == "q_low":
                            dve.wait_ge(done["q_high"][x], nth("q_high", s))
                            nc.vector.scalar_tensor_tensor(
                                out=q_parts[x][:, :, 2, :], in0=q32[x][:].rearrange("p (h d) -> p h d", h=H),
                                scalar=DH ** -0.5, in1=q_parts[x][:, :, 0, :], op0=ALU.mult, op1=ALU.subtract
                            ).then_inc(done["q_low"][x], 1)
                        elif kind == "times":
                            if u[0] == 0:
                                dve.wait_ge(first_weight_loaded[x], 32)
                            dve.wait_ge(done["S"][x], nth("S", s, *u))
                            part = weight[x][:, slots(*u), :]
                            nc.vector.tensor_tensor(part, s_bank[x][u[0] % 2][:].rearrange("p (n k) -> p n k", n=QH), part,
                                                    ALU.mult).then_inc(done["times"][x], 1)
                        elif kind == "lower":
                            dve.wait_ge(done["times"][x], nth("times", s, *u))
                            part = weight[x][:, slots(*u), :]
                            nc.vector.scalar_tensor_tensor(out=part, in0=drop_raw[x][:, slots(*u), :], scalar=MASKED, in1=part,
                                                           op0=ALU.mult, op1=ALU.add).then_inc(done["lower"][x], 1)
                        elif kind == "max":
                            quad_max(x, s, *u)
                        elif kind == "o_norm":
                            normalise(x, s)
                        elif kind == "sum":
                            add_residual(x, s)
                        elif kind == "stats":
                            norm_stats(x, s)
                        elif kind == "centre":
                            dve.wait_ge(done["stats"][x], nth("stats", s))
                            src = x_sum[x] if LN[s]["of"] == "sum" else x_run[x]
                            nc.vector.scalar_tensor_tensor(out=x_sum[x][:], in0=src[:], scalar=mean_var[x][:, 0:1],
                                                           in1=gain[s], op0=ALU.subtract, op1=ALU.mult
                                                           ).then_inc(done["centre"][x], 1)
                        elif kind == "norm":
                            norm_apply(x, s)
                        elif kind in ("h_t0", "h_t1"):
                            half = int(kind[3])
                            dve.wait_ge(done[f"H{half}"][x], nth(f"H{half}", s))
                            for n in range(QH):
                                f = QH * half + n
                                ins = nc.vector.tensor_scalar(h_t[x][:, f, :], bank((f"H{half}", x, s))[:, 128 * n:128 * n + 128],
                                                              b_1[s][:, f:f + 1], 0.0, ALU.add, ALU.max)
                            ins.then_inc(done[kind][x], 1)

            nc.all_engine_barrier(sems_to_clear=range(first_cleared, last_cleared + 1))


def kernel(**inputs):
    import numpy as np
    from concourse import bacc
    from concourse.bass_utils import run_bass_kernel_spmd

    slot_head = [8 * (u // 2) + 2 * n + u % 2 for u in range(QUADS) for n in range(QH)]
    slot_row = [DH * h + d for h in slot_head for d in range(DH)]

    def rows_on_partitions(w):
        return w.reshape(-1, 128, w.shape[1]).transpose(1, 0, 2).reshape(128, -1)

    arrays = {}
    for s in STAGES:
        if s in ATTN:
            q, k, v, o = (np.asarray(inputs[n]) for n in ATTN[s]["w"])
            if s in ("A2", "A3"):
                q, k, v, o = q.T, k.T, v.T, o.T
            parts = [rows_on_partitions(w) for w in (np.concatenate([k, v], axis=1), q, o[slot_row])]
        else:
            w1, w2, b1 = (np.asarray(inputs[FFN[s][k]]) for k in ("w1", "w2", "b1"))
            parts = [rows_on_partitions(w1), rows_on_partitions(w2), b1.reshape(FC, 128).T]
        arrays[f"weights_{s}"] = np.concatenate(parts, axis=1)
        if VECTORS[s]:
            arrays[f"vectors_{s}"] = np.concatenate([np.asarray(inputs[n]) for n in VECTORS[s]])
    arrays["x"] = np.asarray(inputs["x"])
    arrays["ctx_t"] = np.asarray(inputs["ctx_1024"]).transpose(0, 2, 1)
    arrays["fside"] = np.asarray(inputs["fside_Bx16xSxS2_0"])[:, slot_head].transpose(0, 2, 1, 3)
    arrays["ik"] = np.asarray(inputs["mask_BxSxS2_ik1"])
    arrays["kmask"] = np.asarray(inputs["mask_Bx1x1xS2_bf1"])
    arrays["drop"] = np.asarray(inputs["mask_Bx16xSxS2_bk0"])[:, slot_head].transpose(0, 2, 1, 3)
    arrays["sxs"] = np.asarray(inputs["mask_SxS_bk1"])
    arrays = {n: np.ascontiguousarray(a) for n, a in arrays.items()}

    nc = bacc.Bacc("TRN2", target_bir_lowering=False, num_devices=1)
    dram = {n: nc.dram_tensor(f"in_{n}", a.shape, mybir.dt.from_np(a.dtype), kind="ExternalInput").ap()
            for n, a in arrays.items()}
    out = nc.dram_tensor("out_0", (B, N, D), F32, kind="ExternalOutput").ap()
    program(nc, dram, out)
    r = run_bass_kernel_spmd(nc, [{f"in_{n}": a for n, a in arrays.items()}], core_ids=[0])
    return r.results[0]["out_0"]
```

```python
from contextlib import ExitStack

import concourse.bass as bass
from concourse import mybir

F32 = mybir.dt.float32
F16 = mybir.dt.float16
BF16 = mybir.dt.bfloat16
U8 = mybir.dt.uint8
I32 = mybir.dt.int32
ALU = mybir.AluOpType
ACT = mybir.ActivationFunctionType
AX_X = mybir.AxisListType.X

B, N, D, H = 16, 128, 256, 16
DH = D // H
FF = 1024
KC = D // 128
FC = FF // 128
QUADS, QH = 4, 4
STREAMS = 2
SEQS = 4
MASKED = -(2.0 ** 100)
OVERFLOW = 2.0 ** 60
CHAIN_BANKS = 3

ATTN = {
    "A0": dict(w=("L0_xattn_mha_wq", "L0_xattn_mha_wk", "L0_xattn_mha_wv", "L0_xattn_mha_wo"), b=None,
               kv="self", mask=0, nan=True, pre=False, next=["LN0"]),
    "A1": dict(w=("L0_xattn_cmha_wq", "L0_xattn_cmha_wk", "L0_xattn_cmha_wv", "L0_xattn_cmha_wo"), b=None,
               kv="ctx", mask=1, nan=True, pre=False, next=["LN1"]),
    "A2": dict(w=("L1_xattn_Wq", "L1_xattn_Wk", "L1_xattn_Wv", "L1_xattn_Wo"),
               b=("L1_xattn_bq", "L1_xattn_bk", "L1_xattn_bv", "L1_xattn_bo"),
               kv="ctx", mask=2, nan=False, pre=False, next=["LN3"]),
    "A3": dict(w=("L2_xattn_Wq", "L2_xattn_Wk", "L2_xattn_Wv", "L2_xattn_Wo"),
               b=("L2_xattn_bq", "L2_xattn_bk", "L2_xattn_bv", "L2_xattn_bo"),
               kv="ctx", mask=None, nan=True, pre=False, next=["LN4", "LN5"]),
    "A4": dict(w=("L3_xattn_ca_qw", "L3_xattn_ca_kw", "L3_xattn_ca_vw", "L3_xattn_ca_ow"),
               b=("L3_xattn_ca_qb", "L3_xattn_ca_kb", "L3_xattn_ca_vb", "L3_xattn_ca_ob"),
               kv="ctx", mask=None, nan=False, pre=True, next=["LN6"]),
    "A5": dict(w=("L3_xattn_sa_qw", "L3_xattn_sa_kw", "L3_xattn_sa_vw", "L3_xattn_sa_ow"),
               b=("L3_xattn_sa_qb", "L3_xattn_sa_kb", "L3_xattn_sa_vb", "L3_xattn_sa_ob"),
               kv="self", mask=3, nan=True, pre=True, next=["LN7"]),
}
FFN = {
    "F0": dict(w1="L0_xattn_ff_w1", b1="L0_xattn_ff_b1", w2="L0_xattn_ff_w2", b2="L0_xattn_ff_b2",
               gelu=False, pre=False, next=["LN2"]),
    "F1": dict(w1="L3_xattn_w1", b1="L3_xattn_b1", w2="L3_xattn_w2", b2="L3_xattn_b2",
               gelu=True, pre=True, next=[]),
}
STAGES = ["A0", "A1", "F0", "A2", "A3", "A4", "A5", "F1"]
LN = {
    "LN0": dict(g="L0_xattn_g1", b="L0_xattn_b1", ddof=1, eps=1e-6, on_root=True, to="x", of="sum", after=("sum", "A0")),
    "LN1": dict(g="L0_xattn_g2", b="L0_xattn_b2", ddof=1, eps=1e-6, on_root=True, to="x", of="sum", after=("sum", "A1")),
    "LN2": dict(g="L0_xattn_g3", b="L0_xattn_b3", ddof=1, eps=1e-6, on_root=True, to="x", of="sum", after=("sum", "F0")),
    "LN3": dict(g="L1_xattn_gamma", b="L1_xattn_beta", ddof=0, eps=1e-6, on_root=False, to="x", of="sum", after=("sum", "A2")),
    "LN4": dict(g="L2_xattn_gamma", b="L2_xattn_beta", ddof=0, eps=1e-5, on_root=False, to="x", of="sum", after=("sum", "A3")),
    "LN5": dict(g="L3_xattn_ln1_g", b="L3_xattn_ln1_b", ddof=0, eps=1e-5, on_root=False, to="x_norm", of="x", after=("norm", "LN4")),
    "LN6": dict(g="L3_xattn_ln2_g", b="L3_xattn_ln2_b", ddof=0, eps=1e-5, on_root=False, to="x_norm", of="x", after=("sum", "A4")),
    "LN7": dict(g="L3_xattn_ln3_g", b="L3_xattn_ln3_b", ddof=0, eps=1e-5, on_root=False, to="x_norm", of="x", after=("sum", "A5")),
}


ROOTS_SHIFTED = sum(d["on_root"] for d in LN.values())


def norms_after(s):
    return (ATTN.get(s) or FFN[s])["next"]


VECTORS = {s: list((ATTN[s]["b"] or ()) if s in ATTN else (FFN[s]["b2"],))
           + [LN[n][k] for n in norms_after(s) for k in ("g", "b")] for s in STAGES}
WEIGHT_COLS = {s: 4 * KC * D if s in ATTN else KC * FF + FC * D + FC for s in STAGES}


def stream_beats():
    beats = [("bias", "in")]
    for s in STAGES:
        beats += [("xT", s), ("x_t", s)]
        if s in ATTN:
            biased = bool(ATTN[s]["b"])
            for a, b in (("K", "k"), ("Q", "q")):
                beats += [(a, s)] + ([(b + "32", s)] if biased else []) + [(b + "_high", s), (b + "_low", s)]
                beats += [(b + "T", s), (b + "_stack", s)]
            beats += [("V", s), ("v", s)]
            for u in range(QUADS):
                beats += [("S", s, u)] + ([("times", s, u), ("lower", s, u)] if s == "A3" else [])
                beats += [("max", s, u), ("exp", s, u), ("pT", s, u), ("p_t", s, u), ("PV", s, u)]
            beats += [("flag", s)] if ATTN[s]["nan"] else []
            beats += [(k, s) for k in ("o_raw", "oT", "o_norm", "nT", "o_t", "O", "sum")]
        else:
            beats += [b for half in range(2) for b in (("H", s, 2 * half), ("H", s, 2 * half + 1), ("h_t", s, half))]
            beats += [("Y", s, part) for part in range(4)] + [("sum", s)]
        for n in norms_after(s):
            beats += [(k, n) for k in ("stats", "centre", "root", "norm")]
            beats += [("res", n)] if MAKES_RES[n] else []
    return beats


FED_BY = {"LN0": "A1", "LN1": "F0", "LN2": "A2", "LN3": "A3", "LN4": None, "LN5": "A4", "LN6": "A5", "LN7": "F1"}
MAKES_RES = {n: bool(s and (s in FFN or ATTN[s]["b"])) for n, s in FED_BY.items()}

EVEN_ODD = ("p_t", "h_t")

NTH, _seen = {}, {}
for _beat in stream_beats():
    _kind = (_beat[0], _beat[2] % 2) if _beat[0] in EVEN_ODD else _beat[0]
    NTH[_beat] = _seen[_kind] = _seen.get(_kind, 0) + 1
TOTAL = {_kind[0] if isinstance(_kind, tuple) else _kind: n for _kind, n in _seen.items()}

TENSOR = """
xT.0.A0 xT.1.A0 K.0.A0 Q.0.A0 Q.1.A0 K.1.A0 qT.0.A0 kT.0.A0 kT.1.A0 S.0.A0.0 qT.1.A0 S.0.A0.1 V.0.A0 S.1.A0.0
S.0.A0.2 S.1.A0.1 pT.0.A0.0 pT.0.A0.1 V.1.A0 S.0.A0.3 pT.1.A0.0 S.1.A0.2 PV.0.A0.0 pT.0.A0.2 S.1.A0.3 PV.0.A0.1
pT.0.A0.3 K.1.A1 PV.0.A0.2 PV.0.A0.3 pT.1.A0.1 pT.1.A0.2 oT.0.A0 PV.1.A0.0 PV.1.A0.1 pT.1.A0.3 PV.1.A0.2 nT.0.A0
kT.1.A1 PV.1.A0.3 O.0.A0 oT.1.A0 V.1.A1 nT.1.A0 K.0.A1 O.1.A0 xT.0.A1 kT.0.A1 Q.0.A1 xT.1.A1 qT.0.A1 Q.1.A1
S.0.A1.0 S.0.A1.1 V.0.A1 qT.1.A1 S.0.A1.2 pT.0.A1.0 S.1.A1.0 S.0.A1.3 pT.0.A1.1 PV.0.A1.0 S.1.A1.1 pT.0.A1.2
K.0.A2 PV.0.A1.1 pT.0.A1.3 S.1.A1.2 pT.1.A1.0 PV.0.A1.2 PV.0.A1.3 S.1.A1.3 pT.1.A1.1 oT.0.A1 K.1.A2 PV.1.A1.0
nT.0.A1 pT.1.A1.2 PV.1.A1.1 O.0.A1 PV.1.A1.2 pT.1.A1.3 V.0.A2 PV.1.A1.3 V.1.A2 xT.0.F0 oT.1.A1 H.0.F0.0 H.0.F0.1
nT.1.A1 H.0.F0.2 H.0.F0.3 O.1.A1 Y.0.F0.0 Y.0.F0.1 Y.0.F0.2 Y.0.F0.3 xT.1.F0 kT.0.A2 H.1.F0.0 H.1.F0.1 xT.0.A2
H.1.F0.2 Q.0.A2 H.1.F0.3 Y.1.F0.0 Y.1.F0.1 qT.0.A2 Y.1.F0.2 S.0.A2.0 S.0.A2.1 Y.1.F0.3 pT.0.A2.0 kT.1.A2 S.0.A2.2
pT.0.A2.1 xT.1.A2 S.0.A2.3 Q.1.A2 PV.0.A2.0 PV.0.A2.1 K.0.A3 pT.0.A2.2 qT.1.A2 pT.0.A2.3 PV.0.A2.2 S.1.A2.0
PV.0.A2.3 S.1.A2.1 oT.0.A2 S.1.A2.2 nT.0.A2 pT.1.A2.0 S.1.A2.3 pT.1.A2.1 O.0.A2 pT.1.A2.2 PV.1.A2.0 PV.1.A2.1
pT.1.A2.3 K.1.A3 PV.1.A2.2 PV.1.A2.3 xT.0.A3 V.0.A3 oT.1.A2 Q.0.A3 nT.1.A2 kT.0.A3 O.1.A2 qT.0.A3 S.0.A3.0
S.0.A3.1 xT.1.A3 Q.1.A3 kT.1.A3 S.0.A3.2 S.0.A3.3 qT.1.A3 pT.0.A3.0 S.1.A3.0 pT.0.A3.1 K.0.A4 S.1.A3.1 S.1.A3.2
pT.0.A3.2 PV.0.A3.0 PV.0.A3.1 pT.0.A3.3 S.1.A3.3 PV.0.A3.2 PV.0.A3.3 V.1.A3 pT.1.A3.0 oT.0.A3 nT.0.A3 pT.1.A3.1
PV.1.A3.0 O.0.A3 K.1.A4 pT.1.A3.2 PV.1.A3.1 pT.1.A3.3 PV.1.A3.2 PV.1.A3.3 kT.0.A4 oT.1.A3 xT.0.A4 nT.1.A3 Q.0.A4
O.1.A3 kT.1.A4 V.0.A4 qT.0.A4 V.1.A4 S.0.A4.0 S.0.A4.1 xT.1.A4 Q.1.A4 S.0.A4.2 pT.0.A4.0 S.0.A4.3 pT.0.A4.1
PV.0.A4.0 qT.1.A4 pT.0.A4.2 PV.0.A4.1 S.1.A4.0 pT.0.A4.3 PV.0.A4.2 S.1.A4.1 PV.0.A4.3 pT.1.A4.0 oT.0.A4 S.1.A4.2
nT.0.A4 pT.1.A4.1 S.1.A4.3 O.0.A4 PV.1.A4.0 pT.1.A4.2 PV.1.A4.1 pT.1.A4.3 PV.1.A4.2 xT.0.A5 PV.1.A4.3 K.0.A5
oT.1.A4 Q.0.A5 nT.1.A4 kT.0.A5 O.1.A4 qT.0.A5 V.0.A5 S.0.A5.0 xT.1.A5 S.0.A5.1 K.1.A5 Q.1.A5 S.0.A5.2 pT.0.A5.0
S.0.A5.3 kT.1.A5 PV.0.A5.0 pT.0.A5.1 qT.1.A5 pT.0.A5.2 PV.0.A5.1 pT.0.A5.3 PV.0.A5.2 S.1.A5.0 PV.0.A5.3 S.1.A5.1
V.1.A5 oT.0.A5 pT.1.A5.0 S.1.A5.2 nT.0.A5 S.1.A5.3 pT.1.A5.1 O.0.A5 pT.1.A5.2 PV.1.A5.0 PV.1.A5.1 pT.1.A5.3
PV.1.A5.2 PV.1.A5.3 xT.0.F1 oT.1.A5 H.0.F1.0 H.0.F1.1 nT.1.A5 H.0.F1.2 H.0.F1.3 xT.2.A0 O.1.A5 K.2.A0 Q.2.A0
xT.1.F1 kT.2.A0 qT.2.A0 H.1.F1.0 H.1.F1.1 H.1.F1.2 xT.3.A0 H.1.F1.3 S.2.A0.0 S.2.A0.1 K.3.A0 Q.3.A0 S.2.A0.2
V.2.A0 kT.3.A0 qT.3.A0 S.2.A0.3 Y.0.F1.0 pT.2.A0.0 S.3.A0.0 S.3.A0.1 Y.0.F1.1 Y.0.F1.2 Y.0.F1.3 S.3.A0.2 pT.2.A0.1
PV.2.A0.0 pT.2.A0.2 pT.3.A0.0 S.3.A0.3 pT.3.A0.1 pT.2.A0.3 PV.2.A0.1 V.3.A0 Y.1.F1.0 Y.1.F1.1 Y.1.F1.2 PV.2.A0.2
PV.2.A0.3 Y.1.F1.3 pT.3.A0.2 oT.2.A0 PV.3.A0.0 pT.3.A0.3 PV.3.A0.1 nT.2.A0 PV.3.A0.2 PV.3.A0.3 O.2.A0 oT.3.A0
K.2.A1 nT.3.A0 O.3.A0 xT.2.A1 kT.2.A1 Q.2.A1 V.2.A1 xT.3.A1 qT.2.A1 Q.3.A1 S.2.A1.0 S.2.A1.1 K.3.A1 V.3.A1 qT.3.A1
S.2.A1.2 kT.3.A1 pT.2.A1.0 S.2.A1.3 pT.2.A1.1 PV.2.A1.0 S.3.A1.0 S.3.A1.1 PV.2.A1.1 pT.2.A1.2 pT.2.A1.3 K.2.A2
PV.2.A1.2 PV.2.A1.3 S.3.A1.2 pT.3.A1.0 oT.2.A1 V.2.A2 S.3.A1.3 nT.2.A1 pT.3.A1.1 PV.3.A1.0 O.2.A1 pT.3.A1.2
pT.3.A1.3 PV.3.A1.1 K.3.A2 PV.3.A1.2 PV.3.A1.3 xT.2.F0 kT.2.A2 oT.3.A1 H.2.F0.0 H.2.F0.1 nT.3.A1 H.2.F0.2 H.2.F0.3
O.3.A1 Y.2.F0.0 Y.2.F0.1 Y.2.F0.2 Y.2.F0.3 xT.3.F0 V.3.A2 H.3.F0.0 H.3.F0.1 H.3.F0.2 H.3.F0.3 xT.2.A2 Y.3.F0.0
Y.3.F0.1 Q.2.A2 Y.3.F0.2 Y.3.F0.3 qT.2.A2 kT.3.A2 S.2.A2.0 S.2.A2.1 xT.3.A2 Q.3.A2 S.2.A2.2 pT.2.A2.0 S.2.A2.3
K.2.A3 qT.3.A2 pT.2.A2.1 pT.2.A2.2 PV.2.A2.0 S.3.A2.0 PV.2.A2.1 pT.2.A2.3 S.3.A2.1 PV.2.A2.2 PV.2.A2.3 S.3.A2.2
oT.2.A2 pT.3.A2.0 S.3.A2.3 nT.2.A2 pT.3.A2.1 PV.3.A2.0 pT.3.A2.2 O.2.A2 PV.3.A2.1 pT.3.A2.3 PV.3.A2.2 kT.2.A3
PV.3.A2.3 K.3.A3 xT.2.A3 oT.3.A2 Q.2.A3 nT.3.A2 kT.3.A3 O.3.A2 qT.2.A3 V.2.A3 S.2.A3.0 S.2.A3.1 xT.3.A3 S.2.A3.2
Q.3.A3 S.2.A3.3 V.3.A3 qT.3.A3 pT.2.A3.0 S.3.A3.0 S.3.A3.1 pT.2.A3.1 pT.2.A3.2 K.2.A4 PV.2.A3.0 pT.2.A3.3
PV.2.A3.1 S.3.A3.2 PV.2.A3.2 PV.2.A3.3 S.3.A3.3 oT.2.A3 pT.3.A3.0 nT.2.A3 pT.3.A3.1 O.2.A3 pT.3.A3.2 PV.3.A3.0
PV.3.A3.1 pT.3.A3.3 PV.3.A3.2 PV.3.A3.3 K.3.A4 xT.2.A4 oT.3.A3 Q.2.A4 nT.3.A3 kT.2.A4 O.3.A3 qT.2.A4 S.2.A4.0
kT.3.A4 S.2.A4.1 V.2.A4 xT.3.A4 S.2.A4.2 pT.2.A4.0 Q.3.A4 S.2.A4.3 pT.2.A4.1 PV.2.A4.0 pT.2.A4.2 PV.2.A4.1 qT.3.A4
pT.2.A4.3 PV.2.A4.2 S.3.A4.0 PV.2.A4.3 S.3.A4.1 V.3.A4 oT.2.A4 S.3.A4.2 pT.3.A4.0 nT.2.A4 S.3.A4.3 pT.3.A4.1
O.2.A4 PV.3.A4.0 pT.3.A4.2 PV.3.A4.1 pT.3.A4.3 PV.3.A4.2 xT.2.A5 PV.3.A4.3 K.2.A5 oT.3.A4 Q.2.A5 nT.3.A4 kT.2.A5
O.3.A4 qT.2.A5 V.2.A5 S.2.A5.0 xT.3.A5 S.2.A5.1 K.3.A5 Q.3.A5 S.2.A5.2 pT.2.A5.0 pT.2.A5.1 S.2.A5.3 kT.3.A5
qT.3.A5 PV.2.A5.0 PV.2.A5.1 pT.2.A5.2 S.3.A5.0 S.3.A5.1 pT.2.A5.3 V.3.A5 PV.2.A5.2 S.3.A5.2 PV.2.A5.3 pT.3.A5.0
S.3.A5.3 pT.3.A5.1 oT.2.A5 PV.3.A5.0 pT.3.A5.2 PV.3.A5.1 nT.2.A5 pT.3.A5.3 PV.3.A5.2 O.2.A5 PV.3.A5.3 oT.3.A5
nT.3.A5 xT.2.F1 O.3.A5 H.2.F1.0 H.2.F1.1 H.2.F1.2 xT.3.F1 H.2.F1.3 H.3.F1.0 H.3.F1.1 H.3.F1.2 Y.2.F1.0 Y.3.F1.0
H.3.F1.3 Y.2.F1.1 Y.3.F1.1 Y.3.F1.2 Y.2.F1.2 Y.3.F1.3 Y.2.F1.3
"""
VECTOR = """
bias.0.in x_t.1.A0 k_low.0.A0 bias.1.in q_low.0.A0 q_low.1.A0 k_low.1.A0 k_stack.0.A0 k_stack.1.A0 max.0.A0.0
q_stack.1.A0 max.0.A0.1 v.0.A0 max.1.A0.0 max.0.A0.2 p_t.0.A0.0 max.1.A0.1 p_t.0.A0.1 max.0.A0.3 v.1.A0 max.1.A0.2
p_t.1.A0.0 max.1.A0.3 p_t.0.A0.3 k_low.1.A1 p_t.1.A0.1 o_norm.0.A0 o_t.0.A0 k_stack.1.A1 sum.0.A0 o_norm.1.A0
stats.0.LN0 o_t.1.A0 centre.0.LN0 norm.0.LN0 k_low.0.A1 sum.1.A0 stats.1.LN0 centre.1.LN0 norm.1.LN0 q_low.0.A1
q_stack.0.A1 max.0.A1.0 q_low.1.A1 max.0.A1.1 q_stack.1.A1 max.0.A1.2 max.0.A1.3 max.1.A1.0 p_t.0.A1.1 p_t.0.A1.2
max.1.A1.1 p_t.0.A1.3 k32.0.A2 p_t.1.A1.0 max.1.A1.2 max.1.A1.3 o_norm.0.A1 k32.1.A2 p_t.1.A1.2 sum.0.A1
stats.0.LN1 centre.0.LN1 norm.0.LN1 v.0.A2 v.1.A2 o_norm.1.A1 h_t.0.F0.0 o_t.1.A1 sum.1.A1 stats.1.LN1
centre.1.LN1 norm.1.LN1 k_low.0.A2 sum.0.F0 stats.0.LN2 centre.0.LN2 norm.0.LN2 h_t.1.F0.0 q32.0.A2 k_low.1.A2
q_low.0.A2 q_stack.0.A2 max.0.A2.0 max.0.A2.1 sum.1.F0 stats.1.LN2 centre.1.LN2 norm.1.LN2 max.0.A2.2 max.0.A2.3
q32.1.A2 q_low.1.A2 k32.0.A3 q_stack.1.A2 max.1.A2.0 max.1.A2.1 o_norm.0.A2 max.1.A2.2 p_t.1.A2.0 max.1.A2.3
p_t.1.A2.1 sum.0.A2 stats.0.LN3 centre.0.LN3 norm.0.LN3 k32.1.A3 k_low.0.A3 x_t.0.A3 v.0.A3 o_norm.1.A2 k_low.1.A3
q32.0.A3 q_low.0.A3 sum.1.A2 stats.1.LN3 centre.1.LN3 norm.1.LN3 times.0.A3.0 lower.0.A3.0 max.0.A3.0 times.0.A3.1
q32.1.A3 lower.0.A3.1 max.0.A3.1 times.0.A3.2 q_low.1.A3 times.0.A3.3 lower.0.A3.2 max.0.A3.2 lower.0.A3.3
times.1.A3.0 max.0.A3.3 lower.1.A3.0 times.1.A3.1 k32.0.A4 max.1.A3.0 times.1.A3.2 lower.1.A3.1 lower.1.A3.2
max.1.A3.1 v.1.A3 o_norm.0.A3 max.1.A3.2 times.1.A3.3 lower.1.A3.3 max.1.A3.3 k_low.0.A4 sum.0.A3 stats.0.LN4
k32.1.A4 centre.0.LN4 norm.0.LN4 stats.0.LN5 centre.0.LN5 norm.0.LN5 o_norm.1.A3 o_t.1.A3 k_low.1.A4 q32.0.A4
sum.1.A3 stats.1.LN4 q_low.0.A4 centre.1.LN4 norm.1.LN4 stats.1.LN5 centre.1.LN5 v.0.A4 norm.1.LN5 max.0.A4.0
bias.2.in max.0.A4.1 v.1.A4 q32.1.A4 max.0.A4.2 p_t.0.A4.0 q_low.1.A4 max.0.A4.3 q_stack.1.A4 p_t.0.A4.2
max.1.A4.0 p_t.0.A4.3 max.1.A4.1 o_norm.0.A4 max.1.A4.2 max.1.A4.3 sum.0.A4 stats.0.LN6 centre.0.LN6 norm.0.LN6
k32.0.A5 o_norm.1.A4 k_low.0.A5 q32.0.A5 bias.3.in q_low.0.A5 sum.1.A4 stats.1.LN6 centre.1.LN6 norm.1.LN6
max.0.A5.0 v.0.A5 max.0.A5.1 k32.1.A5 q32.1.A5 k_low.1.A5 max.0.A5.2 q_low.1.A5 max.0.A5.3 k_stack.1.A5 p_t.0.A5.1
p_t.0.A5.2 max.1.A5.0 max.1.A5.1 v.1.A5 o_norm.0.A5 max.1.A5.2 max.1.A5.3 p_t.1.A5.1 sum.0.A5 stats.0.LN7
centre.0.LN7 norm.0.LN7 x_t.0.F1 o_norm.1.A5 o_t.1.A5 x_t.2.A0 sum.1.A5 stats.1.LN7 centre.1.LN7 norm.1.LN7
k_low.2.A0 q_low.2.A0 k_stack.2.A0 x_t.3.A0 max.2.A0.0 max.2.A0.1 k_low.3.A0 q_low.3.A0 v.2.A0 k_stack.3.A0
max.2.A0.2 q_stack.3.A0 max.3.A0.0 p_t.2.A0.0 max.2.A0.3 max.3.A0.1 sum.0.F1 p_t.2.A0.2 max.3.A0.2 p_t.3.A0.1
max.3.A0.3 sum.1.F1 o_norm.2.A0 sum.2.A0 o_norm.3.A0 stats.2.LN0 centre.2.LN0 k_low.2.A1 norm.2.LN0 sum.3.A0
stats.3.LN0 centre.3.LN0 norm.3.LN0 q_low.2.A1 x_t.3.A1 q_stack.2.A1 max.2.A1.0 max.2.A1.1 q_low.3.A1 k_low.3.A1
q_stack.3.A1 max.2.A1.2 p_t.2.A1.0 max.2.A1.3 p_t.2.A1.1 max.3.A1.0 max.3.A1.1 p_t.2.A1.2 p_t.2.A1.3 k32.2.A2
max.3.A1.2 o_norm.2.A1 v.2.A2 max.3.A1.3 p_t.3.A1.1 k_low.2.A2 sum.2.A1 stats.2.LN1 centre.2.LN1 norm.2.LN1
k32.3.A2 x_t.2.F0 o_norm.3.A1 sum.3.A1 stats.3.LN1 centre.3.LN1 norm.3.LN1 sum.2.F0 x_t.3.F0 v.3.A2 stats.2.LN2
centre.2.LN2 norm.2.LN2 q32.2.A2 k_low.3.A2 q_low.2.A2 sum.3.F0 stats.3.LN2 centre.3.LN2 norm.3.LN2 max.2.A2.0
x_t.3.A2 max.2.A2.1 q32.3.A2 max.2.A2.2 q_low.3.A2 max.2.A2.3 k32.2.A3 q_stack.3.A2 p_t.2.A2.1 max.3.A2.0
p_t.2.A2.3 max.3.A2.1 k_low.2.A3 max.3.A2.2 o_norm.2.A2 p_t.3.A2.0 max.3.A2.3 p_t.3.A2.1 sum.2.A2 stats.2.LN3
centre.2.LN3 norm.2.LN3 k_stack.2.A3 k32.3.A3 o_norm.3.A2 k_low.3.A3 q32.2.A3 q_low.2.A3 sum.3.A2 stats.3.LN3
centre.3.LN3 v.2.A3 norm.3.LN3 times.2.A3.0 lower.2.A3.0 times.2.A3.1 max.2.A3.0 q32.3.A3 lower.2.A3.1 max.2.A3.1
q_low.3.A3 times.2.A3.2 v.3.A3 lower.2.A3.2 max.2.A3.2 times.2.A3.3 lower.2.A3.3 max.2.A3.3 times.3.A3.0
lower.3.A3.0 max.3.A3.0 times.3.A3.1 lower.3.A3.1 max.3.A3.1 times.3.A3.2 lower.3.A3.2 k32.2.A4 o_norm.2.A3
max.3.A3.2 times.3.A3.3 lower.3.A3.3 max.3.A3.3 sum.2.A3 stats.2.LN4 centre.2.LN4 norm.2.LN4 stats.2.LN5
centre.2.LN5 norm.2.LN5 k32.3.A4 k_low.2.A4 o_norm.3.A3 q32.2.A4 k_low.3.A4 q_low.2.A4 sum.3.A3 stats.3.LN4
centre.3.LN4 norm.3.LN4 stats.3.LN5 max.2.A4.0 centre.3.LN5 norm.3.LN5 max.2.A4.1 v.2.A4 max.2.A4.2 p_t.2.A4.0
q32.3.A4 max.2.A4.3 p_t.2.A4.1 q_low.3.A4 q_stack.3.A4 max.3.A4.0 max.3.A4.1 v.3.A4 o_norm.2.A4 max.3.A4.2
o_t.2.A4 max.3.A4.3 p_t.3.A4.1 sum.2.A4 stats.2.LN6 centre.2.LN6 norm.2.LN6 k32.2.A5 o_norm.3.A4 k_low.2.A5
q32.2.A5 q_low.2.A5 sum.3.A4 stats.3.LN6 centre.3.LN6 norm.3.LN6 max.2.A5.0 v.2.A5 max.2.A5.1 k32.3.A5 q32.3.A5
max.2.A5.2 k_low.3.A5 q_low.3.A5 max.2.A5.3 k_stack.3.A5 q_stack.3.A5 max.3.A5.0 max.3.A5.1 p_t.2.A5.3 v.3.A5
max.3.A5.2 p_t.3.A5.0 max.3.A5.3 o_norm.2.A5 p_t.3.A5.2 o_t.2.A5 p_t.3.A5.3 sum.2.A5 stats.2.LN7 centre.2.LN7
o_norm.3.A5 norm.2.LN7 x_t.2.F1 sum.3.A5 stats.3.LN7 centre.3.LN7 norm.3.LN7 sum.3.F1 sum.2.F1
"""
SCALAR = """
x_t.0.A0 k_high.0.A0 q_high.0.A0 q_high.1.A0 k_high.1.A0 q_stack.0.A0 exp.0.A0.0 exp.0.A0.1 exp.1.A0.0 exp.0.A0.2
exp.1.A0.1 exp.0.A0.3 p_t.0.A0.2 exp.1.A0.2 k_high.1.A1 o_raw.0.A0 exp.1.A0.3 p_t.1.A0.2 p_t.1.A0.3 o_raw.1.A0
v.1.A1 k_high.0.A1 x_t.0.A1 k_stack.0.A1 q_high.0.A1 x_t.1.A1 q_high.1.A1 exp.0.A1.0 exp.0.A1.1 v.0.A1 p_t.0.A1.0
exp.0.A1.2 exp.0.A1.3 exp.1.A1.0 exp.1.A1.1 o_raw.0.A1 p_t.1.A1.1 exp.1.A1.2 o_t.0.A1 exp.1.A1.3 k_high.0.A2
p_t.1.A1.3 o_raw.1.A1 x_t.0.F0 h_t.0.F0.1 x_t.1.F0 k_stack.0.A2 x_t.0.A2 k_high.1.A2 q_high.0.A2 h_t.1.F0.1
exp.0.A2.0 exp.0.A2.1 p_t.0.A2.0 k_stack.1.A2 x_t.1.A2 p_t.0.A2.1 exp.0.A2.2 q_high.1.A2 exp.0.A2.3 p_t.0.A2.2
p_t.0.A2.3 o_raw.0.A2 exp.1.A2.0 exp.1.A2.1 k_high.0.A3 o_t.0.A2 exp.1.A2.2 exp.1.A2.3 p_t.1.A2.2 p_t.1.A2.3
o_raw.1.A2 k_high.1.A3 o_t.1.A2 q_high.0.A3 k_stack.0.A3 q_stack.0.A3 x_t.1.A3 exp.0.A3.0 q_high.1.A3 k_stack.1.A3
exp.0.A3.1 q_stack.1.A3 p_t.0.A3.0 exp.0.A3.2 p_t.0.A3.1 exp.0.A3.3 p_t.0.A3.2 p_t.0.A3.3 exp.1.A3.0 o_raw.0.A3
k_high.0.A4 p_t.1.A3.0 exp.1.A3.1 o_t.0.A3 exp.1.A3.2 p_t.1.A3.1 exp.1.A3.3 p_t.1.A3.2 p_t.1.A3.3 o_raw.1.A3
k_high.1.A4 k_stack.0.A4 x_t.0.A4 q_high.0.A4 k_stack.1.A4 q_stack.0.A4 x_t.1.A4 exp.0.A4.0 exp.0.A4.1 q_high.1.A4
exp.0.A4.2 p_t.0.A4.1 exp.0.A4.3 exp.1.A4.0 o_raw.0.A4 exp.1.A4.1 p_t.1.A4.0 o_t.0.A4 exp.1.A4.2 p_t.1.A4.1
exp.1.A4.3 p_t.1.A4.2 p_t.1.A4.3 x_t.0.A5 o_raw.1.A4 k_high.0.A5 o_t.1.A4 q_high.0.A5 k_stack.0.A5 q_stack.0.A5
x_t.1.A5 exp.0.A5.0 exp.0.A5.1 k_high.1.A5 q_high.1.A5 p_t.0.A5.0 exp.0.A5.2 exp.0.A5.3 q_stack.1.A5 p_t.0.A5.3
o_raw.0.A5 exp.1.A5.0 exp.1.A5.1 p_t.1.A5.0 o_t.0.A5 exp.1.A5.2 exp.1.A5.3 p_t.1.A5.2 p_t.1.A5.3 o_raw.1.A5
h_t.0.F1.0 h_t.0.F1.1 k_high.2.A0 q_high.2.A0 x_t.1.F1 q_stack.2.A0 h_t.1.F1.0 h_t.1.F1.1 exp.2.A0.0 k_high.3.A0
q_high.3.A0 exp.2.A0.1 exp.2.A0.2 exp.3.A0.0 exp.3.A0.1 p_t.2.A0.1 exp.2.A0.3 p_t.3.A0.0 p_t.2.A0.3 exp.3.A0.2
exp.3.A0.3 v.3.A0 o_raw.2.A0 p_t.3.A0.2 p_t.3.A0.3 o_t.2.A0 o_raw.3.A0 k_high.2.A1 o_t.3.A0 x_t.2.A1 k_stack.2.A1
q_high.2.A1 v.2.A1 q_high.3.A1 exp.2.A1.0 k_high.3.A1 v.3.A1 exp.2.A1.1 k_stack.3.A1 exp.2.A1.2 exp.2.A1.3
exp.3.A1.0 exp.3.A1.1 o_raw.2.A1 k_high.2.A2 p_t.3.A1.0 exp.3.A1.2 o_t.2.A1 exp.3.A1.3 p_t.3.A1.2 p_t.3.A1.3
o_raw.3.A1 k_stack.2.A2 o_t.3.A1 h_t.2.F0.0 k_high.3.A2 h_t.2.F0.1 h_t.3.F0.0 x_t.2.A2 h_t.3.F0.1 q_high.2.A2
q_stack.2.A2 k_stack.3.A2 exp.2.A2.0 exp.2.A2.1 q_high.3.A2 p_t.2.A2.0 exp.2.A2.2 exp.2.A2.3 p_t.2.A2.2
k_high.2.A3 exp.3.A2.0 o_raw.2.A2 exp.3.A2.1 exp.3.A2.2 o_t.2.A2 exp.3.A2.3 p_t.3.A2.2 p_t.3.A2.3 o_raw.3.A2
x_t.2.A3 k_high.3.A3 o_t.3.A2 q_high.2.A3 k_stack.3.A3 q_stack.2.A3 x_t.3.A3 q_high.3.A3 exp.2.A3.0 exp.2.A3.1
q_stack.3.A3 p_t.2.A3.0 exp.2.A3.2 p_t.2.A3.1 exp.2.A3.3 p_t.2.A3.2 p_t.2.A3.3 exp.3.A3.0 o_raw.2.A3 exp.3.A3.1
p_t.3.A3.0 o_t.2.A3 p_t.3.A3.1 exp.3.A3.2 exp.3.A3.3 p_t.3.A3.2 p_t.3.A3.3 o_raw.3.A3 k_high.2.A4 x_t.2.A4
k_high.3.A4 o_t.3.A3 q_high.2.A4 k_stack.2.A4 q_stack.2.A4 k_stack.3.A4 exp.2.A4.0 x_t.3.A4 exp.2.A4.1 exp.2.A4.2
q_high.3.A4 exp.2.A4.3 p_t.2.A4.2 p_t.2.A4.3 o_raw.2.A4 exp.3.A4.0 exp.3.A4.1 p_t.3.A4.0 exp.3.A4.2 exp.3.A4.3
p_t.3.A4.2 p_t.3.A4.3 x_t.2.A5 o_raw.3.A4 k_high.2.A5 o_t.3.A4 q_high.2.A5 k_stack.2.A5 q_stack.2.A5 x_t.3.A5
exp.2.A5.0 exp.2.A5.1 k_high.3.A5 q_high.3.A5 p_t.2.A5.0 p_t.2.A5.1 exp.2.A5.2 exp.2.A5.3 p_t.2.A5.2 exp.3.A5.0
exp.3.A5.1 o_raw.2.A5 exp.3.A5.2 p_t.3.A5.1 exp.3.A5.3 o_raw.3.A5 o_t.3.A5 h_t.2.F1.0 x_t.3.F1 h_t.2.F1.1
h_t.3.F1.0 h_t.3.F1.1
"""
POOL = """
flag.1.A0 flag.0.A0 root.0.LN0 root.1.LN0 flag.0.A1 flag.1.A1 root.0.LN1 root.1.LN1 res.0.LN1 root.0.LN2 res.1.LN1
root.1.LN2 res.1.LN2 res.0.LN2 root.0.LN3 root.1.LN3 flag.0.A3 res.0.LN3 root.0.LN4 flag.1.A3 res.1.LN3 root.0.LN5
root.1.LN4 root.1.LN5 res.0.LN5 res.1.LN5 root.0.LN6 res.0.LN6 root.1.LN6 flag.0.A5 flag.1.A5 root.0.LN7 res.0.LN7
res.1.LN6 root.1.LN7 res.1.LN7 flag.3.A0 flag.2.A0 root.2.LN0 root.3.LN0 flag.2.A1 root.2.LN1 res.2.LN1 flag.3.A1
root.3.LN1 root.2.LN2 res.3.LN1 root.3.LN2 res.3.LN2 res.2.LN2 root.2.LN3 res.2.LN3 root.3.LN3 res.3.LN3 flag.2.A3
root.2.LN4 flag.3.A3 root.2.LN5 root.3.LN4 root.3.LN5 res.3.LN5 res.2.LN5 root.2.LN6 root.3.LN6 flag.2.A5
res.2.LN6 flag.3.A5 res.3.LN6 root.2.LN7 res.2.LN7 root.3.LN7 res.3.LN7
"""


def parse(text):
    beats = []
    for word in text.split():
        kind, x, *where = word.split(".")
        beats.append((kind, int(x), where[0], *(int(u) for u in where[1:])))
    return beats


TENSOR_ORDER, VECTOR_ORDER, SCALAR_ORDER, POOL_ORDER = (parse(t) for t in (TENSOR, VECTOR, SCALAR, POOL))
assert sorted(TENSOR_ORDER + VECTOR_ORDER + SCALAR_ORDER + POOL_ORDER) == sorted(
    (b[0], x, *b[1:]) for b in stream_beats() for x in range(SEQS))

COPIES = ("x_t", "v", "k_stack", "q_stack", "p_t", "o_t")


def fills_bank(beat):
    kind = beat[0]
    return kind not in ("S", "PV") and (kind != "H" or beat[3] % 2 == 0) and (kind != "Y" or beat[3] == 0)


def last_reader(kind, s, *u):
    reader = {"xT": "x_t", "V": "v", "kT": "k_stack", "qT": "q_stack", "pT": "p_t", "oT": "o_norm", "nT": "o_t",
              "O": "sum", "Y": "sum", "H": "h_t"}
    if kind in ("K", "Q"):
        return (kind.lower() + ("32" if ATTN[s]["b"] else "_low"), s)
    if kind == "H":
        return ("h_t", s, u[0] // 2)
    return (reader[kind], s) if kind == "Y" else (reader[kind], s, *u)


FILLS = [beat for beat in TENSOR_ORDER if fills_bank(beat)]
FILL_AT = {beat: n for n, beat in enumerate(FILLS)}
OUTPUT_TURNS = [beat[1:3] for beat in TENSOR_ORDER if beat[0] == "PV" and beat[3] == 0]


def program(nc, dram, out):
    with ExitStack() as ctx:
        def sb(name, shape, dt=F32):
            return ctx.enter_context(nc.sbuf_tensor(name, shape, dt))

        def pb(name, shape=(128, 512), dt=F32):
            return ctx.enter_context(nc.psum_tensor(name, list(shape), dt))

        def sem(name):
            return ctx.enter_context(nc.semaphore(name))

        weights = {s: sb(f"weights_{s}", [128, WEIGHT_COLS[s]]) for s in STAGES}
        vectors = {s: sb(f"vectors_{s}", [128, D * len(VECTORS[s])]) for s in STAGES if VECTORS[s]}

        def chunks(s, first, count, width):
            return weights[s][:, first:first + count * width].rearrange("p (c n) -> p c n", c=count)

        def vector(s, name):
            at = D * VECTORS[s].index(name)
            return vectors[s][:, at:at + D]

        w_q, w_k, w_v, w_o = ({s: chunks(s, n * KC * D, KC, D) for s in ATTN} for n in range(4))
        w_1 = {s: chunks(s, 0, KC, FF) for s in FFN}
        w_2 = {s: chunks(s, KC * FF, FC, D) for s in FFN}
        b_1 = {s: weights[s][:, KC * FF + FC * D:] for s in FFN}
        b_q = {s: vector(s, ATTN[s]["b"][0]) for s in ATTN if ATTN[s]["b"]}
        b_k = {s: vector(s, ATTN[s]["b"][1]) for s in ATTN if ATTN[s]["b"]}
        b_v = {s: vector(s, ATTN[s]["b"][2]) for s in ATTN if ATTN[s]["b"]}
        b_res = {s: vector(s, FFN[s]["b2"] if s in FFN else ATTN[s]["b"][3]) for s in STAGES if s in FFN or ATTN[s]["b"]}
        gain = {n: vector(s, LN[n]["g"]) for s in STAGES for n in norms_after(s)}
        shift = {n: vector(s, LN[n]["b"]) for s in STAGES for n in norms_after(s)}

        id32 = sb("id32", [128, 128])
        id16 = sb("id16", [128, 128], F16)
        idb = sb("idb", [128, 128], BF16)
        causal = sb("causal", [128, 128], BF16)
        halves = sb("halves", [128, 2])
        overflow = sb("overflow", [128, H])
        sxs_raw = sb("sxs_raw", [128, 128], U8)
        sxs_bias = sb("sxs_bias", [128, 128], BF16)

        def per_stream(name, shape, dt=F32):
            return [sb(f"{name}{x}", shape, dt) for x in range(STREAMS)] * (SEQS // STREAMS)

        x_run = per_stream("x_run", [128, D])
        x_norm = per_stream("x_norm", [128, D])
        x_sum = per_stream("x_sum", [128, D])
        x_res = per_stream("x_res", [128, D])
        x_t = per_stream("x_t", [128, KC, N])
        ctx_t = per_stream("ctx_t", [128, KC, N])
        q32 = per_stream("q32", [128, D])
        k32 = per_stream("k32", [128, D])
        q_parts = per_stream("q_parts", [128, H, 4, DH], F16)
        k_parts = per_stream("k_parts", [128, H, 4, DH], F16)
        q_stack = per_stream("q_stack", [128, H // 2, N], F16)
        k_stack = per_stream("k_stack", [128, H // 2, N], F16)
        v_one = per_stream("v_one", [128, H, 2 * DH])
        key_raw = per_stream("key_raw", [128, 128], U8)
        ik_raw = per_stream("ik_raw", [128, 128], I32)
        bias = per_stream("bias", [128, 3, 128], BF16)
        weight = per_stream("weight", [128, H, N])
        drop_raw = per_stream("drop_raw", [128, H, N], U8)
        neg_max = per_stream("neg_max", [128, H])
        grown = per_stream("grown", [128, H])
        nan_flag = per_stream("nan_flag", [128, H])
        exps = per_stream("exps", [128, 2, QH * N])
        exps_t = per_stream("exps_t", [128, 2, QH * N])
        o_raw = per_stream("o_raw", [128, QUADS, N])
        recip = per_stream("recip", [128, 2, H])
        o_norm = per_stream("o_norm", [128, D])
        o_t = per_stream("o_t", [128, KC, N])
        h_t = per_stream("h_t", [128, FC, N])
        bn = per_stream("bn", [128, 6])
        mean_var = per_stream("mean_var", [128, 2])
        var_eps = per_stream("var_eps", [128, 1])
        root = per_stream("root", [128, 1])
        root_eps = per_stream("root_eps", [128, 1])
        inv_root = per_stream("inv_root", [128, 1])

        s_bank = [[pb(f"s_bank{x}_{r}") for r in range(2)] for x in range(STREAMS)] * (SEQS // STREAMS)
        o_bank = pb("o_bank")
        chain = [pb(f"chain{b}") for b in range(CHAIN_BANKS)]

        stage_loaded = {s: sem(f"stage_loaded_{s}") for s in STAGES}
        sxs_loaded = sem("sxs_loaded")
        first_x_loaded = [sem(f"first_x_loaded{x}") for x in range(STREAMS)]
        first_ctx_loaded = [sem(f"first_ctx_loaded{x}") for x in range(STREAMS)]
        first_masks_loaded = [sem(f"first_masks_loaded{x}") for x in range(STREAMS)]
        first_weight_loaded = [sem(f"first_weight_loaded{x}") for x in range(STREAMS)]
        cleared = sem("cleared")
        const_made = sem("const_made")
        buffers_cleared = sem("buffers_cleared")
        sxs_made = sem("sxs_made")

        def sems(name):
            return [sem(f"{name}{x}") for x in range(STREAMS)] * (SEQS // STREAMS)

        x_loaded = sems("x_loaded")
        ctx_loaded = sems("ctx_loaded")
        masks_loaded = sems("masks_loaded")
        weight_loaded = sems("weight_loaded")
        stored = sems("stored")
        key_bias_made = sems("key_bias_made")
        done = {k: sems(f"done_{k}_") for k in ("xT", "K", "kT", "Q", "qT", "V", "S", "pT", "PV", "oT", "nT", "O",
                                                "H", "Y")}
        done |= {k: sems(f"done_{k}_") for k in ("bias", "x_t", "k32", "v", "k_high", "k_low", "q32", "q_high", "q_low",
                                                 "k_stack", "q_stack", "times", "lower", "max", "exp", "flag", "o_raw", "o_norm", "o_t",
                                                 "sum", "stats", "centre", "root", "norm", "res")}
        done |= {k: [sems(f"done_{k}_even_"), sems(f"done_{k}_odd_")] for k in EVEN_ODD}
        grown_made = sems("grown_made")
        recip_made = sems("recip_made")
        recip_flagged = sems("recip_flagged")
        bn_made = sems("bn_made")
        aggr_made = sems("aggr_made")
        root_shifted = sems("root_shifted")
        root_inverted = sems("root_inverted")

        first_cleared, last_cleared = x_loaded[0].num, root_inverted[-1].num

        def nth(x, *beat):
            return x // STREAMS * TOTAL[beat[0]] + NTH[beat]

        def quads_before(x, s, u, back):
            return QUADS * (x // STREAMS * len(ATTN) + list(ATTN).index(s)) + u + 1 - back

        def bank(beat):
            return chain[FILL_AT[beat] % CHAIN_BANKS]

        def read_by(beat):
            kind, x, *where = beat
            reader = last_reader(kind, *where)
            if reader[0] in EVEN_ODD:
                return done[reader[0]][reader[2] % 2][x], nth(x, *reader)
            return done[reader[0]][x], nth(x, *reader)

        def source(s):
            return {"A0": None, "A1": "LN0", "F0": "LN1", "A2": "LN2", "A3": "LN3", "A4": "LN5",
                    "A5": "LN6", "F1": "LN7"}[s]

        def stage_input(x, s):
            d = ATTN.get(s) or FFN[s]
            return x_norm[x] if d["pre"] else x_run[x]

        def feeds_res(s):
            return next((n for n, made in MAKES_RES.items() if made and FED_BY[n] == s), None)

        def residual(x, s):
            return x_res[x] if feeds_res(s) else x_run[x]

        def mask_bias(x, s):
            m = ATTN[s]["mask"]
            return sxs_bias[:] if m == 3 else bias[x][:, m, :]

        def four(ap):
            return ap.unsqueeze(1).broadcast_to([128, QH, 128])

        def slots(u):
            return slice(QH * u, QH * u + QH)

        def all_loaded(s):
            return 32

        def one(name, b):
            t = dram[name]
            dims = " ".join("cdef"[:len(t.shape) - 1])
            return t[bass.ds(b, 1)].rearrange(f"a {dims} -> (a {dims[0]}) {dims[2:]}")

        def load_x(queue, x, b, loaded):
            queue.dma_start(x_run[x][:], one("x", b)).then_inc(loaded[x], 16)

        def load_ctx(queue, x, b, loaded):
            queue.dma_start(ctx_t[x][:], dram["ctx_t"][bass.ds(b, 1)].rearrange("a (c p) n -> p (a c) n", p=128)
                            ).then_inc(loaded[x], 16)

        def load_masks(queue, x, b, loaded):
            queue.dma_start(key_raw[x][:], dram["kmask"][bass.ds(b, 1)].rearrange("a c d e -> (a c d) e")
                            .broadcast_to([128, N])).then_inc(loaded[x], 16)
            queue.dma_start(ik_raw[x][:], one("ik", b)).then_inc(loaded[x], 16)

        def load_weight(queue, x, b, loaded):
            queue.dma_start(weight[x][:], one("fside", b)).then_inc(loaded[x], 16)
            queue.dma_start(drop_raw[x][:], one("drop", b)).then_inc(loaded[x], 16)

        def load_stage(queue, s):
            queue.dma_start(weights[s][:], dram[f"weights_{s}"]).then_inc(stage_loaded[s], 16)
            queue.dma_start(vectors[s][:], dram[f"vectors_{s}"].rearrange("(a n) -> a n", a=1)
                            .broadcast_to([128, D * len(VECTORS[s])])).then_inc(stage_loaded[s], 16)

        with nc.Block() as block:
            @block.scalar
            def _(act):
                load_stage(act, "A0")
                for x in range(STREAMS):
                    load_ctx(act, x, x, first_ctx_loaded)
                for s in ("F0", "A3", "A5", "F1"):
                    load_stage(act, s)

            @block.sync
            def _(sp):
                for x in range(STREAMS):
                    load_x(sp, x, x, first_x_loaded)
                for x in range(STREAMS):
                    load_masks(sp, x, x, first_masks_loaded)
                sp.dma_start(sxs_raw[:], dram["sxs"]).then_inc(sxs_loaded, 16)
                load_stage(sp, "A1")
                load_stage(sp, "A2")
                for x in range(STREAMS):
                    load_weight(sp, x, x, first_weight_loaded)
                load_stage(sp, "A4")

            @block.gpsimd
            def _(pool):
                for t in (id32, id16, idb, causal):
                    nc.gpsimd.memset(t[:], 0.0).then_inc(cleared, 1)
                nc.gpsimd.memset(halves[:, 0:1], -0.5).then_inc(const_made, 1)
                nc.gpsimd.memset(halves[:, 1:2], 0.5).then_inc(const_made, 1)
                nc.gpsimd.memset(overflow[:], OVERFLOW).then_inc(const_made, 1)
                pool.wait_ge(cleared, 4)
                for t in (id32, id16, idb):
                    nc.gpsimd.affine_select(out=t[:], in_=t[:], compare_op=ALU.not_equal, fill=1.0, base=0,
                                            pattern=[[-1, 128]], channel_multiplier=1).then_inc(const_made, 1)
                nc.gpsimd.affine_select(out=causal[:], in_=causal[:], compare_op=ALU.is_ge, fill=MASKED, base=0,
                                        pattern=[[-1, 128]], channel_multiplier=1).then_inc(const_made, 1)

            @block.vector
            def _(dve):
                for x in range(STREAMS):
                    nc.vector.memset(v_one[x][:, :, DH:DH + 1], 1.0).then_inc(buffers_cleared, 1)
                    nc.vector.memset(v_one[x][:, :, DH + 1:2 * DH], 0.0).then_inc(buffers_cleared, 1)
                    nc.vector.memset(q_parts[x][:, :, 3, :], 0.0).then_inc(buffers_cleared, 1)
                    nc.vector.memset(k_parts[x][:, :, 3, :], 0.0).then_inc(buffers_cleared, 1)
                dve.wait_ge(sxs_loaded, 16)
                nc.vector.tensor_scalar(sxs_bias[:], sxs_raw[:], 0.0, MASKED, ALU.is_gt, ALU.mult
                                        ).then_inc(sxs_made, 1)

        with nc.Fori(0, B // SEQS) as i:
            with nc.Block() as block:

                @block.sync
                def _(sp):
                    for first in range(0, SEQS, STREAMS):
                        pair = range(first, first + STREAMS)
                        ahead = {x: (SEQS * i + x + STREAMS) & (B - 1) for x in pair}
                        for x in pair:
                            sp.wait_ge(done["bias"][x], nth(x, "bias", "in"))
                            load_masks(sp, x, ahead[x], masks_loaded)
                        for x in pair:
                            sp.wait_ge(done["exp"][x], nth(x, "exp", "A3", QUADS - 1))
                            load_weight(sp, x, ahead[x], weight_loaded)
                        for x in pair:
                            sp.wait_ge(done["K"][x], nth(x, "K", "A4"))
                            sp.wait_ge(done["V"][x], nth(x, "V", "A4"))
                            load_ctx(sp, x, ahead[x], ctx_loaded)
                        for x in pair:
                            sp.wait_ge(done["res"][x], nth(x, "res", "LN7"))
                            load_x(sp, x, ahead[x], x_loaded)
                        for x in pair:
                            sp.wait_ge(done["sum"][x], nth(x, "sum", "F1"))
                            sp.dma_start(out[bass.ds(SEQS * i + x, 1)].rearrange("a q d -> (a q) d"), x_sum[x][:]
                                         ).then_inc(stored[x], 16)
                    for x in range(STREAMS):
                        sp.wait_ge(masks_loaded[x], 32 * SEQS // STREAMS)
                        sp.wait_ge(weight_loaded[x], 32 * SEQS // STREAMS)
                        sp.wait_ge(ctx_loaded[x], 16 * SEQS // STREAMS)
                        sp.wait_ge(x_loaded[x], 16 * SEQS // STREAMS)
                        sp.wait_ge(stored[x], 16 * SEQS // STREAMS)

                @block.gpsimd
                def _(pool):
                    def row_flags(x, s):
                        pool.wait_ge(done["max"][x], nth(x, "max", s, QUADS - 1))
                        nc.gpsimd.tensor_tensor(grown[x][:], neg_max[x][:], overflow[:], ALU.mult
                                                ).then_inc(grown_made[x], 1)
                        pool.wait_ge(grown_made[x], nth(x, "flag", s))
                        nc.gpsimd.tensor_tensor(nan_flag[x][:], grown[x][:], grown[x][:], ALU.subtract
                                                ).then_inc(done["flag"][x], 1)

                    def var_root(x, n):
                        pool.wait_ge(done["stats"][x], nth(x, "stats", n))
                        e = 1 if LN[n]["on_root"] else 0
                        nc.gpsimd.tensor_tensor(root[x][:], var_eps[x][:], halves[:, e:e + 1], ALU.pow
                                                ).then_inc(done["root"][x], 1)

                    def next_residual(x, n):
                        s = FED_BY[n]
                        pool.wait_ge(done["norm"][x], nth(x, "norm", n))
                        pool.wait_ge(stage_loaded[s], all_loaded(s))
                        nc.gpsimd.tensor_tensor(x_res[x][:], x_run[x][:], b_res[s], ALU.add
                                                ).then_inc(done["res"][x], 1)

                    for kind, x, *where in POOL_ORDER:
                        if kind == "flag":
                            row_flags(x, *where)
                        elif kind == "root":
                            var_root(x, *where)
                        elif kind == "res":
                            next_residual(x, *where)

                @block.tensor
                def _(pe):
                    def free_bank(beat):
                        n = FILL_AT[beat] - CHAIN_BANKS
                        if n >= 0:
                            read, times = read_by(FILLS[n])
                            pe.wait_ge(read, times)
                        return bank(beat)

                    def transposes32(dst, src, blocks):
                        for c in range(blocks):
                            mm = nc.tensor.matmul(dst[:, 128 * c:128 * c + 128], src[:, 128 * c:128 * c + 128], id32[:],
                                                  start=True, stop=True, is_transpose=True)
                        return mm

                    def product(dst, left, right, chunks, total):
                        for c in chunks:
                            mm = nc.tensor.matmul(dst, left[:, c, :], right[:, c, :], start=(c == 0), stop=(c == total - 1))
                        return mm

                    def keys_or_values(dst, x, s, w):
                        pe.wait_ge(stage_loaded[s], all_loaded(s))
                        if ATTN[s]["kv"] == "self":
                            pe.wait_ge(done["x_t"][x], nth(x, "x_t", s))
                            source_t = x_t[x]
                        else:
                            if x < STREAMS:
                                pe.wait_ge(first_ctx_loaded[x], 16)
                            else:
                                pe.wait_ge(ctx_loaded[x], 16)
                            source_t = ctx_t[x]
                        return product(dst[:, 0:D], source_t, w[s], range(KC), KC)

                    def stack(dst, parts):
                        flat = parts[:].rearrange("p h t d -> p (h t d)")
                        for pair in range(H // 2):
                            mm = nc.tensor.transpose(dst[:].bitcast(F16)[:, 128 * pair:128 * pair + 128],
                                                     flat[:, 128 * pair:128 * pair + 128], id16[:])
                        return mm

                    def scores(x, s, u):
                        c, r = u // 2, u % 2
                        if u == 0:
                            pe.wait_ge(done["k_stack"][x], nth(x, "k_stack", s))
                            pe.wait_ge(done["q_stack"][x], nth(x, "q_stack", s))
                            if ATTN[s]["mask"] in (0, 1, 2):
                                pe.wait_ge(done["bias"][x], nth(x, "bias", "in"))
                            elif ATTN[s]["mask"] == 3:
                                pe.wait_ge(sxs_made, 1)
                        if s == "A3" and u >= 2:
                            pe.wait_ge(done["times"][x], nth(x, "times", s, u - 2))
                        elif quads_before(x, s, u, 2) > 0:
                            pe.wait_ge(done["exp"][x], quads_before(x, s, u, 2))
                        masked = ATTN[s]["mask"] is not None
                        dst = s_bank[x][r]
                        if masked:
                            nc.tensor.matmul(dst[:], idb[:], four(mask_bias(x, s)), start=True, stop=True)
                        rows = slice(64 * r, 64 * r + 64)
                        for n in range(QH):
                            mm = nc.tensor.matmul(dst[:, 128 * n:128 * n + 128], q_stack[x][rows, QH * c + n, :],
                                                  k_stack[x][rows, QH * c + n, :], start=not masked,
                                                  stop=True, skip_group_check=masked)
                        mm.then_inc(done["S"][x], 1)

                    def outputs(x, s, u):
                        pe.wait_ge(done["p_t"][u % 2][x], nth(x, "p_t", s, u))
                        if u == 0:
                            pe.wait_ge(done["v"][x], nth(x, "v", s))
                            turn = OUTPUT_TURNS.index((x, s))
                            if turn:
                                last_x, last_s = OUTPUT_TURNS[turn - 1]
                                pe.wait_ge(done["o_raw"][last_x], nth(last_x, "o_raw", last_s))
                        for n in range(QH):
                            h = 8 * (u // 2) + 2 * n + u % 2
                            mm = nc.tensor.matmul(o_bank[32 * n:32 * n + 32, 128 * u:128 * u + 128], v_one[x][:, h, :],
                                                  exps_t[x][:, u % 2, 128 * n:128 * n + 128], start=True, stop=True)
                        mm.then_inc(done["PV"][x], 1)

                    def hidden(dst, x, s, part):
                        pe.wait_ge(stage_loaded[s], all_loaded(s))
                        pe.wait_ge(done["x_t"][x], nth(x, "x_t", s))
                        for n in (0, 1):
                            f = 2 * part + n
                            cols = slice(128 * (f % 4), 128 * (f % 4) + 128)
                            for c in range(KC):
                                mm = nc.tensor.matmul(dst[:, cols], w_1[s][:, c, 128 * f:128 * f + 128], x_t[x][:, c, :],
                                                      start=(c == 0), stop=(c == KC - 1))
                        return mm

                    for beat in TENSOR_ORDER:
                        kind, x, s = beat[:3]
                        dst = free_bank(beat) if fills_bank(beat) else None
                        if kind == "xT":
                            if s == "A0" and x < STREAMS:
                                pe.wait_ge(first_x_loaded[x], 16)
                            elif s == "A0":
                                pe.wait_ge(x_loaded[x], 16)
                            else:
                                pe.wait_ge(done["norm"][x], nth(x, "norm", source(s)))
                            transposes32(dst, stage_input(x, s), KC).then_inc(done["xT"][x], 1)
                        elif kind in ("K", "V"):
                            keys_or_values(dst, x, s, w_k if kind == "K" else w_v).then_inc(done[kind][x], 1)
                        elif kind == "Q":
                            pe.wait_ge(stage_loaded[s], all_loaded(s))
                            pe.wait_ge(done["x_t"][x], nth(x, "x_t", s))
                            product(dst[:, 0:D], x_t[x], w_q[s], range(KC), KC).then_inc(done["Q"][x], 1)
                        elif kind == "kT":
                            pe.wait_ge(done["k_low"][x], nth(x, "k_low", s))
                            stack(dst, k_parts[x]).then_inc(done["kT"][x], 1)
                        elif kind == "qT":
                            pe.wait_ge(done["q_low"][x], nth(x, "q_low", s))
                            stack(dst, q_parts[x]).then_inc(done["qT"][x], 1)
                        elif kind == "S":
                            scores(x, s, beat[3])
                        elif kind == "pT":
                            pe.wait_ge(done["exp"][x], nth(x, "exp", s, beat[3]))
                            transposes32(dst, exps[x][:, beat[3] % 2, :], QH).then_inc(done["pT"][x], 1)
                        elif kind == "PV":
                            outputs(x, s, beat[3])
                        elif kind == "oT":
                            pe.wait_ge(done["o_raw"][x], nth(x, "o_raw", s))
                            transposes32(dst, o_raw[x][:].rearrange("p u q -> p (u q)"), QUADS).then_inc(done["oT"][x], 1)
                        elif kind == "nT":
                            pe.wait_ge(done["o_norm"][x], nth(x, "o_norm", s))
                            transposes32(dst, o_norm[x], KC).then_inc(done["nT"][x], 1)
                        elif kind == "O":
                            pe.wait_ge(done["o_t"][x], nth(x, "o_t", s))
                            product(dst[:, 0:D], o_t[x], w_o[s], range(KC), KC).then_inc(done["O"][x], 1)
                        elif kind == "H":
                            hidden(bank(("H", x, s, beat[3] // 2 * 2)), x, s, beat[3]).then_inc(done["H"][x], 1)
                        elif kind == "Y":
                            part = beat[3]
                            pe.wait_ge(done["h_t"][part // 2][x], nth(x, "h_t", s, part // 2))
                            product(bank(("Y", x, s, 0))[:, 0:D], h_t[x], w_2[s], range(2 * part, 2 * part + 2), FC
                                    ).then_inc(done["Y"][x], 1)

                def copy_beat(engine, copy, kind, x, s, u=None):
                    if kind == "x_t":
                        if s == "A0" and x >= STREAMS:
                            engine.wait_ge(done["H"][x], nth(x - STREAMS, "H", "F1", 3))
                        engine.wait_ge(done["xT"][x], nth(x, "xT", s))
                        copy(x_t[x][:], bank(("xT", x, s))[:, 0:D].rearrange("p (c q) -> p c q", c=KC)
                             ).then_inc(done["x_t"][x], 1)
                    elif kind == "v":
                        engine.wait_ge(done["V"][x], nth(x, "V", s))
                        if quads_before(x, s, 0, 1) > 0:
                            engine.wait_ge(done["PV"][x], quads_before(x, s, 0, 1))
                        copy(v_one[x][:, :, 0:DH], bank(("V", x, s))[:, 0:D].rearrange("p (h d) -> p h d", h=H)
                             ).then_inc(done["v"][x], 1)
                    elif kind in ("k_stack", "q_stack"):
                        transposed, dst = ("kT", k_stack) if kind == "k_stack" else ("qT", q_stack)
                        engine.wait_ge(done[transposed][x], nth(x, transposed, s))
                        copy(dst[x][:], bank((transposed, x, s))[:].bitcast(F16).rearrange("p (h k) -> p h k", h=H // 2)
                             ).then_inc(done[kind][x], 1)
                    elif kind == "p_t":
                        engine.wait_ge(done["pT"][x], nth(x, "pT", s, u))
                        if quads_before(x, s, u, 2) > 0:
                            engine.wait_ge(done["PV"][x], quads_before(x, s, u, 2))
                        copy(exps_t[x][:, u % 2, :], bank(("pT", x, s, u))[:]).then_inc(done["p_t"][u % 2][x], 1)
                    elif kind == "o_t":
                        engine.wait_ge(done["nT"][x], nth(x, "nT", s))
                        copy(o_t[x][:], bank(("nT", x, s))[:, 0:D].rearrange("p (c q) -> p c q", c=KC)
                             ).then_inc(done["o_t"][x], 1)

                @block.scalar
                def _(act):
                    def split_high(kind, x, s, parts, raw, scale):
                        product, biased = kind[0].upper(), kind[0] + "32"
                        if ATTN[s]["b"]:
                            act.wait_ge(done[biased][x], nth(x, biased, s))
                            src = raw[:]
                        else:
                            act.wait_ge(done[product][x], nth(x, product, s))
                            src = bank((product, x, s))[:, 0:D]
                        nc.scalar.activation(parts, src.rearrange("p (h t d) -> p h t d", h=H, t=1)
                                             .broadcast_to([128, H, 2, DH]), ACT.Copy, scale=scale
                                             ).then_inc(done[kind][x], 1)

                    def exponentials(x, s, u):
                        act.wait_ge(done["max"][x], nth(x, "max", s, u))
                        if quads_before(x, s, u, 2) > 0:
                            act.wait_ge(done["pT"][x], quads_before(x, s, u, 2))
                        for n in range(QH):
                            cols = slice(128 * n, 128 * n + 128)
                            slot = QH * u + n
                            src = weight[x][:, slot, :] if s == "A3" else s_bank[x][u % 2][:, cols]
                            ins = nc.scalar.activation(exps[x][:, u % 2, cols], src, ACT.Exp,
                                                       bias=neg_max[x][:, slot:slot + 1])
                        ins.then_inc(done["exp"][x], 1)

                    for beat in SCALAR_ORDER:
                        kind, x, s = beat[:3]
                        if kind in COPIES:
                            copy_beat(act, nc.scalar.copy, *beat)
                        elif kind == "k_high":
                            split_high(kind, x, s, k_parts[x][:, :, 0:3:2, :], k32[x], 1.0)
                        elif kind == "q_high":
                            split_high(kind, x, s, q_parts[x][:, :, 0:2, :], q32[x], DH ** -0.5)
                        elif kind == "exp":
                            exponentials(x, s, beat[3])
                        elif kind == "o_raw":
                            act.wait_ge(done["PV"][x], nth(x, "PV", s, QUADS - 1))
                            nc.scalar.copy(o_raw[x][:], o_bank[:].rearrange("p (u q) -> p u q", u=QUADS)
                                           ).then_inc(done["o_raw"][x], 1)
                        elif kind == "h_t":
                            half = beat[3]
                            act.wait_ge(done["H"][x], nth(x, "H", s, 2 * half + 1))
                            for n in range(QH):
                                f = QH * half + n
                                ins = nc.scalar.activation(h_t[x][:, f, :], bank(("H", x, s, 2 * half))[:, 128 * n:128 * n + 128],
                                                           ACT.Gelu if FFN[s]["gelu"] else ACT.Relu, bias=b_1[s][:, f:f + 1])
                            ins.then_inc(done["h_t"][half][x], 1)

                @block.vector
                def _(dve):
                    def mask_biases(x):
                        if x < STREAMS:
                            dve.wait_ge(first_masks_loaded[x], 32)
                        else:
                            dve.wait_ge(masks_loaded[x], 32)
                            dve.wait_ge(done["S"][x], nth(x - STREAMS, "S", "A2", QUADS - 1))
                        nc.vector.tensor_scalar(bias[x][:, 1, :], key_raw[x][:], 0.0, MASKED, ALU.is_equal, ALU.mult
                                                ).then_inc(key_bias_made[x], 1)
                        nc.vector.tensor_scalar(bias[x][:, 2, :], ik_raw[x][:], 0.0, MASKED, ALU.is_equal, ALU.mult
                                                ).then_inc(key_bias_made[x], 1)
                        dve.wait_ge(key_bias_made[x], 2 * nth(x, "bias", "in"))
                        nc.vector.tensor_tensor(bias[x][:, 0, :], bias[x][:, 1, :], causal[:], ALU.add
                                                ).then_inc(done["bias"][x], 1)

                    def values(x, s):
                        dve.wait_ge(done["V"][x], nth(x, "V", s))
                        dve.wait_ge(done["PV"][x], quads_before(x, s, 0, 1))
                        nc.vector.tensor_tensor(v_one[x][:, :, 0:DH], bank(("V", x, s))[:, 0:D].rearrange(
                            "p (h d) -> p h d", h=H), b_v[s].rearrange("p (h d) -> p h d", h=H), ALU.add
                                                ).then_inc(done["v"][x], 1)

                    def quad_max(x, s, u):
                        if s == "A3":
                            dve.wait_ge(done["lower"][x], nth(x, "lower", s, u))
                            heads = weight[x][:, slots(u), :]
                        else:
                            dve.wait_ge(done["S"][x], nth(x, "S", s, u))
                            heads = s_bank[x][u % 2][:].rearrange("p (n k) -> p n k", n=QH)
                        nc.vector.tensor_reduce(neg_max[x][:, slots(u)], heads, AX_X, ALU.max, negate=True
                                                ).then_inc(done["max"][x], 1)

                    def normalise(x, s):
                        heads = bank(("oT", x, s))[:].rearrange("p (h e) -> p h e", h=H)
                        dve.wait_ge(done["oT"][x], nth(x, "oT", s))
                        nc.vector.reciprocal(recip[x][:, 0, :].unsqueeze(2), heads[:, :, DH:DH + 1]
                                             ).then_inc(recip_made[x], 1)
                        dve.wait_ge(recip_made[x], nth(x, "oT", s))
                        which = 0
                        if ATTN[s]["nan"]:
                            dve.wait_ge(done["flag"][x], nth(x, "flag", s))
                            nc.vector.tensor_tensor(recip[x][:, 1, :], recip[x][:, 0, :], nan_flag[x][:], ALU.add
                                                    ).then_inc(recip_flagged[x], 1)
                            dve.wait_ge(recip_flagged[x], nth(x, "flag", s))
                            which = 1
                        nc.vector.tensor_tensor(o_norm[x][:].rearrange("p (h d) -> p h d", h=H), heads[:, :, 0:DH],
                                                recip[x][:, which, :].unsqueeze(2).broadcast_to([128, H, DH]), ALU.mult
                                                ).then_inc(done["o_norm"][x], 1)

                    def add_residual(x, s):
                        product = ("O", x, s) if s in ATTN else ("Y", x, s, 0)
                        dst = x_run[x] if s in ("A4", "A5") else x_sum[x]
                        if s in ATTN:
                            dve.wait_ge(done["O"][x], nth(x, "O", s))
                        else:
                            dve.wait_ge(done["Y"][x], nth(x, "Y", s, 3))
                        if s == "A0" and x >= STREAMS:
                            dve.wait_ge(stored[x], 16)
                        if feeds_res(s):
                            dve.wait_ge(done["res"][x], nth(x, "res", feeds_res(s)))
                        nc.vector.tensor_tensor(dst[:], bank(product)[:, 0:D], residual(x, s)[:], ALU.add
                                                ).then_inc(done["sum"][x], 1)

                    def norm_stats(x, n):
                        d = LN[n]
                        src = x_sum[x] if d["of"] == "sum" else x_run[x]
                        kind, before = d["after"]
                        dve.wait_ge(done[kind][x], nth(x, kind, before))
                        nc.vector.bn_stats(bn[x][:], src[:]).then_inc(bn_made[x], 1)
                        dve.wait_ge(bn_made[x], nth(x, "stats", n))
                        nc.vector.bn_aggr(mean_var[x][:], bn[x][:]).then_inc(aggr_made[x], 1)
                        dve.wait_ge(aggr_made[x], nth(x, "stats", n))
                        scale = D / (D - d["ddof"])
                        nc.vector.tensor_scalar(var_eps[x][:], mean_var[x][:, 1:2], scale, 0.0 if d["on_root"] else d["eps"],
                                                ALU.mult, ALU.add).then_inc(done["stats"][x], 1)

                    def norm_apply(x, n):
                        d = LN[n]
                        dst = x_run[x] if d["to"] == "x" else x_norm[x]
                        dve.wait_ge(done["root"][x], nth(x, "root", n))
                        by = root[x]
                        if d["on_root"]:
                            turn = x // STREAMS * ROOTS_SHIFTED + NTH[("norm", n)]
                            nc.vector.tensor_scalar(root_eps[x][:], root[x][:], d["eps"], None, ALU.add
                                                    ).then_inc(root_shifted[x], 1)
                            dve.wait_ge(root_shifted[x], turn)
                            nc.vector.reciprocal(inv_root[x][:], root_eps[x][:]).then_inc(root_inverted[x], 1)
                            dve.wait_ge(root_inverted[x], turn)
                            by = inv_root[x]
                        dve.wait_ge(done["centre"][x], nth(x, "centre", n))
                        nc.vector.scalar_tensor_tensor(out=dst[:], in0=x_sum[x][:], scalar=by[:, 0:1], in1=shift[n],
                                                       op0=ALU.mult, op1=ALU.add).then_inc(done["norm"][x], 1)

                    for kind, x, s, *u in VECTOR_ORDER:
                        if kind in COPIES and not (kind == "v" and ATTN[s]["b"]):
                            copy_beat(dve, nc.vector.tensor_copy, kind, x, s, *u)
                        elif kind == "bias":
                            mask_biases(x)
                        elif kind in ("k32", "q32"):
                            product, dst, b = ("K", k32, b_k) if kind == "k32" else ("Q", q32, b_q)
                            dve.wait_ge(done[product][x], nth(x, product, s))
                            nc.vector.tensor_tensor(dst[x][:], bank((product, x, s))[:, 0:D], b[s], ALU.add
                                                    ).then_inc(done[kind][x], 1)
                        elif kind == "v":
                            values(x, s)
                        elif kind == "k_low":
                            dve.wait_ge(done["k_high"][x], nth(x, "k_high", s))
                            src = k32[x][:] if ATTN[s]["b"] else bank(("K", x, s))[:, 0:D]
                            nc.vector.tensor_tensor(k_parts[x][:, :, 1, :], src.rearrange("p (h d) -> p h d", h=H),
                                                    k_parts[x][:, :, 0, :], ALU.subtract).then_inc(done["k_low"][x], 1)
                        elif kind == "q_low":
                            dve.wait_ge(done["q_high"][x], nth(x, "q_high", s))
                            src = q32[x][:] if ATTN[s]["b"] else bank(("Q", x, s))[:, 0:D]
                            nc.vector.scalar_tensor_tensor(
                                out=q_parts[x][:, :, 2, :], in0=src.rearrange("p (h d) -> p h d", h=H), scalar=DH ** -0.5,
                                in1=q_parts[x][:, :, 0, :], op0=ALU.mult, op1=ALU.subtract).then_inc(done["q_low"][x], 1)
                        elif kind == "times":
                            if u[0] == 0 and x < STREAMS:
                                dve.wait_ge(first_weight_loaded[x], 32)
                            elif u[0] == 0:
                                dve.wait_ge(weight_loaded[x], 32)
                            dve.wait_ge(done["S"][x], nth(x, "S", s, *u))
                            part = weight[x][:, slots(*u), :]
                            nc.vector.tensor_tensor(part, s_bank[x][u[0] % 2][:].rearrange("p (n k) -> p n k", n=QH), part,
                                                    ALU.mult).then_inc(done["times"][x], 1)
                        elif kind == "lower":
                            dve.wait_ge(done["times"][x], nth(x, "times", s, *u))
                            part = weight[x][:, slots(*u), :]
                            nc.vector.scalar_tensor_tensor(out=part, in0=drop_raw[x][:, slots(*u), :], scalar=MASKED, in1=part,
                                                           op0=ALU.mult, op1=ALU.add).then_inc(done["lower"][x], 1)
                        elif kind == "max":
                            quad_max(x, s, *u)
                        elif kind == "o_norm":
                            normalise(x, s)
                        elif kind == "sum":
                            add_residual(x, s)
                        elif kind == "stats":
                            norm_stats(x, s)
                        elif kind == "centre":
                            dve.wait_ge(done["stats"][x], nth(x, "stats", s))
                            src = x_sum[x] if LN[s]["of"] == "sum" else x_run[x]
                            nc.vector.scalar_tensor_tensor(out=x_sum[x][:], in0=src[:], scalar=mean_var[x][:, 0:1],
                                                           in1=gain[s], op0=ALU.subtract, op1=ALU.mult
                                                           ).then_inc(done["centre"][x], 1)
                        elif kind == "norm":
                            norm_apply(x, s)
                        elif kind == "h_t":
                            half = u[0]
                            dve.wait_ge(done["H"][x], nth(x, "H", s, 2 * half + 1))
                            for n in range(QH):
                                f = QH * half + n
                                ins = nc.vector.tensor_scalar(h_t[x][:, f, :], bank(("H", x, s, 2 * half))[:, 128 * n:128 * n + 128],
                                                              b_1[s][:, f:f + 1], 0.0, ALU.add, ALU.max)
                            ins.then_inc(done["h_t"][half][x], 1)

            nc.all_engine_barrier(sems_to_clear=range(first_cleared, last_cleared + 1))


def kernel(**inputs):
    import numpy as np
    from concourse import bacc
    from concourse.bass_utils import run_bass_kernel_spmd

    slot_head = [8 * (u // 2) + 2 * n + u % 2 for u in range(QUADS) for n in range(QH)]
    slot_row = [DH * h + d for h in slot_head for d in range(DH)]

    def rows_on_partitions(w):
        return w.reshape(-1, 128, w.shape[1]).transpose(1, 0, 2).reshape(128, -1)

    arrays = {}
    for s in STAGES:
        if s in ATTN:
            q, k, v, o = (np.asarray(inputs[n]) for n in ATTN[s]["w"])
            if s in ("A2", "A3"):
                q, k, v, o = q.T, k.T, v.T, o.T
            parts = [rows_on_partitions(w) for w in (q, k, v, o[slot_row])]
        else:
            w1, w2, b1 = (np.asarray(inputs[FFN[s][k]]) for k in ("w1", "w2", "b1"))
            parts = [rows_on_partitions(w1), rows_on_partitions(w2), b1.reshape(FC, 128).T]
        arrays[f"weights_{s}"] = np.concatenate(parts, axis=1)
        if VECTORS[s]:
            arrays[f"vectors_{s}"] = np.concatenate([np.asarray(inputs[n]) for n in VECTORS[s]])
    arrays["x"] = np.asarray(inputs["x"])
    arrays["ctx_t"] = np.asarray(inputs["ctx_1024"]).transpose(0, 2, 1)
    arrays["fside"] = np.asarray(inputs["fside_Bx16xSxS2_0"])[:, slot_head].transpose(0, 2, 1, 3)
    arrays["ik"] = np.asarray(inputs["mask_BxSxS2_ik1"])
    arrays["kmask"] = np.asarray(inputs["mask_Bx1x1xS2_bf1"])
    arrays["drop"] = np.asarray(inputs["mask_Bx16xSxS2_bk0"])[:, slot_head].transpose(0, 2, 1, 3)
    arrays["sxs"] = np.asarray(inputs["mask_SxS_bk1"])
    arrays = {n: np.ascontiguousarray(a) for n, a in arrays.items()}

    nc = bacc.Bacc("TRN2", target_bir_lowering=False, num_devices=1)
    dram = {n: nc.dram_tensor(f"in_{n}", a.shape, mybir.dt.from_np(a.dtype), kind="ExternalInput").ap()
            for n, a in arrays.items()}
    out = nc.dram_tensor("out_0", (B, N, D), F32, kind="ExternalOutput").ap()
    program(nc, dram, out)
    r = run_bass_kernel_spmd(nc, [{f"in_{n}": a for n, a in arrays.items()}], core_ids=[0])
    return r.results[0]["out_0"]
```
